# Optimizing a Trainium2 kernel written in Bass

```python
import numpy as np
import jax
import jax.numpy as jnp

def _softmax(x, axis=-1):
    return jax.nn.softmax(x, axis=axis)

def _gelu(x):
    return jax.nn.gelu(x, approximate=True)

def _silu(x):
    return jax.nn.silu(x)

def _sigmoid(x):
    return jax.nn.sigmoid(x)

def _layernorm(x, axis=-1, eps=1e-05):
    m = jnp.mean(x, axis=axis, keepdims=True)
    v = jnp.var(x, axis=axis, keepdims=True)
    return (x - m) / jnp.sqrt(v + eps)

def _scatter_add(tgt, idx, src, axis=0):
    return tgt.at[idx].add(src)

def _segment_sum(src, seg, n):
    return jax.ops.segment_sum(src, seg, n)
kernel_name = 'mk_gnn_ffn_d2_gnn_r8_7d0d0f'

def setup_inputs(seed: int=0):
    np.random.seed(seed)
    _w = jnp.asarray

    def _rec_inputs():
        import jax
        import jax.numpy as jnp
        _gk = jax.random.key(seed)
        x = -8.776e-05 + 1 * jax.random.normal(jax.random.fold_in(_gk, 1), (6250, 256), jnp.float32)
        src = jax.random.randint(jax.random.fold_in(_gk, 2), (100000,), 0, 6250, jnp.int32)
        dst = jnp.minimum((6250 * jax.random.uniform(jax.random.fold_in(_gk, 3), (100000,)) ** 2.0).astype(jnp.int32), 49999)
        _o = jnp.argsort(dst, stable=True)
        src = src[_o]
        dst = dst[_o]
        return (x, src, dst)
    x, src, dst = _rec_inputs()

    def _L0_gnn_setup():
        import math
        import jax, jax.numpy as jnp
        import numpy as np
        N = 2500
        E = 40000
        D_IN = 256
        D_OUT = 256
        H = 8
        DK = D_OUT // H
        key = jax.random.key(seed)
        ks = jax.random.split(key, 16)
        h = jax.random.normal(ks[0], (N, D_IN), dtype=jnp.float32)
        src = jax.random.randint(ks[1], (E,), 0, N, dtype=jnp.int32)
        dst = jax.random.randint(ks[2], (E,), 0, N, dtype=jnp.int32)
        s = 1.0 / math.sqrt(D_IN)
        Wk = jax.random.uniform(ks[3], (D_OUT, D_IN), jnp.float32, -s, s)
        bk = jnp.zeros((D_OUT,), jnp.float32)
        Wq = jax.random.uniform(ks[4], (D_OUT, D_IN), jnp.float32, -s, s)
        bq = jnp.zeros((D_OUT,), jnp.float32)
        Wv = jax.random.uniform(ks[5], (D_OUT, D_IN), jnp.float32, -s, s)
        bv = jnp.zeros((D_OUT,), jnp.float32)
        so = 1.0 / math.sqrt(D_OUT)
        Wa = jax.random.uniform(ks[6], (D_OUT, D_OUT), jnp.float32, -so, so)
        ba = jnp.zeros((D_OUT,), jnp.float32)
        bound = math.sqrt(6.0 / (DK + DK))
        rel_att = jax.random.uniform(ks[7], (H, DK, DK), jnp.float32, -bound, bound)
        rel_msg = jax.random.uniform(ks[8], (H, DK, DK), jnp.float32, -bound, bound)
        rel_pri = jnp.ones((H,), jnp.float32)
        skip = jnp.ones((), jnp.float32)
        return {'h': h, 'src': src, 'dst': dst, 'Wk': Wk, 'bk': bk, 'Wq': Wq, 'bq': bq, 'Wv': Wv, 'bv': bv, 'Wa': Wa, 'ba': ba, 'rel_att': rel_att, 'rel_msg': rel_msg, 'rel_pri': rel_pri, 'skip': skip}
    _L0_gnn_all = _L0_gnn_setup()
    _L0_gnn_in = {k: v for k, v in _L0_gnn_all.items() if k in ('Wk', 'bk', 'Wq', 'bq', 'Wv', 'bv', 'Wa', 'ba', 'rel_att', 'rel_msg', 'rel_pri', 'skip')}
    del _L0_gnn_all

    def _L0_ffn_setup():
        import jax, jax.numpy as jnp
        import numpy as np
        B, N, D = (16, 512, 256)
        NUM_EXPERTS, TOP_K, HEADS = (4, 2, 4)
        N_EDGES = 131072
        LN_EPS = 1e-05

        def _layernorm(x, g, b):
            mu = x.mean(-1, keepdims=True)
            var = ((x - mu) ** 2).mean(-1, keepdims=True)
            return (x - mu) * jax.lax.rsqrt(var + LN_EPS) * g + b

        def _forward(x, edge_index, W_gat, att_src, att_dst, b_gat, ln_gamma, ln_beta, W1, b1, W2, b2):
            Bc, Nc, Dc = x.shape
            M = Bc * Nc
            x_flat = x.reshape(M, Dc)
            h = (x_flat @ W_gat).reshape(M, HEADS, NUM_EXPERTS)
            loops = jnp.arange(M, dtype=edge_index.dtype)
            src = jnp.concatenate([edge_index[0], loops])
            dst = jnp.concatenate([edge_index[1], loops])
            a_src = (h * att_src).sum(-1)
            a_dst = (h * att_dst).sum(-1)
            e = jax.nn.leaky_relu(a_src[src] + a_dst[dst], negative_slope=0.2)
            e_max = jax.ops.segment_max(e, dst, num_segments=M)
            ee = jnp.exp(e - e_max[dst])
            denom = jax.ops.segment_sum(ee, dst, num_segments=M)
            alpha = ee / (denom[dst] + 1e-16)
            msg = h[src] * alpha[:, :, None]
            agg = jax.ops.segment_sum(msg, dst, num_segments=M).reshape(M, HEADS * NUM_EXPERTS) + b_gat
            scores = _layernorm(agg, ln_gamma, ln_beta).reshape(M, HEADS, NUM_EXPERTS).mean(1)
            scores = scores.reshape(Bc, Nc, NUM_EXPERTS)
            topk_s, topk_i = jax.lax.top_k(scores, TOP_K)
            w = jax.nn.softmax(topk_s, axis=-1)
            out = jnp.zeros_like(x)
            for ei in range(NUM_EXPERTS):
                g = jnp.where(topk_i == ei, w, 0.0).sum(-1)
                hh = jax.nn.gelu(x @ W1[ei] + b1[ei], approximate=False)
                out = out + g[..., None] * (hh @ W2[ei] + b2[ei])
            return out
        key = jax.random.key(seed)
        ks = jax.random.split(key, 8)
        s = 0.05
        return {'x': jax.random.normal(ks[0], (B, N, D), jnp.float32), 'W_gat': jax.random.normal(ks[1], (D, HEADS * NUM_EXPERTS), jnp.float32) * s, 'att_src': jax.random.normal(ks[2], (HEADS, NUM_EXPERTS), jnp.float32) * s, 'att_dst': jax.random.normal(ks[3], (HEADS, NUM_EXPERTS), jnp.float32) * s, 'b_gat': jnp.zeros((HEADS * NUM_EXPERTS,), jnp.float32), 'ln_gamma': jnp.ones((HEADS * NUM_EXPERTS,), jnp.float32), 'ln_beta': jnp.zeros((HEADS * NUM_EXPERTS,), jnp.float32), 'W1': jax.random.normal(ks[4], (NUM_EXPERTS, D, 2 * D), jnp.float32) * s, 'b1': jnp.zeros((NUM_EXPERTS, 2 * D), jnp.float32), 'W2': jax.random.normal(ks[5], (NUM_EXPERTS, 2 * D, D), jnp.float32) * s, 'b2': jnp.zeros((NUM_EXPERTS, D), jnp.float32), 'edge_index': jax.random.randint(ks[6], (2, N_EDGES), 0, B * N, jnp.int32)}
    _L0_ffn_all = _L0_ffn_setup()
    _L0_ffn_in = {k: v for k, v in _L0_ffn_all.items() if k in ('W_gat', 'att_src', 'att_dst', 'b_gat', 'ln_gamma', 'ln_beta', 'W1', 'b1', 'W2', 'b2', 'edge_index')}
    del _L0_ffn_all

    def _L1_gnn_setup():
        import jax, jax.numpy as jnp
        import numpy as np
        N_NODES = 12500
        N_EDGES = 37500
        DIM = 256
        LN_EPS = 1e-05
        key = jax.random.key(seed)
        ks = jax.random.split(key, 4)
        scale = 1.0 / np.sqrt(DIM)
        h = jax.random.normal(ks[0], (N_NODES, DIM), dtype=jnp.float32)
        edge_index = jax.random.randint(ks[1], (2, N_EDGES), 0, N_NODES, dtype=jnp.int64)
        W1 = jax.random.normal(ks[2], (DIM, DIM), dtype=jnp.float32) * scale
        b1 = jnp.zeros((DIM,), dtype=jnp.float32)
        W2 = jax.random.normal(ks[3], (DIM, DIM), dtype=jnp.float32) * scale
        b2 = jnp.zeros((DIM,), dtype=jnp.float32)
        eps = jnp.zeros((), dtype=jnp.float32)
        gamma = jnp.ones((DIM,), dtype=jnp.float32)
        beta = jnp.zeros((DIM,), dtype=jnp.float32)
        return {'h': h, 'edge_index': edge_index, 'W1': W1, 'b1': b1, 'W2': W2, 'b2': b2, 'eps': eps, 'gamma': gamma, 'beta': beta}
    _L1_gnn_all = _L1_gnn_setup()
    _L1_gnn_in = {k: v for k, v in _L1_gnn_all.items() if k in ('W1', 'b1', 'W2', 'b2', 'eps', 'gamma', 'beta')}
    del _L1_gnn_all

    def _L1_ffn_setup():
        import jax, jax.numpy as jnp
        import numpy as np
        BN_EPS = 0.001

        def _bn(h, g, b, m, v):
            return g * (h - m) * jax.lax.rsqrt(v + BN_EPS) + b
        key = jax.random.key(seed)
        ks = jax.random.split(key, 8)
        B, F, Df = (256, 64, 256)
        E, H, D = (8, 256, 256)
        s1 = 1.0 / np.sqrt(Df)
        s2 = 1.0 / np.sqrt(H)
        return {'x': jax.random.normal(ks[0], (B, F, Df), jnp.float32), 'Wr': jax.random.normal(ks[1], (Df, E), jnp.float32) * s1, 'br': jnp.zeros((E,), jnp.float32), 'W1': jax.random.normal(ks[2], (E, Df, H), jnp.float32) * s1, 'b1': jnp.zeros((E, H), jnp.float32), 'g1': jnp.ones((E, H), jnp.float32), 'be1': jnp.zeros((E, H), jnp.float32), 'm1': jnp.zeros((E, H), jnp.float32), 'v1': jnp.ones((E, H), jnp.float32), 'W2': jax.random.normal(ks[3], (E, H, H), jnp.float32) * s2, 'b2': jnp.zeros((E, H), jnp.float32), 'g2': jnp.ones((E, H), jnp.float32), 'be2': jnp.zeros((E, H), jnp.float32), 'm2': jnp.zeros((E, H), jnp.float32), 'v2': jnp.ones((E, H), jnp.float32), 'Wo': jax.random.normal(ks[4], (E, H, D), jnp.float32) * s2, 'bo': jnp.zeros((E, D), jnp.float32)}
    _L1_ffn_all = _L1_ffn_setup()
    _L1_ffn_in = {k: v for k, v in _L1_ffn_all.items() if k in ('Wr', 'br', 'W1', 'b1', 'g1', 'be1', 'm1', 'v1', 'W2', 'b2', 'g2', 'be2', 'm2', 'v2', 'Wo', 'bo')}
    del _L1_ffn_all
    return {'x': x, 'src': src, 'dst': dst, 'L0_gnn_Wk': _L0_gnn_in['Wk'], 'L0_gnn_bk': _L0_gnn_in['bk'], 'L0_gnn_Wq': _L0_gnn_in['Wq'], 'L0_gnn_bq': _L0_gnn_in['bq'], 'L0_gnn_Wv': _L0_gnn_in['Wv'], 'L0_gnn_bv': _L0_gnn_in['bv'], 'L0_gnn_Wa': _L0_gnn_in['Wa'], 'L0_gnn_ba': _L0_gnn_in['ba'], 'L0_gnn_rel_att': _L0_gnn_in['rel_att'], 'L0_gnn_rel_msg': _L0_gnn_in['rel_msg'], 'L0_gnn_rel_pri': _L0_gnn_in['rel_pri'], 'L0_gnn_skip': _L0_gnn_in['skip'], 'L0_ffn_W_gat': _L0_ffn_in['W_gat'], 'L0_ffn_att_src': _L0_ffn_in['att_src'], 'L0_ffn_att_dst': _L0_ffn_in['att_dst'], 'L0_ffn_b_gat': _L0_ffn_in['b_gat'], 'L0_ffn_ln_gamma': _L0_ffn_in['ln_gamma'], 'L0_ffn_ln_beta': _L0_ffn_in['ln_beta'], 'L0_ffn_W1': _L0_ffn_in['W1'], 'L0_ffn_b1': _L0_ffn_in['b1'], 'L0_ffn_W2': _L0_ffn_in['W2'], 'L0_ffn_b2': _L0_ffn_in['b2'], 'L0_ffn_edge_index': _L0_ffn_in['edge_index'], 'L1_gnn_W1': _L1_gnn_in['W1'], 'L1_gnn_b1': _L1_gnn_in['b1'], 'L1_gnn_W2': _L1_gnn_in['W2'], 'L1_gnn_b2': _L1_gnn_in['b2'], 'L1_gnn_eps': _L1_gnn_in['eps'], 'L1_gnn_gamma': _L1_gnn_in['gamma'], 'L1_gnn_beta': _L1_gnn_in['beta'], 'L1_ffn_Wr': _L1_ffn_in['Wr'], 'L1_ffn_br': _L1_ffn_in['br'], 'L1_ffn_W1': _L1_ffn_in['W1'], 'L1_ffn_b1': _L1_ffn_in['b1'], 'L1_ffn_g1': _L1_ffn_in['g1'], 'L1_ffn_be1': _L1_ffn_in['be1'], 'L1_ffn_m1': _L1_ffn_in['m1'], 'L1_ffn_v1': _L1_ffn_in['v1'], 'L1_ffn_W2': _L1_ffn_in['W2'], 'L1_ffn_b2': _L1_ffn_in['b2'], 'L1_ffn_g2': _L1_ffn_in['g2'], 'L1_ffn_be2': _L1_ffn_in['be2'], 'L1_ffn_m2': _L1_ffn_in['m2'], 'L1_ffn_v2': _L1_ffn_in['v2'], 'L1_ffn_Wo': _L1_ffn_in['Wo'], 'L1_ffn_bo': _L1_ffn_in['bo']}

def reference(x, src, dst, L0_gnn_Wk, L0_gnn_bk, L0_gnn_Wq, L0_gnn_bq, L0_gnn_Wv, L0_gnn_bv, L0_gnn_Wa, L0_gnn_ba, L0_gnn_rel_att, L0_gnn_rel_msg, L0_gnn_rel_pri, L0_gnn_skip, L0_ffn_W_gat, L0_ffn_att_src, L0_ffn_att_dst, L0_ffn_b_gat, L0_ffn_ln_gamma, L0_ffn_ln_beta, L0_ffn_W1, L0_ffn_b1, L0_ffn_W2, L0_ffn_b2, L0_ffn_edge_index, L1_gnn_W1, L1_gnn_b1, L1_gnn_W2, L1_gnn_b2, L1_gnn_eps, L1_gnn_gamma, L1_gnn_beta, L1_ffn_Wr, L1_ffn_br, L1_ffn_W1, L1_ffn_b1, L1_ffn_g1, L1_ffn_be1, L1_ffn_m1, L1_ffn_v1, L1_ffn_W2, L1_ffn_b2, L1_ffn_g2, L1_ffn_be2, L1_ffn_m2, L1_ffn_v2, L1_ffn_Wo, L1_ffn_bo):
    import jax
    import jax.numpy as jnp

    def _L0_gnn_ref(h, src, dst, Wk, bk, Wq, bq, Wv, bv, Wa, ba, rel_att, rel_msg, rel_pri, skip):
        import math
        import jax, jax.numpy as jnp
        import numpy as np
        N = 2500
        E = 40000
        D_IN = 256
        D_OUT = 256
        H = 8
        DK = D_OUT // H
        n = h.shape[0]
        sqrt_dk = math.sqrt(DK)
        k = (h @ Wk.T + bk).reshape(n, H, DK)
        q = (h @ Wq.T + bq).reshape(n, H, DK)
        v = (h @ Wv.T + bv).reshape(n, H, DK)
        k = jnp.einsum('nhd,hde->nhe', k, rel_att)
        v = jnp.einsum('nhd,hde->nhe', v, rel_msg)
        score = jnp.einsum('ehd,ehd->eh', q[dst], k[src]) * rel_pri / sqrt_dk
        m = jax.ops.segment_max(score, dst, num_segments=n)
        ex = jnp.exp(score - m[dst])
        z = jax.ops.segment_sum(ex, dst, num_segments=n)
        attn = ex / z[dst]
        agg = jax.ops.segment_sum(v[src] * attn[:, :, None], dst, num_segments=n)
        t = agg.reshape(n, D_OUT)
        trans = t @ Wa.T + ba
        alpha = jax.nn.sigmoid(skip)
        return trans * alpha + h * (1.0 - alpha)

    def _L0_ffn_ref(x, W_gat, att_src, att_dst, b_gat, ln_gamma, ln_beta, W1, b1, W2, b2, edge_index):
        import jax, jax.numpy as jnp
        import numpy as np
        B, N, D = (16, 512, 256)
        NUM_EXPERTS, TOP_K, HEADS = (4, 2, 4)
        N_EDGES = 131072
        LN_EPS = 1e-05

        def _layernorm(x, g, b):
            mu = x.mean(-1, keepdims=True)
            var = ((x - mu) ** 2).mean(-1, keepdims=True)
            return (x - mu) * jax.lax.rsqrt(var + LN_EPS) * g + b

        def _forward(x, edge_index, W_gat, att_src, att_dst, b_gat, ln_gamma, ln_beta, W1, b1, W2, b2):
            Bc, Nc, Dc = x.shape
            M = Bc * Nc
            x_flat = x.reshape(M, Dc)
            h = (x_flat @ W_gat).reshape(M, HEADS, NUM_EXPERTS)
            loops = jnp.arange(M, dtype=edge_index.dtype)
            src = jnp.concatenate([edge_index[0], loops])
            dst = jnp.concatenate([edge_index[1], loops])
            a_src = (h * att_src).sum(-1)
            a_dst = (h * att_dst).sum(-1)
            e = jax.nn.leaky_relu(a_src[src] + a_dst[dst], negative_slope=0.2)
            e_max = jax.ops.segment_max(e, dst, num_segments=M)
            ee = jnp.exp(e - e_max[dst])
            denom = jax.ops.segment_sum(ee, dst, num_segments=M)
            alpha = ee / (denom[dst] + 1e-16)
            msg = h[src] * alpha[:, :, None]
            agg = jax.ops.segment_sum(msg, dst, num_segments=M).reshape(M, HEADS * NUM_EXPERTS) + b_gat
            scores = _layernorm(agg, ln_gamma, ln_beta).reshape(M, HEADS, NUM_EXPERTS).mean(1)
            scores = scores.reshape(Bc, Nc, NUM_EXPERTS)
            topk_s, topk_i = jax.lax.top_k(scores, TOP_K)
            w = jax.nn.softmax(topk_s, axis=-1)
            out = jnp.zeros_like(x)
            for ei in range(NUM_EXPERTS):
                g = jnp.where(topk_i == ei, w, 0.0).sum(-1)
                hh = jax.nn.gelu(x @ W1[ei] + b1[ei], approximate=False)
                out = out + g[..., None] * (hh @ W2[ei] + b2[ei])
            return out
        return _forward(x, edge_index, W_gat, att_src, att_dst, b_gat, ln_gamma, ln_beta, W1, b1, W2, b2)

    def _L1_gnn_ref(h, edge_index, W1, b1, W2, b2, eps, gamma, beta):
        import jax, jax.numpy as jnp
        import numpy as np
        N_NODES = 12500
        N_EDGES = 37500
        DIM = 256
        LN_EPS = 1e-05
        src, dst = (edge_index[0], edge_index[1])
        agg = jax.ops.segment_sum(h[src], dst, num_segments=h.shape[0])
        z = (1.0 + eps) * h + agg
        z = jax.nn.relu(z @ W1 + b1) @ W2 + b2
        r = z + h
        mu = jnp.mean(r, axis=-1, keepdims=True)
        var = jnp.mean(jnp.square(r - mu), axis=-1, keepdims=True)
        ln = (r - mu) * jax.lax.rsqrt(var + LN_EPS) * gamma + beta
        return jax.nn.relu(ln)

    def _L1_ffn_ref(x, Wr, br, W1, b1, g1, be1, m1, v1, W2, b2, g2, be2, m2, v2, Wo, bo):
        import jax, jax.numpy as jnp
        import numpy as np
        BN_EPS = 0.001

        def _bn(h, g, b, m, v):
            return g * (h - m) * jax.lax.rsqrt(v + BN_EPS) + b
        feat = jnp.mean(x, axis=0)
        w = jax.nn.softmax(feat @ Wr + br, axis=-1)
        h = jnp.einsum('bfd,edh->bfeh', x, W1) + b1
        h = jax.nn.relu(_bn(h, g1, be1, m1, v1))
        h = jnp.einsum('bfeh,ehk->bfek', h, W2) + b2
        h = jax.nn.relu(_bn(h, g2, be2, m2, v2))
        y = jnp.einsum('bfeh,ehd->bfed', h, Wo) + bo
        return jnp.einsum('bfed,fe->bfd', y, w)
    edge_index = jnp.stack([src, dst])
    x = x + _L0_gnn_ref(_layernorm(x, axis=-1), src, dst, L0_gnn_Wk, L0_gnn_bk, L0_gnn_Wq, L0_gnn_bq, L0_gnn_Wv, L0_gnn_bv, L0_gnn_Wa, L0_gnn_ba, L0_gnn_rel_att, L0_gnn_rel_msg, L0_gnn_rel_pri, L0_gnn_skip)
    x = x + _L0_ffn_ref(_layernorm(x, axis=-1)[None], L0_ffn_W_gat, L0_ffn_att_src, L0_ffn_att_dst, L0_ffn_b_gat, L0_ffn_ln_gamma, L0_ffn_ln_beta, L0_ffn_W1, L0_ffn_b1, L0_ffn_W2, L0_ffn_b2, L0_ffn_edge_index)[0]
    x = x + _L1_gnn_ref(_layernorm(x, axis=-1), edge_index, L1_gnn_W1, L1_gnn_b1, L1_gnn_W2, L1_gnn_b2, L1_gnn_eps, L1_gnn_gamma, L1_gnn_beta)
    x = x + _L1_ffn_ref(_layernorm(x, axis=-1)[None], L1_ffn_Wr, L1_ffn_br, L1_ffn_W1, L1_ffn_b1, L1_ffn_g1, L1_ffn_be1, L1_ffn_m1, L1_ffn_v1, L1_ffn_W2, L1_ffn_b2, L1_ffn_g2, L1_ffn_be2, L1_ffn_m2, L1_ffn_v2, L1_ffn_Wo, L1_ffn_bo)[0]
    return x

_drawn_inputs = setup_inputs


def setup_inputs(seed=0):
    import zlib

    import numpy as np

    out = dict(_drawn_inputs(seed))
    spreads = {'L0_gnn_bk': (0.0, 0.8),
     'L0_gnn_bq': (0.0, 0.594),
     'L0_gnn_bv': (0.0, 0.1),
     'L0_gnn_ba': (0.0, 0.1),
     'L0_gnn_rel_pri': (1.0, 0.6),
     'L0_ffn_b_gat': (0.0, 0.1),
     'L0_ffn_ln_gamma': (1.0, 0.2),
     'L0_ffn_ln_beta': (0.0, 0.1),
     'L0_ffn_b1': (0.0, 0.1),
     'L0_ffn_b2': (0.0, 0.1),
     'L1_gnn_b1': (0.0, 0.757),
     'L1_gnn_b2': (0.0, 0.5),
     'L1_gnn_gamma': (1.0, 0.2),
     'L1_gnn_beta': (0.0, 0.1),
     'L1_ffn_br': (0.0, 0.8),
     'L1_ffn_b1': (0.0, 0.483),
     'L1_ffn_g1': (1.0, 0.2),
     'L1_ffn_be1': (0.0, 0.532),
     'L1_ffn_m1': (0.0, 0.503),
     'L1_ffn_v1': (1.0, 0.6),
     'L1_ffn_b2': (0.0, 0.363),
     'L1_ffn_g2': (1.0, 0.2),
     'L1_ffn_be2': (0.0, 0.399),
     'L1_ffn_m2': (0.0, 0.352),
     'L1_ffn_v2': (1.0, 0.6),
     'L1_ffn_bo': (0.0, 0.271)}
    factors = {}
    for name, (base, spread) in spreads.items():
        noise = np.random.default_rng([zlib.crc32(name.encode()), seed]).standard_normal(out[name].shape)
        drawn = base * np.exp(spread * noise) if base else spread * noise
        out[name] = jnp.asarray(drawn.astype(out[name].dtype))
    for name, factor in factors.items():
        out[name] = (out[name] * factor).astype(out[name].dtype)
    return out
```

```python
import concourse.bass as bass
from concourse import mybir
from contextlib import ExitStack, contextmanager

P = 128
N = 6250
TILES = (N + P - 1) // P
DUMP = TILES
KEYS = 64
WAY = 8
NO_NODE = 16384
BIG = 1.0e30

D = 256
HEADS = 8
DK = D // HEADS
GH = 4
GE = 4
LN_EPS = 1e-05
BN_EPS = 0.001
UNIT = 4
SLOTS = 4
PAIRS = (TILES + 1) // 2
ROWS = (2 * PAIRS + 2) * P
WAY_PAIR = 2 * WAY
COLS1 = (100000 // P + 1 + WAY_PAIR - 1) // WAY_PAIR * WAY_PAIR
COLS2 = (131072 // P + TILES + WAY_PAIR - 1) // WAY_PAIR * WAY_PAIR
CHUNKS1 = (100000 // P + 1 + TILES + SLOTS * UNIT - 1) // (SLOTS * UNIT) * (SLOTS * UNIT)
CHUNKS2 = (131072 // P + TILES + TILES + SLOTS * UNIT - 1) // (SLOTS * UNIT) * (SLOTS * UNIT)
STAGE = 4

f32 = mybir.dt.float32
bf16 = mybir.dt.bfloat16
i32 = mybir.dt.int32
u32 = mybir.dt.uint32
ALU = mybir.AluOpType
ACT = mybir.ActivationFunctionType
AX = mybir.AxisListType


@contextmanager
def signal(nc, name):
    sem = nc.alloc_semaphore(name)
    yield sem
    nc.gpsimd.sem_clear(sem)
    nc.release_semaphore(sem)


def pool_dma_signals(nc, name, count=2):
    return [nc.alloc_semaphore(f"{name}_pool_dma{i}") for i in range(count)]


def columns(ap, width):
    return ap.unsqueeze(2).to_broadcast([ap.shape[0], ap.shape[1], width])


def rows(ap, count):
    return ap.unsqueeze(1).to_broadcast([ap.shape[0], count, ap.shape[1]])


def sort_edges(nc, name, cols, chunks, loops, src, dst, sorted_rec, consts):
    edges = src.shape[0]
    full = edges // P
    rest = edges - full * P
    used = full + (1 if rest else 0)
    steps = cols // WAY
    LIM = chunks * P
    ident, identb, tri, ones, iota = consts["ident"], consts["identb"], consts["tri"], consts["ones"], consts["iota"]
    with ExitStack() as ctx:
        def sb(n, s, d):
            return ctx.enter_context(nc.sbuf_tensor(f"{name}_{n}", s, d))

        def ps(n, s, d):
            return ctx.enter_context(nc.psum_tensor(f"{name}_{n}", s, d))

        def sem(n):
            return ctx.enter_context(signal(nc, f"{name}_{n}"))

        rec = sb("rec", [P, cols, 2], i32)
        raw = sb("raw", [P, 2, cols], i32)
        key_i = sb("key_i", [P, 2, cols], i32)
        key = sb("key", [P, 2, cols + WAY], f32)
        fill = sb("fill", [P, chunks, 2], i32)
        OL = sb("OL", [P, 2, WAY, P], bf16)
        OH = sb("OH", [P, 2, WAY, KEYS], bf16)
        OLT = sb("OLT", [P, WAY, P], f32)
        OLTb = sb("OLTb", [P, WAY, P], bf16)
        same = sb("same", [P, WAY, P], bf16)
        table = sb("table", [P, WAY, KEYS], f32)
        base = sb("base", [P, WAY, KEYS], f32)
        tot = sb("tot", [P, KEYS], f32)
        size = sb("size", [P, KEYS], f32)
        size_i = sb("size_i", [P, KEYS], i32)
        nul = sb("nul", [P, KEYS], f32)
        start = sb("start", [P, KEYS], f32)
        picked = sb("picked", [P, WAY, KEYS], f32)
        pos = sb("pos", [P, WAY], f32)
        pos_i = sb("pos_i", [P, 3, WAY], i32)
        over = sb("over", [P, WAY], f32)
        slot = sb("slot", [P, WAY], f32)
        addr = sb("addr", [P, 2, WAY], i32)
        recs = sb("recs", [P, 2, WAY, 2], i32)
        zb = sb("zb", [P, WAY * KEYS], bf16)
        H = ps("H", [P, WAY * KEYS], f32)
        G = ps("G", [P, 2 * KEYS], f32)
        OT = ps("OT", [P, WAY, P], bf16)
        A = ps("A", [P, WAY, P], f32)
        T = ps("T", [P, WAY * KEYS], f32)
        W = ps("W", [P, WAY * KEYS], f32)

        loaded, keyed = sem("loaded"), sem("keyed")
        hot, counted, filled = sem("hot"), sem("counted"), sem("filled")
        chain = sem("chain")
        totals, summed, based = sem("totals"), sem("summed"), sem("based")
        r_hot, turned, turned_sb, alike, alike_sb = (sem(n) for n in ("r_hot", "turned", "turned_sb", "alike", "alike_sb"))
        table_sb, ranked, addressed = (sem(n) for n in ("table_sb", "ranked", "addressed"))
        scattered = pool_dma_signals(nc, name)
        issue, lchain, updated, idle, freed = (sem(n) for n in ("issue", "lchain", "updated", "idle", "freed"))

        block = ctx.enter_context(nc.Block())

        @block.sync
        def _(sp):
            sp.wait_ge(filled, 1)
            for which, part in ((0, src), (1, dst)):
                sp.dma_start(raw[:, which, 0:full], part[0:full * P].rearrange("(p c) -> p c", p=P)).then_inc(loaded, 16)
                if rest:
                    with nc.allow_non_contiguous_dma("the last few edges"):
                        sp.dma_start(raw[0:rest, which, full:full + 1],
                                     part[full * P:edges].rearrange("(p c) -> p c", c=1)).then_inc(loaded, 16)
            sp.wait_ge(loaded, 64 if rest else 32)

        @block.gpsimd
        def _(pool):
            nc.gpsimd.memset(raw[:, 0, full:cols], 0)
            nc.gpsimd.memset(raw[:, 1, full:cols], KEYS * P - 1)
            nc.gpsimd.memset(fill[:, :, 0], 0)
            last = nc.gpsimd.memset(fill[:, :, 1], NO_NODE)
            if loops:
                last.then_inc(issue, 1)
                pool.wait_ge(issue, 1)
                for which in range(2):
                    last = nc.gpsimd.iota(raw[:, which, used:used + TILES], [[P, TILES]], base=0, channel_multiplier=1)
            last.then_inc(filled, 1)
            bound = pool.to_reg(LIM - 1)
            pool.sem_inc(freed, 1)
            pool.wait_ge(filled, 1)
            pool.dma_start(sorted_rec.rearrange("(p c) w -> p (c w)", p=P),
                           fill[:].rearrange("p c w -> p (c w)")).then_inc(scattered[1], 16)
            pool.wait_ge(scattered[1], 16)
            with pool.Fori(0, steps // 2) as t:
                for half in range(2):
                    pool.wait_ge(addressed, t * 2 + (half + 1))
                    pool.sem_inc(idle, 1)
                    for k in range(WAY):
                        nc.gpsimd.indirect_dma_start(
                            sorted_rec, bass.IndirectOffsetOnAxis(ap=addr[:, half, k:k + 1].bitcast(u32), axis=0),
                            recs[:, half, k, :], None, bounds_check=bound, oob_is_err=False).then_inc(scattered[half], 16)
                    if half:
                        pool.wait_ge(scattered[0], t * (16 * WAY) + 16 * WAY)
                    else:
                        pool.wait_ge(scattered[1], t * (16 * WAY) + 16)
                    pool.sem_inc(freed, 1)
            pool.wait_ge(scattered[0], 16 * WAY * (steps // 2))
            pool.wait_ge(scattered[1], 16 * WAY * (steps // 2) + 16)

        @block.vector
        def _(dve):
            n = [0]

            def link(ins):
                n[0] += 1
                ins.then_inc(chain, 1)
                dve.wait_ge(chain, n[0])

            dve.wait_ge(loaded, 64 if rest else 32)
            link(nc.vector.memset(zb[:], 0.0))
            link(nc.vector.memset(nul[:], 0.0))
            nc.vector.tensor_scalar(rec[:, :, 0], raw[:, 0, :], N - 1, None, ALU.min)
            nc.vector.tensor_copy(rec[:, :, 1], raw[:, 1, :])
            nc.vector.tensor_scalar(key_i[:, 0, :], raw[:, 1, :], P - 1, None, ALU.bitwise_and)
            link(nc.vector.tensor_scalar(key_i[:, 1, :], raw[:, 1, :], 7, None, ALU.logical_shift_right))
            nc.vector.memset(key[:, :, cols:cols + WAY], 0.0)
            link(nc.vector.tensor_copy(key[:, :, 0:cols], key_i[:]))

            def one_hots(t, half, signal):
                c = bass.ds(t * 2 * WAY + half * WAY, WAY)
                nc.vector.tensor_tensor(OL[:, half], rows(iota[:, :], WAY), columns(key[:, 0, c], P), ALU.is_equal)
                nc.vector.tensor_tensor(OH[:, half], rows(iota[:, 0:KEYS], WAY), columns(key[:, 1, c], KEYS),
                                        ALU.is_equal).then_inc(signal, 1)

            dve.sem_inc(keyed, 1)
            with dve.Fori(0, steps // 2) as t:
                for half in range(2):
                    dve.wait_ge(counted, t * 2 + half + 1)
                    one_hots(t, half, hot)
            dve.wait_ge(counted, steps + 2)
            link(nc.vector.tensor_copy(base[:].rearrange("p k h -> p (k h)"), H[:]))
            link(nc.vector.tensor_reduce(tot[:], base[:].rearrange("p k h -> p h k"), AX.X, ALU.add))
            dve.sem_inc(totals, 1)
            dve.wait_ge(summed, 1)
            link(nc.vector.tensor_scalar(size_i[:], G[:, 0:KEYS], float(P - 1), None, ALU.add))
            link(nc.vector.tensor_scalar(size_i[:], size_i[:], 7, None, ALU.logical_shift_right))
            link(nc.vector.tensor_scalar(size[:], size_i[:], float(P), None, ALU.mult))
            link(nc.vector.tensor_tensor_scan(start[:], size[:], nul[:], 0.0, ALU.add, ALU.add))
            link(nc.vector.tensor_tensor(start[:], start[:], size[:], ALU.subtract))
            link(nc.vector.tensor_tensor(tot[:], start[:], G[:, KEYS:2 * KEYS], ALU.add))
            for k in range(WAY):
                link(nc.vector.tensor_copy(size[:], base[:, k, :]))
                link(nc.vector.tensor_copy(base[:, k, :], tot[:]))
                link(nc.vector.tensor_tensor(tot[:], tot[:], size[:], ALU.add))
            dve.sem_inc(based, 1)
            dve.sem_inc(lchain, 8)

            def hot_for_rank(half, at):
                nc.vector.tensor_tensor(OL[:, half], rows(iota[:, :], WAY), columns(key[:, 0, at], P), ALU.is_equal)
                nc.vector.tensor_tensor(OH[:, half], rows(iota[:, 0:KEYS], WAY), columns(key[:, 1, at], KEYS),
                                        ALU.is_equal).then_inc(r_hot, 1)

            def earlier_alike():
                nc.vector.tensor_tensor(same[:], A[:], rows(tri[:, :], WAY), ALU.mult).then_inc(alike_sb, 1)

            hot_for_rank(0, slice(0, WAY))
            dve.wait_ge(alike, 1)
            earlier_alike()
            with dve.Fori(0, steps // 2) as t:
                for half in range(2):
                    dve.wait_ge(updated, t * 2 + half + 1)
                    hot_for_rank(1 - half, bass.ds(t * 2 * WAY + (half + 1) * WAY, WAY))
                    dve.wait_ge(ranked, t * 2 + half + 1)
                    step = t * 16 + half * 8 + 8
                    nc.vector.tensor_tensor(picked[:].rearrange("p k h -> p (k h)"), W[:],
                                            OH[:, half].rearrange("p k h -> p (k h)"), ALU.mult).then_inc(lchain, 1)
                    dve.wait_ge(lchain, step + 1)
                    nc.vector.tensor_reduce(pos[:], picked[:], AX.X, ALU.add).then_inc(lchain, 1)
                    dve.wait_ge(alike, t * 2 + half + 2)
                    earlier_alike()
                    dve.wait_ge(lchain, step + 2)
                    nc.vector.tensor_copy(pos_i[:, 0, :], pos[:]).then_inc(lchain, 1)
                    nc.vector.tensor_scalar(over[:], pos[:], float(LIM), float(1 << 20), ALU.is_ge, ALU.mult).then_inc(lchain, 1)
                    dve.wait_ge(lchain, step + 4)
                    nc.vector.tensor_scalar(pos_i[:, 1, :], pos_i[:, 0, :], 7, None, ALU.logical_shift_right).then_inc(lchain, 1)
                    nc.vector.tensor_scalar(pos_i[:, 2, :], pos_i[:, 0, :], P - 1, None, ALU.bitwise_and).then_inc(lchain, 1)
                    dve.wait_ge(lchain, step + 6)
                    nc.vector.scalar_tensor_tensor(slot[:], pos_i[:, 2, :], float(chunks), pos_i[:, 1, :],
                                                   ALU.mult, ALU.add).then_inc(lchain, 1)
                    dve.wait_ge(freed, t * 2 + half + 1)
                    nc.vector.tensor_copy(recs[:, half], rec[:, bass.ds(t * 2 * WAY + half * WAY, WAY), :]).then_inc(lchain, 1)
                    dve.wait_ge(lchain, step + 8)
                    nc.vector.tensor_tensor(addr[:, half], slot[:], over[:], ALU.add).then_inc(addressed, 1)

        @block.scalar
        def _(act):
            def turn_copy():
                nc.scalar.activation(OLT[:], OT[:], ACT.Copy)
                nc.scalar.activation(OLTb[:], OT[:], ACT.Copy).then_inc(turned_sb, 1)

            def table_copy():
                nc.scalar.activation(table[:].rearrange("p k h -> p (k h)"), T[:], ACT.Copy).then_inc(table_sb, 1)

            act.wait_ge(turned, 1)
            turn_copy()
            act.wait_ge(updated, 1)
            table_copy()
            with act.Fori(0, steps) as t:
                act.wait_ge(turned, t + 2)
                turn_copy()
                act.wait_ge(updated, t + 2)
                table_copy()

        @block.tensor
        def _(pe):
            pe.wait_ge(keyed, 1)
            nc.tensor.matmul(H[:], zb[:, 0:P], zb[:], start=True, stop=True, skip_group_check=True).then_inc(counted, 2)
            with pe.Fori(0, steps // 2) as t:
                for half in range(2):
                    pe.wait_ge(hot, t * 2 + half + 1)
                    for k in range(WAY):
                        last = nc.tensor.matmul(H[:, k * KEYS:(k + 1) * KEYS], OL[:, half, k, :], OH[:, half, k, :],
                                                start=False, stop=True, skip_group_check=True)
                    last.then_inc(counted, 1)
            pe.wait_ge(totals, 1)
            nc.tensor.matmul(G[:, 0:KEYS], ones[:, :], tot[:], start=True, stop=True, skip_group_check=True)
            nc.tensor.matmul(G[:, KEYS:2 * KEYS], tri[:, :], tot[:], start=True, stop=True, skip_group_check=True).then_inc(summed, 1)
            pe.wait_ge(based, 1)
            nc.tensor.matmul(T[:], ident[:, :], base[:].rearrange("p k h -> p (k h)"), start=True, stop=True,
                             skip_group_check=True).then_inc(updated, 1)

            def turn(half):
                for k in range(WAY):
                    last = nc.tensor.transpose(OT[:, k, :], OL[:, half, k, :], identb[:, :])
                last.then_inc(turned, 1)

            def compare():
                for k in range(WAY):
                    last = nc.tensor.matmul(A[:, k, :], OLTb[:, k, :], OLTb[:, k, :], start=True, stop=True, skip_group_check=True)
                last.then_inc(alike, 1)

            pe.wait_ge(r_hot, 1)
            turn(0)
            pe.wait_ge(turned_sb, 1)
            compare()
            with pe.Fori(0, steps // 2) as t:
                for half in range(2):
                    pe.wait_ge(alike_sb, t * 2 + half + 1)
                    pe.wait_ge(table_sb, t * 2 + half + 1)
                    pe.wait_ge(lchain, t * 16 + half * 8 + 1)
                    nc.tensor.matmul(W[:], zb[:, 0:P], zb[:], start=True, stop=True, skip_group_check=True)
                    for k in range(WAY):
                        w = W[:, k * KEYS:(k + 1) * KEYS]
                        nc.tensor.matmul(w, OLT[:, k, :], table[:, k, :], start=False, stop=True, skip_group_check=True)
                        last = nc.tensor.matmul(w, same[:, k, :], OH[:, half, k, :], start=False, stop=True, skip_group_check=True)
                    last.then_inc(ranked, 1)
                    pe.wait_ge(r_hot, t * 2 + half + 2)
                    turn(1 - half)
                    for k in range(WAY):
                        last = nc.tensor.matmul(T[:, k * KEYS:(k + 1) * KEYS], OL[:, half, k, :], OH[:, half, k, :],
                                                start=False, stop=True, skip_group_check=True)
                    last.then_inc(updated, 1)
                    pe.wait_ge(turned_sb, t * 2 + half + 2)
                    compare()


def make_consts(nc, ctx):
    def sb(n, s, d):
        return ctx.enter_context(nc.sbuf_tensor(n, s, d))
    c = {"ident": sb("ident", [P, P], f32), "identb": sb("identb", [P, P], bf16), "tri": sb("tri", [P, P], f32),
         "ones": sb("ones", [P, P], f32), "iota": sb("iota", [P, P], f32), "iota_i": sb("iota_i", [P, P], i32),
         "minus_half": sb("minus_half", [P, 1], f32)}
    with signal(nc, "const_step") as step, signal(nc, "const_done") as done, signal(nc, "const_float") as floated, nc.Block() as block:
        @block.gpsimd
        def _(pool):
            nc.gpsimd.memset(c["ident"][:], 0.0)
            nc.gpsimd.memset(c["identb"][:], 0.0)
            nc.gpsimd.memset(c["ones"][:], 1.0)
            nc.gpsimd.memset(c["minus_half"][:], -0.5)
            nc.gpsimd.iota(c["iota_i"][:], [[1, P]], base=0, channel_multiplier=0).then_inc(step, 1)
            pool.wait_ge(step, 1)
            for one in ("ident", "identb"):
                nc.gpsimd.affine_select(out=c[one][:], in_=c[one][:], pattern=[[-1, P]], compare_op=ALU.not_equal,
                                        fill=1.0, base=0, channel_multiplier=1)
            nc.gpsimd.affine_select(out=c["tri"][:], in_=c["ones"][:], pattern=[[1, P]], compare_op=ALU.is_gt,
                                    fill=0.0, base=0, channel_multiplier=-1).then_inc(done, 1)
            pool.wait_ge(done, 1)

        @block.vector
        def _(dve):
            dve.wait_ge(step, 1)
            nc.vector.tensor_copy(c["iota"][:], c["iota_i"][:]).then_inc(floated, 1)
            dve.wait_ge(floated, 1)
    return c




def chunk_arrays(nc, ctx, name, chunks, sorted_rec):
    wide = (chunks + P - 1) // P * P + 2 * UNIT
    arr = {
        "src": ctx.enter_context(nc.sbuf_tensor(f"{name}_src", [P, wide], i32)),
        "lo": ctx.enter_context(nc.sbuf_tensor(f"{name}_lo", [P, wide], f32)),
        "tile": ctx.enter_context(nc.sbuf_tensor(f"{name}_tile", [1, wide], i32)),
    }
    with (
        nc.sbuf_tensor(f"{name}_both", [P, chunks, 2], i32) as both,
        nc.sbuf_tensor(f"{name}_part", [P, 2, wide], i32) as part,
        nc.sbuf_tensor(f"{name}_none", [P, wide], f32) as none,
        signal(nc, f"{name}_in") as loaded,
        signal(nc, f"{name}_c") as chain,
        nc.Block() as block,
    ):
        @block.sync
        def _(sp):
            sp.dma_start(both[:].rearrange("p c w -> p (c w)"),
                         sorted_rec.rearrange("(p c) w -> p (c w)", p=P)).then_inc(loaded, 16)
            sp.wait_ge(loaded, 16)

        @block.vector
        def _(dve):
            n = [0]

            def link(ins):
                n[0] += 1
                ins.then_inc(chain, 1)
                dve.wait_ge(chain, n[0])

            nc.vector.memset(arr["src"][:], 0)
            nc.vector.memset(arr["tile"][:], DUMP)
            nc.vector.memset(none[:], 0.0)
            link(nc.vector.memset(part[:], NO_NODE))
            dve.wait_ge(loaded, 16)
            nc.vector.tensor_copy(arr["src"][:, 0:chunks], both[:, :, 0])
            link(nc.vector.tensor_copy(part[:, 1, 0:chunks], both[:, :, 1]))
            nc.vector.tensor_scalar(none[:], part[:, 1, :], float(NO_NODE), 1000.0, ALU.is_ge, ALU.mult)
            link(nc.vector.tensor_scalar(part[:, 0, :], part[:, 1, :], P - 1, None, ALU.bitwise_and))
            link(nc.vector.tensor_tensor(arr["lo"][:], part[:, 0, :], none[:], ALU.add))
            link(nc.vector.tensor_scalar(part[0:1, 0, :], part[0:1, 1, :], 7, None, ALU.logical_shift_right))
            link(nc.vector.tensor_scalar(arr["tile"][:], part[0:1, 0, :], DUMP, None, ALU.min))
    return arr


def segment_softmax_numerators(nc, name, heads, chunks, sorted_rec, S, consts):
    B = (chunks + P - 1) // P
    W = B * P
    ident = consts["ident"]
    with ExitStack() as ctx:
        def sb(n, s, d=f32):
            return ctx.enter_context(nc.sbuf_tensor(f"{name}_{n}", s, d))

        def sem(n):
            return ctx.enter_context(signal(nc, f"{name}_{n}"))

        Z = sb("Z", [P, heads, B, P])
        scan = sb("scan", [P, B, P])
        both = sb("both", [P, chunks, 2], i32)
        dst = sb("dst", [P, W])
        D = sb("D", [P, B, P])
        cut_f = sb("cut_f", [P, B, P])
        cut_b = sb("cut_b", [P, B, P])
        before = sb("before", [P, B, 2], i32)
        first = sb("first", [P, B])
        inner = sb("inner", [P, B])
        spread = sb("spread", [P, 3, B, heads])
        low = sb("low", [heads, 5, W])
        turn = [ctx.enter_context(nc.psum_tensor(f"{name}_turn{i}", [P, 4, P], f32)) for i in range(2)]
        lowp = [ctx.enter_context(nc.psum_tensor(f"{name}_low{i}", [P, 512], f32)) for i in range(3)]
        back = ctx.enter_context(nc.psum_tensor(f"{name}_back", [P, B, heads], f32))
        loaded, chain, ready, turned, used = (sem(n) for n in ("loaded", "chain", "ready", "turned", "used"))
        expd = sem("expd")

        jobs = [("dst", b) for b in range(B)] + [("S", h, b) for h in range(heads) for b in range(B)]
        outs = [(h, b) for h in range(heads) for b in range(B)]
        quads_in = [jobs[i:i + 4] for i in range(0, len(jobs), 4)]
        quads_out = [outs[i:i + 4] for i in range(0, len(outs), 4)]
        block = ctx.enter_context(nc.Block())

        @block.sync
        def _(sp):
            sp.dma_start(both[:].rearrange("p c w -> p (c w)"),
                         sorted_rec.rearrange("(p c) w -> p (c w)", p=P)).then_inc(loaded, 16)
            sp.wait_ge(ready, 1)
            whole = B - 1 if chunks % P else B
            last_slot = (P - 1) * chunks - 1
            with nc.allow_non_contiguous_dma("one word per chunk"):
                sp.dma_start(before[:, 0:whole, :],
                             sorted_rec[last_slot:last_slot + whole * P, :].rearrange("(b c) w -> c b w", c=P)
                             ).then_inc(loaded, 16)
                if chunks % P:
                    part = chunks - whole * P
                    sp.dma_start(before[0:part, whole:B, :],
                                 sorted_rec[last_slot + whole * P:last_slot + chunks, :].rearrange("(b c) w -> c b w", b=1)
                                 ).then_inc(loaded, 16)
            sp.wait_ge(loaded, 48 if chunks % P else 32)

        @block.vector
        def _(dve):
            n = [0]

            def link(ins):
                n[0] += 1
                ins.then_inc(chain, 1)
                dve.wait_ge(chain, n[0])

            link(nc.vector.memset(before[:], -1))
            dve.sem_inc(ready, 1)
            link(nc.vector.memset(dst[:], float(NO_NODE)))
            dve.wait_ge(loaded, 48 if chunks % P else 32)
            link(nc.vector.tensor_copy(dst[:, 0:chunks], both[:, :, 1]))
            dve.sem_inc(ready, 1)
            for i, quad in enumerate(quads_in):
                dve.wait_ge(turned, i + 1)
                for j, job in enumerate(quad):
                    to = D[:, job[1], :] if job[0] == "dst" else Z[:, job[1], job[2], :]
                    last = nc.vector.tensor_copy(to, turn[i % 2][:, j, :])
                last.then_inc(used, 1)
            dve.wait_ge(used, len(quads_in))
            link(nc.vector.tensor_copy(first[:], before[:, :, 1]))
            link(nc.vector.tensor_tensor(first[:], D[:, :, 0], first[:], ALU.not_equal))
            link(nc.vector.tensor_scalar(first[:], first[:], -BIG, None, ALU.mult))
            nc.vector.memset(cut_f[:, :, 0], -BIG)
            nc.vector.memset(cut_b[:, :, P - 1], -BIG)
            link(nc.vector.tensor_tensor(cut_f[:, :, 1:P], D[:, :, 1:P], D[:, :, 0:P - 1], ALU.not_equal))
            link(nc.vector.tensor_scalar(cut_f[:, :, 1:P], cut_f[:, :, 1:P], -BIG, None, ALU.mult))
            nc.vector.tensor_copy(cut_b[:, :, 0:P - 1], cut_f[:, :, 1:P])
            link(nc.vector.tensor_reduce(inner[:], cut_f[:, :, 1:P], AX.X, ALU.min))
            flat = lambda t: t.rearrange("p b e -> p (b e)")
            for h in range(heads):
                nc.vector.tensor_copy(spread[:, 1, :, h], first[:])
                nc.vector.tensor_copy(spread[:, 2, :, h], inner[:])
                link(nc.vector.tensor_tensor_scan(flat(scan[:]), flat(cut_f[:]), flat(Z[:, h]), -BIG, ALU.add, ALU.max))
                link(nc.vector.tensor_copy(spread[:, 0, :, h], scan[:, :, P - 1]))
            dve.sem_inc(ready, 1)

            def low_copy(which, count):
                at = 0
                for i in range(count):
                    width = min(512, W - at)
                    last = nc.vector.tensor_copy(low[:, which, at:at + width], lowp[i][0:heads, 0:width])
                    at += width
                link(last)

            NB = (W + 511) // 512
            for which in range(3):
                dve.wait_ge(turned, len(quads_in) + which + 1)
                low_copy(which, NB)
                dve.sem_inc(used, 1)
            link(nc.vector.tensor_tensor(low[:, 3, :], low[:, 1, :], low[:, 2, :], ALU.add))
            link(nc.vector.tensor_tensor_scan(low[:, 4, :], low[:, 3, :], low[:, 0, :], -BIG, ALU.add, ALU.max))
            link(nc.vector.memset(low[:, 3, 0:1], -BIG))
            link(nc.vector.tensor_tensor(low[:, 3, 1:W], low[:, 4, 0:W - 1], low[:, 1, 1:W], ALU.add))
            dve.sem_inc(ready, 1)
            dve.wait_ge(turned, len(quads_in) + 4)
            zfirst = Z[:, :, :, 0].rearrange("p h b -> p b h")
            link(nc.vector.tensor_tensor(zfirst, zfirst, back[:], ALU.max))
            for h in range(heads):
                link(nc.vector.tensor_tensor_scan(flat(Z[:, h]), flat(cut_f[:]), flat(Z[:, h]), -BIG, ALU.add, ALU.max))
            for h in range(heads):
                link(nc.vector.tensor_tensor_scan(flat(scan[:])[:, ::-1], flat(cut_b[:])[:, ::-1], flat(Z[:, h])[:, ::-1],
                                                  -BIG, ALU.add, ALU.max))
                link(nc.vector.tensor_copy(spread[:, 0, :, h], scan[:, :, 0]))
            dve.sem_inc(ready, 1)
            dve.wait_ge(turned, len(quads_in) + 5)
            low_copy(0, NB)
            link(nc.vector.memset(low[:, 3, W - 1:W], -BIG))
            link(nc.vector.tensor_tensor(low[:, 3, 0:W - 1], low[:, 1, 1:W], low[:, 2, 0:W - 1], ALU.add))
            link(nc.vector.tensor_tensor_scan(low[:, 4, ::-1], low[:, 3, ::-1], low[:, 0, ::-1], -BIG, ALU.add, ALU.max))
            link(nc.vector.tensor_tensor(low[:, 3, 0:W - 1], low[:, 4, 1:W], low[:, 1, 1:W], ALU.add))
            dve.sem_inc(ready, 1)
            dve.wait_ge(turned, len(quads_in) + 6)
            zlast = Z[:, :, :, P - 1].rearrange("p h b -> p b h")
            link(nc.vector.tensor_tensor(zlast, zlast, back[:], ALU.max))
            for h in range(heads):
                link(nc.vector.tensor_tensor_scan(flat(Z[:, h])[:, ::-1], flat(cut_b[:])[:, ::-1], flat(Z[:, h])[:, ::-1],
                                                  -BIG, ALU.add, ALU.max))
            dve.sem_inc(ready, 1)
            for i, quad in enumerate(quads_out):
                dve.wait_ge(turned, len(quads_in) + 6 + i + 1)
                for j, (h, b) in enumerate(quad):
                    s = S[:, h, b * P:(b + 1) * P]
                    last = nc.vector.tensor_tensor(s, s, turn[i % 2][:, j, :], ALU.subtract)
                last.then_inc(used, 1)

        @block.tensor
        def _(pe):
            pe.wait_ge(ready, 2)
            for i, quad in enumerate(quads_in):
                if i >= 2:
                    pe.wait_ge(used, i - 1)
                for j, job in enumerate(quad):
                    what = dst[:, job[1] * P:(job[1] + 1) * P] if job[0] == "dst" else S[:, job[1], job[2] * P:(job[2] + 1) * P]
                    last = nc.tensor.transpose(turn[i % 2][:, j, :], what, ident[:, :])
                last.then_inc(turned, 1)

            def per_chunk(which):
                for b in range(B):
                    last = nc.tensor.transpose(lowp[b // 4][0:heads, b % 4 * P:(b % 4 + 1) * P], spread[:, which, b, :], ident[:, :])
                last.then_inc(turned, 1)

            def per_chunk_back():
                for b in range(B):
                    last = nc.tensor.transpose(back[:, b, :], low[:, 3, b * P:(b + 1) * P], ident[0:heads, 0:heads])
                last.then_inc(turned, 1)

            pe.wait_ge(ready, 3)
            for which in range(3):
                if which:
                    pe.wait_ge(used, len(quads_in) + which)
                per_chunk(which)
            pe.wait_ge(ready, 4)
            per_chunk_back()
            pe.wait_ge(ready, 5)
            per_chunk(0)
            pe.wait_ge(ready, 6)
            per_chunk_back()
            pe.wait_ge(ready, 7)
            for i, quad in enumerate(quads_out):
                if i >= 2:
                    pe.wait_ge(used, len(quads_in) + 3 + i - 1)
                for j, (h, b) in enumerate(quad):
                    last = nc.tensor.transpose(turn[i % 2][:, j, :], Z[:, h, b, :], ident[:, :])
                last.then_inc(turned, 1)

        @block.scalar
        def _(act):
            act.wait_ge(used, len(quads_in) + 3 + len(quads_out))
            for h in range(heads):
                last = nc.scalar.activation(S[:, h, :], S[:, h, :], ACT.Exp)
            last.then_inc(expd, 1)
            act.wait_ge(expd, 1)


def load_tiles(engine, name, arr, at):
    regs = [engine.alloc_register(f"{name}_tile{k}") for k in range(UNIT)]
    engine.load(regs, arr["tile"][0:1, at])
    return [engine.snap(r, donate=True, min_val=0, max_val=DUMP) for r in regs]


def free_tiles(engine, tiles):
    for one in tiles:
        engine.free_register(one.val)


def gather_rows(nc, pool, table, got, idx, indexed, aside, gathered, steps, one_more=False):
    bound = pool.to_reg(table.shape[0] - 1)

    def step(slot):
        for k in range(UNIT):
            nc.gpsimd.indirect_dma_start(
                got[:, slot, k, :], None, table,
                bass.IndirectOffsetOnAxis(ap=idx[:, slot, k:k + 1].bitcast(u32), axis=0),
                bounds_check=bound, oob_is_err=False).then_inc(gathered[slot], 16)

    with pool.Fori(0, steps // SLOTS) as t:
        for slot in range(SLOTS):
            pool.wait_ge(indexed, t * SLOTS + (slot + 1))
            pool.sem_inc(aside, 1)
            step(slot)
    if one_more:
        pool.wait_ge(indexed, steps + 1)
        step(0)


def edge_scores(nc, name, width, heads, chunks, table, Q, arr, S, feats, consts):
    steps = chunks // UNIT
    ident, iota = consts["ident"], consts["iota"]
    qw = Q.shape[2]
    with ExitStack() as ctx:
        def sb(n, s, d=f32):
            return ctx.enter_context(nc.sbuf_tensor(f"{name}_{n}", s, d))

        def sem(n):
            return ctx.enter_context(signal(nc, f"{name}_{n}"))

        got = sb("got", [P, SLOTS, UNIT, width])
        idx = sb("idx", [P, SLOTS, UNIT], i32)
        OL = sb("OL", [P, 2, UNIT, P])
        OLT = sb("OLT", [P, 2, UNIT, P])
        prod = sb("prod", [P, UNIT * width])
        OT = [ctx.enter_context(nc.psum_tensor(f"{name}_OT{i}", [P, UNIT, P], f32)) for i in range(2)]
        QP = [ctx.enter_context(nc.psum_tensor(f"{name}_QP{i}", [P, UNIT, qw], f32)) for i in range(2)]
        indexed, hot, turned, turned_sb, queried, scored, multiplied, pool_aside, act_aside = (
            sem(n) for n in ("indexed", "hot", "turned", "turned_sb", "queried", "scored", "multiplied",
                             "pool_aside", "act_aside"))
        gathered = pool_dma_signals(nc, name, SLOTS)
        block = ctx.enter_context(nc.Block())

        @block.gpsimd
        def _(pool):
            gather_rows(nc, pool, table, got, idx, indexed, pool_aside, gathered, steps)

        @block.scalar
        def _(act):
            def indices(slot, at):
                nc.scalar.activation(idx[:, slot, :], arr["src"][:, at], ACT.Copy).then_inc(indexed, 1)

            def turn_copy(half):
                nc.scalar.activation(OLT[:, half], OT[half][:], ACT.Copy).then_inc(turned_sb, 1)

            indices(0, slice(0, UNIT))
            indices(1, slice(UNIT, 2 * UNIT))
            act.wait_ge(turned, 1)
            turn_copy(0)
            with act.Fori(0, steps // SLOTS) as t:
                for slot in range(SLOTS):
                    act.wait_ge(scored, t * SLOTS + (slot + 1))
                    act.sem_inc(act_aside, 1)
                    indices((slot + 2) % SLOTS, bass.ds(t * SLOTS * UNIT + (slot + 2) * UNIT, UNIT))
                    act.wait_ge(queried, t * SLOTS + (slot + 1))
                    act.wait_ge(turned, t * SLOTS + (slot + 2))
                    turn_copy((slot + 1) % 2)

        @block.vector
        def _(dve):
            def one_hots(half, at):
                nc.vector.tensor_tensor(OL[:, half], rows(iota[:, :], UNIT), columns(arr["lo"][:, at], P),
                                        ALU.is_equal).then_inc(hot, 1)

            dve.sem_inc(scored, 2)
            one_hots(0, slice(0, UNIT))
            with dve.Fori(0, steps // SLOTS) as t:
                for slot in range(SLOTS):
                    half = slot % 2
                    at = bass.ds(t * SLOTS * UNIT + slot * UNIT, UNIT)
                    one_hots(1 - half, bass.ds(t * SLOTS * UNIT + (slot + 1) * UNIT, UNIT))
                    dve.wait_ge(queried, t * SLOTS + (slot + 2))
                    dve.wait_ge(gathered[slot], t * (16 * UNIT) + 16 * UNIT)
                    if feats is None:
                        dve.wait_ge(scored, t * SLOTS + (slot + 2))
                        nc.vector.tensor_tensor(prod[:], got[:, slot].rearrange("p k d -> p (k d)"),
                                                QP[half][:].rearrange("p k d -> p (k d)"), ALU.mult).then_inc(multiplied, 1)
                        dve.wait_ge(multiplied, t * SLOTS + (slot + 1))
                        nc.vector.tensor_reduce(
                            S[:, :, at].rearrange("p h c -> p c h"),
                            prod[:].rearrange("p (k h d) -> p k h d", k=UNIT, h=heads), AX.X, ALU.add).then_inc(scored, 1)
                    else:
                        nc.vector.tensor_copy(feats[:, at, :], got[:, slot, :, 0:feats.shape[2]]).then_inc(multiplied, 1)
                        nc.vector.tensor_tensor(S[:, :, at].rearrange("p h c -> p c h"),
                                                got[:, slot, :, feats.shape[2]:feats.shape[2] + heads],
                                                QP[half][:], ALU.add).then_inc(scored, 1)
            dve.wait_ge(scored, steps + 2)

        @block.tensor
        def _(pe):
            def turn(half):
                for k in range(UNIT):
                    last = nc.tensor.transpose(OT[half][:, k, :], OL[:, half, k, :], ident[:, :])
                last.then_inc(turned, 1)

            pe.sem_inc(queried, 1)
            pe.wait_ge(hot, 1)
            turn(0)
            with pe.Fori(0, steps // SLOTS) as t:
                for slot in range(SLOTS):
                    half = slot % 2
                    tiles = load_tiles(pe, f"{name}_pe{slot}", arr, bass.ds(t * SLOTS * UNIT + slot * UNIT, UNIT))
                    pe.wait_ge(turned_sb, t * SLOTS + (slot + 1))
                    pe.wait_ge(scored, t * SLOTS + (slot + 1))
                    for k in range(UNIT):
                        last = nc.tensor.matmul(QP[half][:, k, :], OLT[:, half, k, :],
                                                Q[:, bass.ds(tiles[k], 1), :].rearrange("p a d -> p (a d)"),
                                                start=True, stop=True, skip_group_check=True)
                    last.then_inc(queried, 1)
                    free_tiles(pe, tiles)
                    pe.wait_ge(hot, t * SLOTS + (slot + 2))
                    turn(1 - half)


def edge_sums(nc, name, width, heads, chunks, table, AGG, arr, EX, consts):
    steps = chunks // UNIT
    iota = consts["iota"]
    total = AGG.shape[2]
    with ExitStack() as ctx:
        def sb(n, s, d=f32):
            return ctx.enter_context(nc.sbuf_tensor(f"{name}_{n}", s, d))

        def sem(n):
            return ctx.enter_context(signal(nc, f"{name}_{n}"))

        got = sb("got", [P, SLOTS, UNIT, width])
        W = sb("W", [P, 2, UNIT, total]) if EX is not None else None
        idx = sb("idx", [P, SLOTS, UNIT], i32)
        OL = sb("OL", [P, 2, UNIT, P])
        SP = [[ctx.enter_context(nc.psum_tensor(f"{name}_SP{i}{k}", [P, 512], f32)) for k in range(UNIT)] for i in range(2)]
        indexed, hot, weighted, summed, added, pool_aside, act_aside, cleared = (
            sem(n) for n in ("indexed", "hot", "weighted", "summed", "added", "pool_aside", "act_aside", "cleared"))
        gathered = pool_dma_signals(nc, name, SLOTS)
        CR = 2 * UNIT
        block = ctx.enter_context(nc.Block())

        @block.gpsimd
        def _(pool):
            nc.gpsimd.memset(AGG[:], 0.0).then_inc(cleared, 1)
            gather_rows(nc, pool, table, got, idx, indexed, pool_aside, gathered, steps, one_more=EX is not None)

        @block.scalar
        def _(act):
            def indices(slot, at):
                nc.scalar.activation(idx[:, slot, :], arr["src"][:, at], ACT.Copy).then_inc(indexed, 1)

            indices(0, slice(0, UNIT))
            indices(1, slice(UNIT, 2 * UNIT))
            with act.Fori(0, steps // SLOTS) as t:
                for slot in range(SLOTS):
                    act.wait_ge(weighted if EX is not None else summed,
                                t * (SLOTS * UNIT) + ((slot - 1) * UNIT + CR))
                    act.sem_inc(act_aside, 1)
                    indices((slot + 2) % SLOTS, bass.ds(t * SLOTS * UNIT + (slot + 2) * UNIT, UNIT))

        @block.vector
        def _(dve):
            def one_hots(half, at):
                nc.vector.tensor_tensor(OL[:, half], rows(iota[:, :], UNIT), columns(arr["lo"][:, at], P),
                                        ALU.is_equal).then_inc(hot, 1)

            def weigh(slot, k, c, at):
                per = (total - heads) // heads
                rows_in = got[:, slot, k, :]
                w = EX[:, :, at]
                nc.vector.tensor_tensor(
                    W[:, c, k, 0:total - heads].rearrange("p (h d) -> p h d", h=heads),
                    rows_in.rearrange("p (h d) -> p h d", h=heads), w.to_broadcast([P, heads, per]), ALU.mult)
                nc.vector.tensor_copy(W[:, c, k, total - heads:total], w.rearrange("p h c -> p (h c)")).then_inc(weighted, 1)

            dve.wait_ge(cleared, 1)
            dve.sem_inc(added, CR)
            one_hots(0, slice(0, UNIT))
            if EX is not None:
                dve.sem_inc(weighted, CR)
                dve.wait_ge(gathered[0], 16 * UNIT)
                for k in range(UNIT):
                    weigh(0, k, 0, slice(k, k + 1))
            with dve.Fori(0, steps // SLOTS) as t:
                for slot in range(SLOTS):
                    half = slot % 2
                    one_hots(1 - half, bass.ds(t * SLOTS * UNIT + (slot + 1) * UNIT, UNIT))
                    tiles = load_tiles(dve, f"{name}_dve{slot}", arr, bass.ds(t * SLOTS * UNIT + slot * UNIT, UNIT))
                    if EX is not None:
                        dve.wait_ge(gathered[(slot + 1) % SLOTS],
                                    t * (16 * UNIT) + (16 * UNIT if slot + 1 < SLOTS else 32 * UNIT))
                    for k in range(UNIT):
                        if EX is not None:
                            weigh((slot + 1) % SLOTS, k, 1 - half,
                                  bass.ds(t * SLOTS * UNIT + ((slot + 1) * UNIT + k), 1))
                        n = t * (SLOTS * UNIT) + (slot * UNIT + k)
                        dve.wait_ge(summed, n + (1 + CR))
                        dve.wait_ge(added, n + CR)
                        a = AGG[:, bass.ds(tiles[k], 1), :].rearrange("p a d -> p (a d)")
                        nc.vector.tensor_tensor(a, a, SP[half][k][:, 0:total], ALU.add).then_inc(added, 1)
                    free_tiles(dve, tiles)
            dve.wait_ge(added, steps * UNIT + CR)

        @block.tensor
        def _(pe):
            pe.sem_inc(summed, CR)
            with pe.Fori(0, steps // SLOTS) as t:
                for slot in range(SLOTS):
                    half = slot % 2
                    pe.wait_ge(hot, t * SLOTS + (slot + 1))
                    if EX is None:
                        pe.wait_ge(gathered[slot], t * (16 * UNIT) + 16 * UNIT)
                    for k in range(UNIT):
                        n = t * (SLOTS * UNIT) + (slot * UNIT + k)
                        if EX is not None:
                            pe.wait_ge(weighted, n + (1 + CR))
                        pe.wait_ge(added, n + 1)
                        nc.tensor.matmul(SP[half][k][:, 0:total], OL[:, half, k, :],
                                         W[:, half, k, :] if EX is not None else got[:, slot, k, :],
                                         start=True, stop=True, skip_group_check=True).then_inc(summed, 1)


def graph_sums(nc, chunks, AGG, arr, EX, feats, consts):
    steps = chunks // UNIT
    iota = consts["iota"]
    G = GH * GE
    with ExitStack() as ctx:
        def sb(n, s, d=f32):
            return ctx.enter_context(nc.sbuf_tensor(f"ev2_{n}", s, d))

        def sem(n):
            return ctx.enter_context(signal(nc, f"ev2_{n}"))

        W = sb("W", [P, 2, UNIT, G + GH])
        OL = sb("OL", [P, 2, UNIT, P])
        SP = [ctx.enter_context(nc.psum_tensor(f"ev2_SP{i}", [P, UNIT, G + GH], f32)) for i in range(2)]
        weighted, summed, added, chain = (sem(n) for n in ("weighted", "summed", "added", "chain"))
        block = ctx.enter_context(nc.Block())

        @block.vector
        def _(dve):
            def weigh(half, at):
                w = EX[:, :, at].rearrange("p h c -> p c h")
                nc.vector.tensor_tensor(OL[:, half], rows(iota[:, :], UNIT), columns(arr["lo"][:, at], P), ALU.is_equal)
                nc.vector.tensor_tensor(W[:, half, :, 0:G].rearrange("p k (h e) -> p k h e", h=GH),
                                        feats[:, at, :].rearrange("p k (h e) -> p k h e", h=GH),
                                        w.unsqueeze(3).to_broadcast([P, UNIT, GH, GE]), ALU.mult)
                nc.vector.tensor_copy(W[:, half, :, G:G + GH], w).then_inc(weighted, 1)

            nc.vector.memset(AGG[:], 0.0).then_inc(chain, 1)
            dve.wait_ge(chain, 1)
            dve.sem_inc(added, 1)
            weigh(0, slice(0, UNIT))
            with dve.Fori(0, steps // SLOTS) as t:
                for slot in range(SLOTS):
                    weigh(1 - slot % 2, bass.ds(t * SLOTS * UNIT + (slot + 1) * UNIT, UNIT))
                    tiles = load_tiles(dve, f"ev2_dve{slot}", arr, bass.ds(t * SLOTS * UNIT + slot * UNIT, UNIT))
                    dve.wait_ge(summed, t * SLOTS + (slot + 1))
                    dve.wait_ge(added, t * SLOTS + (slot + 1))
                    for k in range(UNIT):
                        a = AGG[:, k, bass.ds(tiles[k], 1), :].rearrange("p a d -> p (a d)")
                        last = nc.vector.tensor_tensor(a, a, SP[slot % 2][:, k, :], ALU.add)
                    last.then_inc(added, 1)
                    free_tiles(dve, tiles)
            dve.wait_ge(added, steps + 1)

        @block.tensor
        def _(pe):
            with pe.Fori(0, steps // SLOTS) as t:
                for slot in range(SLOTS):
                    pe.wait_ge(weighted, t * SLOTS + (slot + 1))
                    for k in range(UNIT):
                        last = nc.tensor.matmul(SP[slot % 2][:, k, :], OL[:, slot % 2, k, :], W[:, slot % 2, k, :],
                                                start=True, stop=True, skip_group_check=True)
                    last.then_inc(summed, 1)


def layer_norm(nc, root, link, x, stats, mean_var, rstd, out):
    link(nc.vector.bn_stats(stats, x))
    root.step_aside()
    link(nc.vector.bn_aggr(mean_var, stats))
    link(nc.vector.tensor_scalar(rstd[:], mean_var[:, 1:2], LN_EPS, None, ALU.add))
    root()
    link(nc.vector.tensor_scalar(out, x, mean_var[:, 0:1], rstd[:], ALU.subtract, ALU.mult))


def raise_to_minus_half(nc, pool, asked, raised, value, consts, times):
    with pool.Fori(0, times) as r:
        pool.wait_ge(asked, r + 1)
        nc.gpsimd.tensor_tensor(value, value, consts["minus_half"][:], ALU.pow).then_inc(raised, 1)


class Root:

    def __init__(self, engine, asked, raised, per, aside):
        self.aside = aside
        self.engine, self.asked, self.raised, self.per, self.n, self.base, self.t = engine, asked, raised, per, 0, 0, None

    def start(self, t):
        self.base, self.n, self.t = self.n, 0, t

    def step_aside(self):
        self.engine.sem_inc(self.aside, 1)

    def __call__(self):
        self.n += 1
        self.engine.sem_inc(self.asked, 1)
        self.engine.wait_ge(self.raised, self.n if self.t is None else self.t * self.per + (self.base + self.n))


class Chain:

    def __init__(self, engine, sem, per=0):
        self.engine, self.sem, self.per, self.n, self.base = engine, sem, per, 0, 0
        self.t = None

    def start(self, t):
        self.base, self.n, self.t = self.n, 0, t

    def link(self, ins):
        self.n += 1
        ins.then_inc(self.sem, 1)
        if self.t is None:
            self.engine.wait_ge(self.sem, self.n)
        else:
            self.engine.wait_ge(self.sem, self.t * self.per + (self.base + self.n))

    def end(self):
        assert self.n == self.per, (self.n, self.per)


def gnn_weights(nc, ctx, Wq, bq, Wk, bk, Wv, bv, Wa, ba, rel_att, rel_msg, rel_pri, skip, consts):
    wt = {}
    for n in ("q", "k", "v", "a"):
        wt[n] = ctx.enter_context(nc.sbuf_tensor(f"w_{n}", [P, 2, D], f32))
        wt["b" + n] = ctx.enter_context(nc.sbuf_tensor(f"b_{n}", [P, D], f32))
    wt["keep"] = ctx.enter_context(nc.sbuf_tensor("w_keep", [P, 2], f32))
    with ExitStack() as tmp:
        def sb(n, s, d=f32):
            return tmp.enter_context(nc.sbuf_tensor(f"gw_{n}", s, d))

        raw = {n: sb(f"raw_{n}", [P, 2, D]) for n in ("q", "k", "v", "a")}
        rel = {n: sb(f"rel_{n}", [P, 2, D]) for n in ("k", "v")}
        eye = sb("eye", [P, 2, D])
        pri = sb("pri", [P, HEADS])
        bias = {n: sb(f"bias_{n}", [P, 2]) for n in ("k", "v")}
        wide = {n: sb(f"wide_{n}", [P, 2, P]) for n in ("k", "v")}
        acc = {n: tmp.enter_context(nc.psum_tensor(f"gw_acc_{n}", [P, 2, D], f32)) for n in ("q", "k", "v", "a")}
        bacc = tmp.enter_context(nc.psum_tensor("gw_bacc", [P, 2, D], f32))
        zeroed, loaded, chain, made, folded, sig = (tmp.enter_context(signal(nc, f"gw_{n}")) for n in
                                                    ("zeroed", "loaded", "chain", "made", "folded", "sig"))
        block = tmp.enter_context(nc.Block())

        @block.gpsimd
        def _(pool):
            for n in ("k", "v"):
                last = nc.gpsimd.memset(rel[n][:], 0.0)
            last.then_inc(zeroed, 1)

        loads = 4 + 2 * HEADS + 1 + 2 + 2 + 1

        @block.sync
        def _(sp):
            for n, w in (("q", Wq), ("k", Wk), ("v", Wv), ("a", Wa)):
                sp.dma_start(raw[n][:], w.rearrange("(c p) d -> p c d", p=P)).then_inc(loaded, 16)
            sp.wait_ge(zeroed, 1)
            for n, r in (("k", rel_att), ("v", rel_msg)):
                for h in range(HEADS):
                    at = h * DK
                    sp.dma_start(rel[n][at % P:at % P + DK, at // P, at:at + DK], r[h]).then_inc(loaded, 16)
            sp.dma_start(pri[:], rel_pri.partition_broadcast(P)).then_inc(loaded, 16)
            for n, b in (("bq", bq), ("ba", ba)):
                sp.dma_start(wt[n][:], b.partition_broadcast(P)).then_inc(loaded, 16)
            with nc.allow_non_contiguous_dma("two short vectors"):
                for n, b in (("k", bk), ("v", bv)):
                    sp.dma_start(bias[n][:], b.rearrange("(c p) -> p c", p=P)).then_inc(loaded, 16)
                sp.dma_start(wt["keep"][:, 0:1], skip.partition_broadcast(P)).then_inc(loaded, 16)
            sp.wait_ge(loaded, 16 * loads)

        @block.scalar
        def _(act):
            act.wait_ge(loaded, 16 * loads)
            nc.scalar.activation(wt["keep"][:, 0:1], wt["keep"][:, 0:1], ACT.Sigmoid).then_inc(sig, 1)

        @block.vector
        def _(dve):
            c = Chain(dve, chain)
            c.link(nc.vector.memset(eye[:], 0.0))
            nc.vector.tensor_copy(eye[:, 0, 0:P], consts["ident"][:])
            c.link(nc.vector.tensor_copy(eye[:, 1, P:D], consts["ident"][:]))
            dve.wait_ge(loaded, 16 * loads)
            c.link(nc.vector.tensor_scalar(pri[:], pri[:], float(DK) ** -0.5, None, ALU.mult))
            for i in range(2):
                v = rel["k"][:, i, :].rearrange("p (h d) -> p h d", h=HEADS)
                c.link(nc.vector.tensor_tensor(v, v, columns(pri[:], DK), ALU.mult))
                for n in ("k", "v"):
                    c.link(nc.vector.tensor_copy(wide[n][:, i, :], bias[n][:, i:i + 1].to_broadcast([P, P])))
            dve.sem_inc(made, 1)
            dve.wait_ge(sig, 1)
            c.link(nc.vector.tensor_scalar(wt["keep"][:, 1:2], wt["keep"][:, 0:1], -1.0, 1.0, ALU.mult, ALU.add))
            dve.wait_ge(folded, 1)
            for n in ("q", "k", "v", "a"):
                nc.vector.tensor_copy(wt[n][:], acc[n][:])
            nc.vector.tensor_copy(wt["bk"][:], bacc[:, 0, :])
            c.link(nc.vector.tensor_copy(wt["bv"][:], bacc[:, 1, :]))

        @block.tensor
        def _(pe):
            pe.wait_ge(made, 1)
            for n, by in (("q", eye), ("k", rel["k"]), ("v", rel["v"]), ("a", eye)):
                for c in range(2):
                    for o in range(2):
                        nc.tensor.matmul(acc[n][:, c, :], raw[n][:, o, c * P:(c + 1) * P], by[:, o, :],
                                         start=(o == 0), stop=(o == 1), skip_group_check=True)
            for i, n in enumerate(("k", "v")):
                for o in range(2):
                    last = nc.tensor.matmul(bacc[:, i, :], wide[n][:, o, :], rel[n][:, o, :],
                                            start=(o == 0), stop=(o == 1), skip_group_check=True)
            last.then_inc(folded, 1)
    return wt


def copy_in(nc, x, X, later):
    spare = 2 * PAIRS * P
    with (
        nc.sbuf_tensor("ci_zero", [P, D], f32) as zero,
        signal(nc, "ci_zeroed") as zeroed,
        signal(nc, "ci_done") as done,
        nc.Block() as block,
    ):
        @block.vector
        def _(dve):
            nc.vector.memset(zero[:], 0.0).then_inc(zeroed, 1)

        @block.sync
        def _(sp):
            sp.dma_start(X[0:N, :], x).then_inc(done, 16)
            sp.wait_ge(zeroed, 1)
            first = TILES * P - N
            sp.dma_start(X[N:N + first, :], zero[0:first, :]).then_inc(done, 16)
            blank = [(X, i * P) for i in range(TILES, ROWS // P)] + [(one, r) for one in later for r in (spare, spare + P)]
            for one, r in blank:
                sp.dma_start(one[r:r + P, :], zero[:]).then_inc(done, 16)
            sp.wait_ge(done, 16 * (2 + len(blank)))


def project(nc, X, Q, K, V, wt, consts):
    ident = consts["ident"]
    with ExitStack() as ctx:
        def sb(n, s, d=f32):
            return ctx.enter_context(nc.sbuf_tensor(f"pj_{n}", s, d))

        def ps(n, s):
            return ctx.enter_context(nc.psum_tensor(f"pj_{n}", s, f32))

        def sem(n):
            return ctx.enter_context(signal(nc, f"pj_{n}"))

        x = sb("x", [P, 2, D])
        stats, mv, rstd = sb("stats", [P, 6]), sb("mv", [P, 2]), sb("rstd", [P, 1])
        xn = sb("xn", [P, 2, D])
        xT = sb("xT", [P, 2, 2, P])
        kv = sb("kv", [P, 2, 2, D])
        XT = [ps(f"XT{i}", [P, 2, P]) for i in range(2)]
        QP = [ps(f"QP{i}", [P, 512]) for i in range(2)]
        KV = [ps(f"KV{i}", [P, 2, D]) for i in range(2)]
        loaded = [sem("loaded0"), sem("loaded1")]
        stored = [sem("stored0"), sem("stored1")]
        normed, turned, turned_sb, projected, ready, chain, free = (
            sem(n) for n in ("normed", "turned", "turned_sb", "projected", "ready", "chain", "free"))
        asked, raised, aside = sem("asked"), sem("raised"), sem("aside")
        block = ctx.enter_context(nc.Block())

        @block.gpsimd
        def _(pool):
            raise_to_minus_half(nc, pool, asked, raised, rstd[:], consts, 2 * PAIRS + 1)

        @block.sync
        def _(sp):
            def load(half, at):
                sp.dma_start(x[:, half, :], X[at, :]).then_inc(loaded[half], 16)

            sp.sem_inc(free, 2)
            load(0, slice(0, P))
            load(1, slice(P, 2 * P))
            with sp.Fori(0, PAIRS) as t:
                for half in range(2):
                    sp.wait_ge(normed, t * 2 + half + 1)
                    load(half, bass.ds((t * 2 + half + 2) * P, P))
                    sp.wait_ge(ready, t * 2 + half + 3)
                    at = bass.ds((t * 2 + half) * P, P)
                    sp.dma_start(K[at, :], kv[:, half, 0, :]).then_inc(stored[half], 16)
                    sp.dma_start(V[at, :], kv[:, half, 1, :]).then_inc(stored[half], 16)
                    sp.wait_ge(stored[half], t * 32 + 32)
                    sp.sem_inc(free, 1)
            for half in range(2):
                sp.wait_ge(loaded[half], 16 * (PAIRS + 1))

        @block.vector
        def _(dve):
            c = Chain(dve, chain, per=2 * 4)
            root = Root(dve, asked, raised, 2, aside)

            def norm(t, half, step):
                dve.wait_ge(loaded[half], t * 16 + (16 if step < 2 else 32))
                layer_norm(nc, root, c.link, x[:, half, :], stats[:], mv[:], rstd, xn[:, half, :])
                dve.sem_inc(normed, 1)

            dve.sem_inc(ready, 2)
            norm(0, 0, 0)
            with dve.Fori(0, PAIRS) as t:
                c.start(t)
                root.start(t)
                for half in range(2):
                    norm(t, 1 - half, 0 if half == 0 else 2)
                    dve.wait_ge(projected, t * 2 + half + 2)
                    dve.wait_ge(free, t * 2 + half + 1)
                    nc.vector.tensor_tensor(Q[:, bass.ds(t * 2 + half, 1), :].rearrange("p a d -> p (a d)"),
                                            QP[half][:, 0:D], wt["bq"][:], ALU.add)
                    nc.vector.tensor_tensor(kv[:, half, 0, :], KV[half][:, 0, :], wt["bk"][:], ALU.add)
                    nc.vector.tensor_tensor(kv[:, half, 1, :], KV[half][:, 1, :], wt["bv"][:], ALU.add).then_inc(ready, 1)
                c.end()

        @block.scalar
        def _(act):
            def turn_copy(half):
                nc.scalar.activation(xT[:, half], XT[half][:], ACT.Copy).then_inc(turned_sb, 1)

            act.wait_ge(turned, 1)
            turn_copy(0)
            with act.Fori(0, PAIRS) as t:
                for half in range(2):
                    act.wait_ge(projected, t * 2 + half + 1)
                    act.wait_ge(turned, t * 2 + half + 2)
                    turn_copy(1 - half)

        @block.tensor
        def _(pe):
            def turn(half):
                for c in range(2):
                    last = nc.tensor.transpose(XT[half][:, c, :], xn[:, half, c * P:(c + 1) * P], ident[:, :])
                last.then_inc(turned, 1)

            pe.wait_ge(normed, 1)
            turn(0)
            pe.sem_inc(projected, 1)
            with pe.Fori(0, PAIRS) as t:
                for half in range(2):
                    pe.wait_ge(turned_sb, t * 2 + half + 1)
                    pe.wait_ge(ready, t * 2 + half + 1)
                    for n, to in (("q", QP[half][:, 0:D]), ("k", KV[half][:, 0, :]), ("v", KV[half][:, 1, :])):
                        for c in range(2):
                            last = nc.tensor.matmul(to, xT[:, half, c, :], wt[n][:, c, :], start=(c == 0), stop=(c == 1),
                                                    skip_group_check=True)
                    last.then_inc(projected, 1)
                    pe.wait_ge(normed, t * 2 + half + 2)
                    turn(1 - half)


def attention_out(nc, X, AGG, X_out, wt, consts):
    ident = consts["ident"]
    with ExitStack() as ctx:
        def sb(n, s, d=f32):
            return ctx.enter_context(nc.sbuf_tensor(f"ao_{n}", s, d))

        def ps(n, s):
            return ctx.enter_context(nc.psum_tensor(f"ao_{n}", s, f32))

        def sem(n):
            return ctx.enter_context(signal(nc, f"ao_{n}"))

        x = sb("x", [P, 2, D])
        stats, mv, rstd = sb("stats", [P, 6]), sb("mv", [P, 2]), sb("rstd", [P, 1])
        z = sb("z", [P, HEADS])
        xn, mean = sb("xn", [P, 2, D]), sb("mean", [P, 2, D])
        mT = sb("mT", [P, 2, 2, P])
        u, out = sb("u", [P, D]), sb("out", [P, 2, D])
        MT = [ps(f"MT{i}", [P, 2, P]) for i in range(2)]
        YP = [ps(f"YP{i}", [P, 512]) for i in range(2)]
        loaded = [sem("loaded0"), sem("loaded1")]
        stored = [sem("stored0"), sem("stored1")]
        normed, turned, turned_sb, projected, ready, chain, free = (
            sem(n) for n in ("normed", "turned", "turned_sb", "projected", "ready", "chain", "free"))
        asked, raised, aside = sem("asked"), sem("raised"), sem("aside")
        block = ctx.enter_context(nc.Block())

        @block.gpsimd
        def _(pool):
            raise_to_minus_half(nc, pool, asked, raised, rstd[:], consts, 2 * PAIRS + 1)

        @block.sync
        def _(sp):
            def load(half, at):
                sp.dma_start(x[:, half, :], X[at, :]).then_inc(loaded[half], 16)

            sp.sem_inc(free, 2)
            load(0, slice(0, P))
            load(1, slice(P, 2 * P))
            with sp.Fori(0, PAIRS) as t:
                for half in range(2):
                    sp.wait_ge(ready, t * 2 + half + 3)
                    sp.dma_start(X_out[bass.ds((t * 2 + half) * P, P), :], out[:, half, :]).then_inc(stored[half], 16)
                    load(half, bass.ds((t * 2 + half + 2) * P, P))
                    sp.wait_ge(stored[half], t * 16 + 16)
                    sp.sem_inc(free, 1)
            for half in range(2):
                sp.wait_ge(loaded[half], 16 * (PAIRS + 1))

        @block.vector
        def _(dve):
            c = Chain(dve, chain, per=2 * (4 + 3 + 3))
            root = Root(dve, asked, raised, 2, aside)

            def front(half, at, arrived):
                dve.wait_ge(loaded[half], arrived)
                layer_norm(nc, root, c.link, x[:, half, :], stats[:], mv[:], rstd, xn[:, half, :])
                c.link(nc.vector.tensor_scalar(z[:], AGG[:, at, D:D + HEADS].rearrange("p a h -> p (a h)"), 1e-30, None, ALU.max))
                c.link(nc.vector.reciprocal(z[:], z[:]))
                c.link(nc.vector.tensor_tensor(mean[:, half, :].rearrange("p (h d) -> p h d", h=HEADS),
                                               AGG[:, at, 0:D].rearrange("p a (h d) -> p (a h) d", h=HEADS),
                                               columns(z[:], DK), ALU.mult))
                dve.sem_inc(normed, 1)

            dve.sem_inc(ready, 2)
            front(0, slice(0, 1), 16)
            with dve.Fori(0, PAIRS) as t:
                c.start(t)
                root.start(t)
                for half in range(2):
                    front(1 - half, bass.ds(t * 2 + half + 1, 1), t * 16 + (16 if half == 0 else 32))
                    dve.wait_ge(projected, t * 2 + half + 2)
                    dve.wait_ge(free, t * 2 + half + 1)
                    c.link(nc.vector.tensor_tensor(u[:], YP[half][:, 0:D], wt["ba"][:], ALU.add))
                    c.link(nc.vector.scalar_tensor_tensor(out[:, half, :], u[:], wt["keep"][:, 0:1], x[:, half, :],
                                                          ALU.mult, ALU.add))
                    c.link(nc.vector.scalar_tensor_tensor(out[:, half, :], xn[:, half, :], wt["keep"][:, 1:2],
                                                          out[:, half, :], ALU.mult, ALU.add))
                    dve.sem_inc(ready, 1)
                c.end()

        @block.scalar
        def _(act):
            def turn_copy(half):
                nc.scalar.activation(mT[:, half], MT[half][:], ACT.Copy).then_inc(turned_sb, 1)

            act.wait_ge(turned, 1)
            turn_copy(0)
            with act.Fori(0, PAIRS) as t:
                for half in range(2):
                    act.wait_ge(projected, t * 2 + half + 1)
                    act.wait_ge(turned, t * 2 + half + 2)
                    turn_copy(1 - half)

        @block.tensor
        def _(pe):
            def turn(half):
                for c in range(2):
                    last = nc.tensor.transpose(MT[half][:, c, :], mean[:, half, c * P:(c + 1) * P], ident[:, :])
                last.then_inc(turned, 1)

            pe.sem_inc(projected, 1)
            pe.wait_ge(normed, 1)
            turn(0)
            with pe.Fori(0, PAIRS) as t:
                for half in range(2):
                    pe.wait_ge(turned_sb, t * 2 + half + 1)
                    pe.wait_ge(ready, t * 2 + half + 1)
                    for c in range(2):
                        last = nc.tensor.matmul(YP[half][:, 0:D], mT[:, half, c, :], wt["a"][:, c, :],
                                                start=(c == 0), stop=(c == 1), skip_group_check=True)
                    last.then_inc(projected, 1)
                    pe.wait_ge(normed, t * 2 + half + 2)
                    turn(1 - half)


def load_weights(nc, name, items):
    with signal(nc, f"{name}_loaded") as loaded, nc.Block() as block:
        @block.sync
        def _(sp):
            with nc.allow_non_contiguous_dma("short vectors"):
                for to, part in items:
                    sp.dma_start(to, part).then_inc(loaded, 16)
            sp.wait_ge(loaded, 16 * len(items))


def gat_project(nc, X, TAB, ADST, W_gat, att_src, att_dst, consts):
    ident = consts["ident"]
    G = GH * GE
    with ExitStack() as ctx:
        def sb(n, s, d=f32):
            return ctx.enter_context(nc.sbuf_tensor(f"gp_{n}", s, d))

        def ps(n, s):
            return ctx.enter_context(nc.psum_tensor(f"gp_{n}", s, f32))

        def sem(n):
            return ctx.enter_context(signal(nc, f"gp_{n}"))

        w = sb("w", [P, 2, G])
        att = sb("att", [P, 2, G])
        w24 = sb("w24", [P, 2, G + 2 * GH])
        tmp = sb("tmp", [P, G])
        x = sb("x", [P, 2, D])
        stats, mv, rstd = sb("stats", [P, 6]), sb("mv", [P, 2]), sb("rstd", [P, 1])
        xn = sb("xn", [P, 2, D])
        xT = sb("xT", [P, 2, 2, P])
        row = sb("row", [P, 2, G + GH])
        XT = [ps(f"XT{i}", [P, 2, P]) for i in range(2)]
        YP = [ps(f"YP{i}", [P, 512]) for i in range(2)]
        loaded = [sem("loaded0"), sem("loaded1")]
        stored = [sem("stored0"), sem("stored1")]
        normed, turned, turned_sb, projected, ready, chain, free, wl = (
            sem(n) for n in ("normed", "turned", "turned_sb", "projected", "ready", "chain", "free", "wl"))
        asked, raised, aside = sem("asked"), sem("raised"), sem("aside")
        block = ctx.enter_context(nc.Block())

        @block.gpsimd
        def _(pool):
            raise_to_minus_half(nc, pool, asked, raised, rstd[:], consts, 2 * PAIRS + 1)

        @block.sync
        def _(sp):
            def load(half, at):
                sp.dma_start(x[:, half, :], X[at, :]).then_inc(loaded[half], 16)

            sp.dma_start(w[:], W_gat.rearrange("(c p) g -> p c g", p=P)).then_inc(wl, 16)
            sp.dma_start(att[:, 0, :], att_src.rearrange("h e -> (h e)").partition_broadcast(P)).then_inc(wl, 16)
            sp.dma_start(att[:, 1, :], att_dst.rearrange("h e -> (h e)").partition_broadcast(P)).then_inc(wl, 16)
            sp.sem_inc(free, 2)
            load(0, slice(0, P))
            load(1, slice(P, 2 * P))
            with sp.Fori(0, PAIRS) as t:
                for half in range(2):
                    sp.wait_ge(normed, t * 2 + half + 1)
                    load(half, bass.ds((t * 2 + half + 2) * P, P))
                    sp.wait_ge(ready, t * 2 + half + 3)
                    sp.dma_start(TAB[bass.ds((t * 2 + half) * P, P), :], row[:, half, :]).then_inc(stored[half], 16)
                    sp.wait_ge(stored[half], t * 16 + 16)
                    sp.sem_inc(free, 1)
            for half in range(2):
                sp.wait_ge(loaded[half], 16 * (PAIRS + 1))

        @block.vector
        def _(dve):
            c = Chain(dve, chain, per=8)
            root = Root(dve, asked, raised, 2, aside)
            dve.wait_ge(wl, 48)
            for i in range(2):
                nc.vector.tensor_copy(w24[:, i, 0:G], w[:, i, :])
                for j in range(2):
                    c.link(nc.vector.tensor_tensor(tmp[:], w[:, i, :], att[:, j, :], ALU.mult))
                    c.link(nc.vector.tensor_reduce(w24[:, i, G + j * GH:G + (j + 1) * GH],
                                                   tmp[:].rearrange("p (h e) -> p h e", h=GH), AX.X, ALU.add))

            def norm(half, arrived):
                dve.wait_ge(loaded[half], arrived)
                layer_norm(nc, root, c.link, x[:, half, :], stats[:], mv[:], rstd, xn[:, half, :])
                dve.sem_inc(normed, 1)

            dve.sem_inc(ready, 2)
            norm(0, 16)
            with dve.Fori(0, PAIRS) as t:
                c.start(t)
                root.start(t)
                for half in range(2):
                    norm(1 - half, t * 16 + (16 if half == 0 else 32))
                    dve.wait_ge(projected, t * 2 + half + 2)
                    dve.wait_ge(free, t * 2 + half + 1)
                    nc.vector.tensor_copy(row[:, half, :], YP[half][:, 0:G + GH])
                    nc.vector.tensor_scalar(ADST[:, bass.ds(t * 2 + half, 1), :].rearrange("p a d -> p (a d)"),
                                            YP[half][:, G + GH:G + 2 * GH], 1.0, None, ALU.mult).then_inc(ready, 1)
                c.end()

        @block.scalar
        def _(act):
            def turn_copy(half):
                nc.scalar.activation(xT[:, half], XT[half][:], ACT.Copy).then_inc(turned_sb, 1)

            act.wait_ge(turned, 1)
            turn_copy(0)
            with act.Fori(0, PAIRS) as t:
                for half in range(2):
                    act.wait_ge(projected, t * 2 + half + 1)
                    act.wait_ge(turned, t * 2 + half + 2)
                    turn_copy(1 - half)

        @block.tensor
        def _(pe):
            def turn(half):
                for c in range(2):
                    last = nc.tensor.transpose(XT[half][:, c, :], xn[:, half, c * P:(c + 1) * P], ident[:, :])
                last.then_inc(turned, 1)

            pe.sem_inc(projected, 1)
            pe.wait_ge(normed, 1)
            turn(0)
            with pe.Fori(0, PAIRS) as t:
                for half in range(2):
                    pe.wait_ge(turned_sb, t * 2 + half + 1)
                    pe.wait_ge(ready, t * 2 + half + 1)
                    for c in range(2):
                        last = nc.tensor.matmul(YP[half][:, 0:G + 2 * GH], xT[:, half, c, :], w24[:, c, :],
                                                start=(c == 0), stop=(c == 1), skip_group_check=True)
                    last.then_inc(projected, 1)
                    pe.wait_ge(normed, t * 2 + half + 2)
                    turn(1 - half)


def leaky(nc, S, chunks):
    with nc.sbuf_tensor("lk_low", [P, S.shape[2]], f32) as low, signal(nc, "lk_chain") as chain, nc.Block() as block:
        @block.vector
        def _(dve):
            c = Chain(dve, chain)
            for h in range(S.shape[1]):
                c.link(nc.vector.tensor_scalar(low[:], S[:, h, :], 0.2, None, ALU.mult))
                c.link(nc.vector.tensor_tensor(S[:, h, :], S[:, h, :], low[:], ALU.max))


def gates(nc, AGG, GATE, b_gat, gamma, beta, consts):
    G = GH * GE
    T = AGG.shape[2]
    with ExitStack() as ctx:
        def sb(n, s, d=f32):
            return ctx.enter_context(nc.sbuf_tensor(f"gt_{n}", s, d))

        par = sb("par", [P, 3, G])
        a = sb("a", [P, T, G])
        sq = sb("sq", [P, T, G])
        z = sb("z", [P, T, GH])
        mean, var = sb("mean", [P, T]), sb("var", [P, T])
        sc, ex, rank, cmp, best = sb("sc", [P, T, GE]), sb("ex", [P, T, GE]), sb("rank", [P, T, GE]), sb("cmp", [P, T]), sb("best", [P, T])
        wl, chain, ready, done, asked, raised = (
            ctx.enter_context(signal(nc, f"gt_{n}")) for n in ("wl", "chain", "ready", "done", "asked", "raised"))
        block = ctx.enter_context(nc.Block())

        @block.gpsimd
        def _(pool):
            pool.wait_ge(asked, 1)
            nc.gpsimd.tensor_tensor(var[:], var[:], consts["minus_half"][:].to_broadcast([P, T]), ALU.pow).then_inc(raised, 1)

        @block.sync
        def _(sp):
            for i, v in enumerate((b_gat, gamma, beta)):
                sp.dma_start(par[:, i, :], v.partition_broadcast(P)).then_inc(wl, 16)
            sp.wait_ge(wl, 48)

        @block.scalar
        def _(act):
            act.wait_ge(ready, 1)
            nc.scalar.activation(ex[:], sc[:], ACT.Exp).then_inc(done, 1)

        @block.vector
        def _(dve):
            c = Chain(dve, chain)
            V = nc.vector
            bc = lambda i: par[:, i, :].unsqueeze(1).to_broadcast([P, T, G])
            wide = lambda v, n: v.unsqueeze(2).to_broadcast([P, T, n])
            dve.wait_ge(wl, 48)
            for k in range(1, UNIT):
                c.link(V.tensor_tensor(AGG[:, 0], AGG[:, 0], AGG[:, k], ALU.add))
            c.link(V.tensor_scalar(z[:], AGG[:, 0, :, G:G + GH], 1e-16, None, ALU.add))
            c.link(V.reciprocal(z[:], z[:]))
            c.link(V.tensor_tensor(a[:].rearrange("p t (h e) -> p t h e", h=GH),
                                   AGG[:, 0, :, 0:G].rearrange("p t (h e) -> p t h e", h=GH),
                                   z[:].unsqueeze(3).to_broadcast([P, T, GH, GE]), ALU.mult))
            c.link(V.tensor_tensor(a[:], a[:], bc(0), ALU.add))
            c.link(V.tensor_reduce(mean[:], a[:], AX.X, ALU.add))
            c.link(V.tensor_scalar(mean[:], mean[:], 1.0 / G, None, ALU.mult))
            c.link(V.tensor_tensor(a[:], a[:], wide(mean[:], G), ALU.subtract))
            c.link(V.tensor_tensor(sq[:], a[:], a[:], ALU.mult))
            c.link(V.tensor_reduce(var[:], sq[:], AX.X, ALU.add))
            c.link(V.tensor_scalar(var[:], var[:], 1.0 / G, LN_EPS, ALU.mult, ALU.add))
            dve.sem_inc(asked, 1)
            dve.wait_ge(raised, 1)
            c.link(V.tensor_tensor(a[:], a[:], wide(var[:], G), ALU.mult))
            c.link(V.tensor_tensor(a[:], a[:], bc(1), ALU.mult))
            c.link(V.tensor_tensor(a[:], a[:], bc(2), ALU.add))
            c.link(V.tensor_reduce(sc[:], a[:].rearrange("p t (h e) -> p t e h", h=GH), AX.X, ALU.add))
            c.link(V.tensor_scalar(sc[:], sc[:], 1.0 / GH, None, ALU.mult))
            c.link(V.memset(rank[:], 0.0))
            for i in range(GE):
                for j in range(GE):
                    if i != j:
                        c.link(V.tensor_tensor(cmp[:], sc[:, :, j], sc[:, :, i], ALU.is_ge if j < i else ALU.is_gt))
                        c.link(V.tensor_tensor(rank[:, :, i], rank[:, :, i], cmp[:], ALU.add))
            c.link(V.tensor_scalar(rank[:], rank[:], 2.0, None, ALU.is_lt))
            c.link(V.tensor_reduce(best[:], sc[:], AX.X, ALU.max))
            c.link(V.tensor_tensor(sc[:], sc[:], wide(best[:], GE), ALU.subtract))
            dve.sem_inc(ready, 1)
            dve.wait_ge(done, 1)
            c.link(V.tensor_tensor(ex[:], ex[:], rank[:], ALU.mult))
            c.link(V.tensor_reduce(best[:], ex[:], AX.X, ALU.add))
            c.link(V.reciprocal(best[:], best[:]))
            c.link(V.tensor_tensor(GATE[:, 0:T, :], ex[:], wide(best[:], GE), ALU.mult))


def experts(nc, name, X, X_out, count, hidden, layers, w_first, w_mid, w_last, bias, scale, func, GATE, router, consts):
    ident = consts["ident"]
    HC = hidden // P
    with ExitStack() as ctx:
        def sb(n, s, d=f32):
            return ctx.enter_context(nc.sbuf_tensor(f"{name}_{n}", s, d))

        def ps(n, s):
            return ctx.enter_context(nc.psum_tensor(f"{name}_{n}", s, f32))

        def sem(n):
            return ctx.enter_context(signal(nc, f"{name}_{n}"))

        x = sb("x", [P, 2, D])
        stats, mv, rstd = sb("stats", [P, 6]), sb("mv", [P, 2]), sb("rstd", [P, 1])
        xn = sb("xn", [P, 2, D])
        xT = sb("xT", [P, 2, 2, P])
        hT = [sb(f"hT{l}", [P, 2, HC, P]) for l in range(layers)]
        out = sb("out", [P, 2, D])
        gate = sb("gate", [P, 2, count])
        gmax, gsum = sb("gmax", [P, 1]), sb("gsum", [P, 1])
        XT = ps("XT", [P, 2, P])
        HP = [[ps(f"HP{l}{i}", [P, 512]) for i in range(2)] for l in range(layers)]
        YP = [ps(f"YP{i}", [P, 512]) for i in range(2)]
        RP = ps("RP", [P, 512])
        loaded = [sem("loaded0"), sem("loaded1")]
        stored = [sem("stored0"), sem("stored1")]
        normed, turned, turned_sb, ready, chain, free, taken = (
            sem(n) for n in ("normed", "turned", "turned_sb", "ready", "chain", "free", "taken"))
        hid = [sem(f"hid{l}") for l in range(layers)]
        hid_sb = [sem(f"hid_sb{l}") for l in range(layers)]
        summed, routed, logits, exped = sem("summed"), sem("routed"), sem("logits"), sem("exped")
        asked, raised, aside = sem("asked"), sem("raised"), sem("aside")
        block = ctx.enter_context(nc.Block())

        @block.gpsimd
        def _(pool):
            raise_to_minus_half(nc, pool, asked, raised, rstd[:], consts, 2 * PAIRS + 1)

        @block.sync
        def _(sp):
            def load(half, at):
                sp.dma_start(x[:, half, :], X[at, :]).then_inc(loaded[half], 16)

            sp.sem_inc(free, 2)
            load(0, slice(0, P))
            load(1, slice(P, 2 * P))
            with sp.Fori(0, PAIRS) as t:
                for half in range(2):
                    sp.wait_ge(ready, t * 2 + half + 1)
                    sp.dma_start(X_out[bass.ds((t * 2 + half) * P, P), :], out[:, half, :]).then_inc(stored[half], 16)
                    load(half, bass.ds((t * 2 + half + 2) * P, P))
                    sp.wait_ge(stored[half], t * 16 + 16)
                    sp.sem_inc(free, 1)
            for half in range(2):
                sp.wait_ge(loaded[half], 16 * (PAIRS + 1))

        gate_steps = 0 if GATE is not None else 4

        @block.vector
        def _(dve):
            c = Chain(dve, chain, per=2 * (4 + gate_steps + count))
            root = Root(dve, asked, raised, 2, aside)

            def norm(half, arrived):
                dve.wait_ge(loaded[half], arrived)
                layer_norm(nc, root, c.link, x[:, half, :], stats[:], mv[:], rstd, xn[:, half, :])
                dve.sem_inc(normed, 1)

            dve.sem_inc(taken, 2)
            norm(0, 16)
            with dve.Fori(0, PAIRS) as t:
                c.start(t)
                root.start(t)
                for half in range(2):
                    norm(1 - half, t * 16 + (16 if half == 0 else 32))
                    if GATE is None:
                        dve.wait_ge(routed, t * 2 + half + 1)
                        c.link(nc.vector.tensor_tensor(gate[:, half, :], RP[:, 0:count], router[1], ALU.add))
                        c.link(nc.vector.tensor_reduce(gmax[:], gate[:, half, :], AX.X, ALU.max, negate=True))
                        dve.sem_inc(logits, 1)
                        dve.wait_ge(exped, t * 2 + half + 1)
                        c.link(nc.vector.reciprocal(gsum[:], gsum[:]))
                        c.link(nc.vector.tensor_scalar(gate[:, half, :], gate[:, half, :], gsum[:], None, ALU.mult))
                    dve.wait_ge(free, t * 2 + half + 1)
                    for e in range(count):
                        dve.wait_ge(summed, t * (2 * count) + (half * count + e + 3))
                        g = gate[:, half, e:e + 1] if GATE is None else \
                            GATE[:, bass.ds(t * 2 + half, 1), e:e + 1].rearrange("p a b -> p (a b)")
                        c.link(nc.vector.scalar_tensor_tensor(
                            out[:, half, :], YP[e % 2][:, 0:D], g, x[:, half, :] if e == 0 else out[:, half, :],
                            ALU.mult, ALU.add))
                        dve.sem_inc(taken, 1)
                    dve.sem_inc(ready, 1)
                c.end()

        units = 2 * count

        @block.scalar
        def _(act):
            def turn_copy(half):
                nc.scalar.activation(xT[:, half], XT[:], ACT.Copy).then_inc(turned_sb, 1)

            def hide(l, e, slot):
                for j in range(HC):
                    last = nc.scalar.activation(hT[l][:, slot, j, :], HP[l][slot][:, j * P:(j + 1) * P], func,
                                                bias=bias[l][:, e, j:j + 1],
                                                scale=1.0 if scale is None else scale[l][:, e, j:j + 1])
                last.then_inc(hid_sb[l], 1)

            for l in range(layers):
                act.sem_inc(hid_sb[l], 1)
            act.wait_ge(turned, 1)
            turn_copy(0)
            for last in range(layers):
                for l in range(last + 1):
                    act.wait_ge(hid[l], last - l + 1)
                    hide(l, last - l, (last - l) % 2)
            with act.Fori(0, PAIRS) as t:
                for v in range(units):
                    if v % count == 1 and GATE is None:
                        half = v // count
                        act.wait_ge(logits, t * 2 + half + 1)
                        nc.scalar.activation(gate[:, half, :], gate[:, half, :], ACT.Exp, bias=gmax[:],
                                             accum_out=gsum[:]).then_inc(exped, 1)
                    if v % count == count - layers - 1:
                        act.wait_ge(turned, t * 2 + (v // count + 2))
                        turn_copy(1 - v // count)
                    for l in range(layers):
                        u = v + layers - l
                        act.wait_ge(hid[l], t * units + (u + 1))
                        if l == layers - 1:
                            act.wait_ge(summed, t * units + (u - 2 + 1 + 2))
                        else:
                            act.wait_ge(hid[l + 1], t * units + (u - 2 + 1))
                        hide(l, u % count, u % 2)

        @block.tensor
        def _(pe):
            def turn(half):
                for c in range(2):
                    last = nc.tensor.transpose(XT[:, c, :], xn[:, half, c * P:(c + 1) * P], ident[:, :])
                last.then_inc(turned, 1)

            def layer(l, e, slot, half):
                for j in range(HC):
                    to = HP[l][slot][:, j * P:(j + 1) * P]
                    for c in range(2 if l == 0 else HC):
                        w = (w_first if l == 0 else w_mid)[:, e, c, j * P:(j + 1) * P]
                        r = xT[:, half, c, :] if l == 0 else hT[l - 1][:, slot, c, :]
                        last = nc.tensor.matmul(to, w, r, start=(c == 0), stop=(c == (2 if l == 0 else HC) - 1),
                                                skip_group_check=True)
                last.then_inc(hid[l], 1)

            def route(half):
                for c in range(2):
                    last = nc.tensor.matmul(RP[:, 0:count], xT[:, half, c, :], router[0][:, c, :], start=(c == 0),
                                            stop=(c == 1), skip_group_check=True)
                last.then_inc(routed, 1)

            pe.sem_inc(summed, 2)
            pe.wait_ge(normed, 1)
            turn(0)
            pe.wait_ge(turned_sb, 1)
            for last in range(layers):
                for l in range(last + 1):
                    u = last - l
                    if l > 0:
                        pe.wait_ge(hid_sb[l - 1], u + 2)
                    layer(l, u, u % 2, 0)
            with pe.Fori(0, PAIRS) as t:
                for v in range(units):
                    half = v // count
                    if v % count == 0 and GATE is None:
                        route(half)
                    if v % count == count - layers - 1:
                        pe.wait_ge(normed, t * 2 + half + 2)
                        turn(1 - half)
                    if v % count == count - layers:
                        pe.wait_ge(turned_sb, t * 2 + half + 2)
                    for l in range(layers):
                        u = v + layers - l
                        pe.wait_ge(hid_sb[l], t * units + u)
                        if l > 0:
                            pe.wait_ge(hid_sb[l - 1], t * units + (u + 2))
                        layer(l, u % count, u % 2, (u // count) % 2)
                    pe.wait_ge(hid_sb[layers - 1], t * units + (v + 2))
                    pe.wait_ge(taken, t * units + (v + 1))
                    y = YP[v % 2][:, 0:D]
                    for c in range(HC):
                        nc.tensor.matmul(y, hT[layers - 1][:, v % 2, c, :], w_last[:, v % count, c, :],
                                         start=(c == 0), stop=False, skip_group_check=True)
                    nc.tensor.matmul(y, consts["ones"][0:1, :], bias[layers][0:1, v % count, :], start=False, stop=True,
                                     skip_group_check=True).then_inc(summed, 1)


def norm_table(nc, X, XN, consts):
    with ExitStack() as ctx:
        def sb(n, s, d=f32):
            return ctx.enter_context(nc.sbuf_tensor(f"nt_{n}", s, d))

        def sem(n):
            return ctx.enter_context(signal(nc, f"nt_{n}"))

        x, xn = sb("x", [P, 2, D]), sb("xn", [P, 2, D])
        stats, mv, rstd = sb("stats", [P, 6]), sb("mv", [P, 2]), sb("rstd", [P, 1])
        loaded = [sem("loaded0"), sem("loaded1")]
        stored = [sem("stored0"), sem("stored1")]
        normed, chain, free = sem("normed"), sem("chain"), sem("free")
        asked, raised, aside = sem("asked"), sem("raised"), sem("aside")
        block = ctx.enter_context(nc.Block())

        @block.gpsimd
        def _(pool):
            raise_to_minus_half(nc, pool, asked, raised, rstd[:], consts, 2 * PAIRS)

        @block.sync
        def _(sp):
            def load(half, at):
                sp.dma_start(x[:, half, :], X[at, :]).then_inc(loaded[half], 16)

            load(0, slice(0, P))
            load(1, slice(P, 2 * P))
            with sp.Fori(0, PAIRS) as t:
                for half in range(2):
                    sp.wait_ge(normed, t * 2 + half + 1)
                    load(half, bass.ds((t * 2 + half + 2) * P, P))
            for half in range(2):
                sp.wait_ge(loaded[half], 16 * (PAIRS + 1))

        @block.scalar
        def _(act):
            act.sem_inc(free, 2)
            with act.Fori(0, PAIRS) as t:
                for half in range(2):
                    act.wait_ge(normed, t * 2 + half + 1)
                    act.dma_start(XN[bass.ds((t * 2 + half) * P, P), :], xn[:, half, :]).then_inc(stored[half], 16)
                    act.wait_ge(stored[half], t * 16 + 16)
                    act.sem_inc(free, 1)

        @block.vector
        def _(dve):
            c = Chain(dve, chain, per=8)
            root = Root(dve, asked, raised, 2, aside)
            with dve.Fori(0, PAIRS) as t:
                c.start(t)
                root.start(t)
                for half in range(2):
                    dve.wait_ge(loaded[half], t * 16 + 16)
                    dve.wait_ge(free, t * 2 + half + 1)
                    layer_norm(nc, root, c.link, x[:, half, :], stats[:], mv[:], rstd, xn[:, half, :])
                    dve.sem_inc(normed, 1)
                c.end()


def isomorphism_layer(nc, X, AGG, X_out, W1, b1, W2, b2, eps, gamma, beta, consts):
    ident = consts["ident"]
    with ExitStack() as ctx:
        def sb(n, s, d=f32):
            return ctx.enter_context(nc.sbuf_tensor(f"gi_{n}", s, d))

        def ps(n, s):
            return ctx.enter_context(nc.psum_tensor(f"gi_{n}", s, f32))

        def sem(n):
            return ctx.enter_context(signal(nc, f"gi_{n}"))

        w1, w2 = sb("w1", [P, 2, D]), sb("w2", [P, 2, D])
        bias1 = sb("bias1", [P, 2])
        row = sb("row", [P, 3, D])
        keep = sb("keep", [P, 1])
        load_weights(nc, "gi", [
            (w1[:], W1.rearrange("(c p) d -> p c d", p=P)), (w2[:], W2.rearrange("(c p) d -> p c d", p=P)),
            (bias1[:], b1.rearrange("(c p) -> p c", p=P)), (row[:, 0, :], b2.partition_broadcast(P)),
            (row[:, 1, :], gamma.partition_broadcast(P)), (row[:, 2, :], beta.partition_broadcast(P)),
            (keep[:], eps.partition_broadcast(P))])
        x = sb("x", [P, 2, D])
        stats, mv, rstd = sb("stats", [P, 6]), sb("mv", [P, 2]), sb("rstd", [P, 1])
        xn, z = sb("xn", [P, 2, D]), sb("z", [P, 2, D])
        zT, hT = sb("zT", [P, 2, 2, P]), sb("hT", [P, 2, 2, P])
        r, out = sb("r", [P, D]), sb("out", [P, 2, D])
        ZT = [ps(f"ZT{i}", [P, 2, P]) for i in range(2)]
        HP = [ps(f"HP{i}", [P, 2, P]) for i in range(2)]
        YP = [ps(f"YP{i}", [P, 512]) for i in range(2)]
        loaded = [sem("loaded0"), sem("loaded1")]
        stored = [sem("stored0"), sem("stored1")]
        normed, turned, turned_sb, hid, hid_sb, projected, ready, chain, free = (
            sem(n) for n in ("normed", "turned", "turned_sb", "hid", "hid_sb", "projected", "ready", "chain", "free"))
        asked, raised, aside = sem("asked"), sem("raised"), sem("aside")
        block = ctx.enter_context(nc.Block())

        @block.gpsimd
        def _(pool):
            raise_to_minus_half(nc, pool, asked, raised, rstd[:], consts, 4 * PAIRS + 1)

        @block.sync
        def _(sp):
            def load(half, at):
                sp.dma_start(x[:, half, :], X[at, :]).then_inc(loaded[half], 16)

            sp.sem_inc(free, 2)
            load(0, slice(0, P))
            load(1, slice(P, 2 * P))
            with sp.Fori(0, PAIRS) as t:
                for half in range(2):
                    sp.wait_ge(ready, t * 2 + half + 3)
                    sp.dma_start(X_out[bass.ds((t * 2 + half) * P, P), :], out[:, half, :]).then_inc(stored[half], 16)
                    load(half, bass.ds((t * 2 + half + 2) * P, P))
                    sp.wait_ge(stored[half], t * 16 + 16)
                    sp.sem_inc(free, 1)
            for half in range(2):
                sp.wait_ge(loaded[half], 16 * (PAIRS + 1))

        @block.vector
        def _(dve):
            c = Chain(dve, chain, per=2 * (5 + 9))
            root = Root(dve, asked, raised, 4, aside)
            V = nc.vector
            c.link(V.tensor_scalar(keep[:], keep[:], 1.0, None, ALU.add))

            def front(half, at, arrived):
                dve.wait_ge(loaded[half], arrived)
                layer_norm(nc, root, c.link, x[:, half, :], stats[:], mv[:], rstd, xn[:, half, :])
                c.link(V.scalar_tensor_tensor(z[:, half, :], xn[:, half, :], keep[:],
                                              AGG[:, at, :].rearrange("p a d -> p (a d)"), ALU.mult, ALU.add))
                dve.sem_inc(normed, 1)

            dve.sem_inc(ready, 2)
            front(0, slice(0, 1), 16)
            with dve.Fori(0, PAIRS) as t:
                c.start(t)
                root.start(t)
                for half in range(2):
                    front(1 - half, bass.ds(t * 2 + half + 1, 1), t * 16 + (16 if half == 0 else 32))
                    dve.wait_ge(projected, t * 2 + half + 2)
                    dve.wait_ge(free, t * 2 + half + 1)
                    c.link(V.tensor_tensor(r[:], YP[half][:, 0:D], row[:, 0, :], ALU.add))
                    c.link(V.tensor_tensor(r[:], r[:], xn[:, half, :], ALU.add))
                    layer_norm(nc, root, c.link, r[:], stats[:], mv[:], rstd, r[:])
                    c.link(V.tensor_tensor(r[:], r[:], row[:, 1, :], ALU.mult))
                    c.link(V.tensor_tensor(r[:], r[:], row[:, 2, :], ALU.add))
                    c.link(V.scalar_tensor_tensor(out[:, half, :], r[:], 0.0, x[:, half, :], ALU.max, ALU.add))
                    dve.sem_inc(ready, 1)
                c.end()

        @block.scalar
        def _(act):
            def turn_copy(half):
                nc.scalar.activation(zT[:, half], ZT[half][:], ACT.Copy).then_inc(turned_sb, 1)

            act.wait_ge(turned, 1)
            turn_copy(0)
            with act.Fori(0, PAIRS) as t:
                for half in range(2):
                    act.wait_ge(hid, t * 2 + half + 1)
                    act.wait_ge(projected, t * 2 + half + 1)
                    for j in range(2):
                        last = nc.scalar.activation(hT[:, half, j, :], HP[half][:, j, :], ACT.Relu, bias=bias1[:, j:j + 1])
                    last.then_inc(hid_sb, 1)
                    act.wait_ge(turned, t * 2 + half + 2)
                    turn_copy(1 - half)

        @block.tensor
        def _(pe):
            def turn(half):
                for c in range(2):
                    last = nc.tensor.transpose(ZT[half][:, c, :], z[:, half, c * P:(c + 1) * P], ident[:, :])
                last.then_inc(turned, 1)

            pe.sem_inc(projected, 1)
            pe.wait_ge(normed, 1)
            turn(0)
            with pe.Fori(0, PAIRS) as t:
                for half in range(2):
                    pe.wait_ge(turned_sb, t * 2 + half + 1)
                    for j in range(2):
                        for c in range(2):
                            last = nc.tensor.matmul(HP[half][:, j, :], w1[:, c, j * P:(j + 1) * P], zT[:, half, c, :],
                                                    start=(c == 0), stop=(c == 1), skip_group_check=True)
                    last.then_inc(hid, 1)
                    pe.wait_ge(hid_sb, t * 2 + half + 1)
                    pe.wait_ge(ready, t * 2 + half + 1)
                    for c in range(2):
                        last = nc.tensor.matmul(YP[half][:, 0:D], hT[:, half, c, :], w2[:, c, :],
                                                start=(c == 0), stop=(c == 1), skip_group_check=True)
                    last.then_inc(projected, 1)
                    pe.wait_ge(normed, t * 2 + half + 2)
                    turn(1 - half)


def first_experts(nc, X, X_out, GATE, W1, b1, W2, b2, consts):
    hidden = W1.shape[2]
    HC = hidden // P
    with ExitStack() as ctx:
        def sb(n, s, d=f32):
            return ctx.enter_context(nc.sbuf_tensor(f"fe_{n}", s, d))

        w1, w2 = sb("w1", [P, GE, 2, hidden]), sb("w2", [P, GE, HC, D])
        bias1, bias2 = sb("bias1", [P, GE, HC]), sb("bias2", [1, GE, D])
        items = [(bias2[:].rearrange("p e d -> p (e d)"), b2.rearrange("e d -> (e d)").unsqueeze(0))]
        for e in range(GE):
            items += [(w1[:, e], W1[e].rearrange("(c p) h -> p c h", p=P)), (w2[:, e], W2[e].rearrange("(c p) d -> p c d", p=P)),
                      (bias1[:, e, :], b1[e].rearrange("(c p) -> p c", p=P))]
        load_weights(nc, "fe", items)
        experts(nc, "fx", X, X_out, GE, hidden, 1, w1, None, w2, [bias1, bias2], None, ACT.Gelu, GATE, None, consts)


def second_experts(nc, X, X_out, Wr, br, W1, b1, g1, be1, m1, v1, W2, b2, g2, be2, m2, v2, Wo, bo, consts):
    count = W1.shape[0]
    with ExitStack() as ctx:
        def sb(n, s, d=f32):
            return ctx.enter_context(nc.sbuf_tensor(f"se_{n}", s, d))

        w = [sb(f"w{i}", [P, count, 2, D]) for i in range(3)]
        wr, rb = sb("wr", [P, 2, count]), sb("rb", [P, count])
        raw = sb("raw", [P, 2, 5, count, 2])
        scale, bias = [sb(f"scale{i}", [P, count, 2]) for i in range(2)], [sb(f"bias{i}", [P, count, 2]) for i in range(2)]
        bias3 = sb("bias3", [1, count, D])
        items = [(wr[:], Wr.rearrange("(c p) e -> p c e", p=P)), (rb[:], br.partition_broadcast(P)),
                 (bias3[:].rearrange("p e d -> p (e d)"), bo.rearrange("e d -> (e d)").unsqueeze(0))]
        for i, one in enumerate((W1, W2, Wo)):
            for e in range(count):
                items.append((w[i][:, e], one[e].rearrange("(c p) d -> p c d", p=P)))
        for l, group in enumerate(((b1, g1, be1, m1, v1), (b2, g2, be2, m2, v2))):
            for j, one in enumerate(group):
                items.append((raw[:, l, j].rearrange("p e c -> p (e c)"), one.rearrange("e (c p) -> p (e c)", p=P)))
        load_weights(nc, "se", items)
        with (signal(nc, "se_chain") as chain, signal(nc, "se_asked") as asked, signal(nc, "se_raised") as raised,
              nc.Block() as block):
            @block.gpsimd
            def _(pool):
                pool.wait_ge(asked, 1)
                for l in range(2):
                    v = raw[:, l, 4].rearrange("p e c -> p (e c)")
                    nc.gpsimd.tensor_tensor(v, v, consts["minus_half"][:].to_broadcast([P, 2 * count]),
                                            ALU.pow).then_inc(raised, 1)

            @block.vector
            def _(dve):
                c = Chain(dve, chain)
                for l in range(2):
                    v = raw[:, l, 4]
                    c.link(nc.vector.tensor_scalar(v, v, BN_EPS, None, ALU.add))
                dve.sem_inc(asked, 1)
                dve.wait_ge(raised, 2)
                for l in range(2):
                    b, g, be, m, v = (raw[:, l, j] for j in range(5))
                    c.link(nc.vector.tensor_tensor(scale[l][:], v, g, ALU.mult))
                    c.link(nc.vector.tensor_tensor(b, b, m, ALU.subtract))
                    c.link(nc.vector.tensor_tensor(b, b, scale[l][:], ALU.mult))
                    c.link(nc.vector.tensor_tensor(bias[l][:], b, be, ALU.add))
        experts(nc, "sx", X, X_out, count, D, 2, w[0], w[1], w[2], [bias[0], bias[1], bias3], scale, ACT.Relu,
                None, (wr, rb[:]), consts)


def copy_out(nc, X, out):
    with signal(nc, "co_done") as done, nc.Block() as block:
        @block.sync
        def _(sp):
            sp.dma_start(out, X[0:N, :]).then_inc(done, 16)
            sp.wait_ge(done, 16)


def build(nc, ins, out):
    i = ins
    wide = lambda name, r, c, d=f32: nc.dram_tensor(name, [r, c], d, kind="Internal").ap()
    rec1, rec2 = wide("rec1", CHUNKS1 * P, 2, i32), wide("rec2", CHUNKS2 * P, 2, i32)
    X0, X1, X2, X3, X4 = (wide(f"X{n}", ROWS, D) for n in range(5))
    K, V, XN = wide("K", ROWS, D), wide("V", ROWS, D), wide("XN", ROWS, D)
    TAB = wide("TAB", ROWS, GH * GE + GH)
    G = GH * GE
    w1 = (CHUNKS1 + P - 1) // P * P
    w2 = (CHUNKS2 + P - 1) // P * P
    with ExitStack() as ctx:
        c = make_consts(nc, ctx)
        sort_edges(nc, "s1", COLS1, CHUNKS1, False, i["src"], i["dst"], rec1, c)
        copy_in(nc, i["x"], X0, (X1, X2, X3))
        with ExitStack() as layer:
            arr = chunk_arrays(nc, layer, "c1", CHUNKS1, rec1)
            wt = gnn_weights(nc, layer, *(i["L0_gnn_" + n] for n in
                                          ("Wq", "bq", "Wk", "bk", "Wv", "bv", "Wa", "ba", "rel_att", "rel_msg", "rel_pri", "skip")), c)
            S = layer.enter_context(nc.sbuf_tensor("S1", [P, HEADS, w1], f32))
            with nc.sbuf_tensor("Q", [P, TILES + 1, D], f32) as Q:
                project(nc, X0, Q, K, V, wt, c)
                clear(nc, "cs1", [S[:], Q[:, DUMP, :]])
                edge_scores(nc, "es1", D, HEADS, CHUNKS1, K[0:N, :], Q, arr, S, None, c)
            segment_softmax_numerators(nc, "sm1", HEADS, CHUNKS1, rec1, S, c)
            with nc.sbuf_tensor("AGG1", [P, TILES + 2, D + HEADS], f32) as AGG:
                edge_sums(nc, "ev1", D, HEADS, CHUNKS1, V[0:N, :], AGG, arr, S, c)
                attention_out(nc, X0, AGG, X1, wt, c)
        if STAGE == 1:
            return copy_out(nc, X1, out)
        sort_edges(nc, "s2", COLS2, CHUNKS2, True, i["L0_ffn_edge_index"][0], i["L0_ffn_edge_index"][1], rec2, c)
        with ExitStack() as layer:
            GATE = layer.enter_context(nc.sbuf_tensor("GATE", [P, TILES + 1, GE], f32))
            with ExitStack() as inner:
                arr = chunk_arrays(nc, inner, "c2", CHUNKS2, rec2)
                S = inner.enter_context(nc.sbuf_tensor("S2", [P, GH, w2], f32))
                ADST = inner.enter_context(nc.sbuf_tensor("ADST", [P, TILES + 1, GH], f32))
                feats = inner.enter_context(nc.sbuf_tensor("feats", [P, CHUNKS2 + UNIT, G], f32))
                gat_project(nc, X1, TAB, ADST, i["L0_ffn_W_gat"], i["L0_ffn_att_src"], i["L0_ffn_att_dst"], c)
                clear(nc, "cs2", [S[:], feats[:, CHUNKS2:CHUNKS2 + UNIT, :]])
                edge_scores(nc, "es2", G + GH, GH, CHUNKS2, TAB[0:N, :], ADST, arr, S, feats, c)
                leaky(nc, S, CHUNKS2)
                segment_softmax_numerators(nc, "sm2", GH, CHUNKS2, rec2, S, c)
                AGG = inner.enter_context(nc.sbuf_tensor("AGG2", [P, UNIT, TILES + 1, G + GH], f32))
                graph_sums(nc, CHUNKS2, AGG, arr, S, feats, c)
                gates(nc, AGG, GATE, i["L0_ffn_b_gat"], i["L0_ffn_ln_gamma"], i["L0_ffn_ln_beta"], c)
            first_experts(nc, X1, X2, GATE, *(i["L0_ffn_" + n] for n in ("W1", "b1", "W2", "b2")), c)
        if STAGE == 2:
            return copy_out(nc, X2, out)
        norm_table(nc, X2, XN, c)
        with ExitStack() as layer:
            arr = chunk_arrays(nc, layer, "c3", CHUNKS1, rec1)
            AGG = layer.enter_context(nc.sbuf_tensor("AGG3", [P, TILES + 2, D], f32))
            edge_sums(nc, "ev3", D, 0, CHUNKS1, XN[0:N, :], AGG, arr, None, c)
            isomorphism_layer(nc, X2, AGG, X3, *(i["L1_gnn_" + n] for n in ("W1", "b1", "W2", "b2", "eps", "gamma", "beta")), c)
        if STAGE == 3:
            return copy_out(nc, X3, out)
        second_experts(nc, X3, X4, *(i["L1_ffn_" + n] for n in
                                     ("Wr", "br", "W1", "b1", "g1", "be1", "m1", "v1", "W2", "b2", "g2", "be2", "m2", "v2", "Wo", "bo")), c)
        copy_out(nc, X4, out)


def clear(nc, name, tiles):
    with signal(nc, name) as done, nc.Block() as block:
        @block.vector
        def _(dve):
            for one in tiles:
                last = nc.vector.memset(one, 0.0)
            last.then_inc(done, 1)
            dve.wait_ge(done, 1)




_INS = ['x', 'src', 'dst', 'L0_gnn_Wk', 'L0_gnn_bk', 'L0_gnn_Wq', 'L0_gnn_bq', 'L0_gnn_Wv', 'L0_gnn_bv', 'L0_gnn_Wa', 'L0_gnn_ba', 'L0_gnn_rel_att', 'L0_gnn_rel_msg', 'L0_gnn_rel_pri', 'L0_gnn_skip', 'L0_ffn_W_gat', 'L0_ffn_att_src', 'L0_ffn_att_dst', 'L0_ffn_b_gat', 'L0_ffn_ln_gamma', 'L0_ffn_ln_beta', 'L0_ffn_W1', 'L0_ffn_b1', 'L0_ffn_W2', 'L0_ffn_b2', 'L0_ffn_edge_index', 'L1_gnn_W1', 'L1_gnn_b1', 'L1_gnn_W2', 'L1_gnn_b2', 'L1_gnn_eps', 'L1_gnn_gamma', 'L1_gnn_beta', 'L1_ffn_Wr', 'L1_ffn_br', 'L1_ffn_W1', 'L1_ffn_b1', 'L1_ffn_g1', 'L1_ffn_be1', 'L1_ffn_m1', 'L1_ffn_v1', 'L1_ffn_W2', 'L1_ffn_b2', 'L1_ffn_g2', 'L1_ffn_be2', 'L1_ffn_m2', 'L1_ffn_v2', 'L1_ffn_Wo', 'L1_ffn_bo']
_OUTS = [((6250, 256), 'float32')]


def kernel(**inputs):
    import numpy as _np
    import concourse.bacc as _bacc
    from concourse import mybir as _mybir
    from concourse.bass_utils import run_bass_kernel_spmd as _run

    nc = _bacc.Bacc("TRN2", target_bir_lowering=False, num_devices=1)
    arrays, args = {}, {}
    for name in _INS:
        a = _np.ascontiguousarray(inputs[name])
        if not a.ndim or a.shape == ():
            a = a.reshape(1)
        arrays[f"in_{name}_dram"] = a
        args[name] = nc.dram_tensor(f"in_{name}_dram", a.shape, _mybir.dt.from_np(a.dtype), kind="ExternalInput").ap()
    (shape, dtype), = _OUTS
    out = nc.dram_tensor("out_0_dram", shape, _mybir.dt.from_np(_np.dtype(dtype)), kind="ExternalOutput").ap()
    build(nc, args, out)
    r = _run(nc, [arrays], core_ids=[0])
    return r.results[0]["out_0_dram"]
```

```python
import concourse.bass as bass
from concourse import mybir
from contextlib import ExitStack, contextmanager

P = 128
N = 6250
TILES = (N + P - 1) // P
DUMP = TILES
KEYS = 64
WAY = 8
NO_NODE = 16384
BIG = 1.0e30

D = 256
HEADS = 8
DK = D // HEADS
GH = 4
GE = 4
LN_EPS = 1e-05
BN_EPS = 0.001
UNIT = 4
SLOTS = 4
PAIRS = (TILES + 1) // 2
ROWS = (2 * PAIRS + 4) * P
WAY_PAIR = 2 * WAY
COLS1 = (100000 // P + 1 + WAY_PAIR - 1) // WAY_PAIR * WAY_PAIR
COLS2 = (131072 // P + TILES + WAY_PAIR - 1) // WAY_PAIR * WAY_PAIR
CHUNKS1 = (100000 // P + 1 + TILES + SLOTS * UNIT - 1) // (SLOTS * UNIT) * (SLOTS * UNIT)
CHUNKS2 = (131072 // P + TILES + TILES + SLOTS * UNIT - 1) // (SLOTS * UNIT) * (SLOTS * UNIT)

f32 = mybir.dt.float32
bf16 = mybir.dt.bfloat16
i32 = mybir.dt.int32
u32 = mybir.dt.uint32
ALU = mybir.AluOpType
ACT = mybir.ActivationFunctionType
AX = mybir.AxisListType


@contextmanager
def signal(nc, name):
    sem = nc.alloc_semaphore(name)
    yield sem
    nc.gpsimd.sem_clear(sem)
    nc.release_semaphore(sem)


def pool_dma_signals(nc, name, count=2):
    return [nc.alloc_semaphore(f"{name}_pool_dma{i}") for i in range(count)]


def columns(ap, width):
    return ap.unsqueeze(2).to_broadcast([ap.shape[0], ap.shape[1], width])


def rows(ap, count):
    return ap.unsqueeze(1).to_broadcast([ap.shape[0], count, ap.shape[1]])


def sort_edges(nc, name, cols, chunks, loops, src, dst, sorted_rec, consts):
    edges = src.shape[0]
    full = edges // P
    rest = edges - full * P
    used = full + (1 if rest else 0)
    steps = cols // WAY
    LIM = chunks * P
    ident, identb, tri, ones, iota = consts["ident"], consts["identb"], consts["tri"], consts["ones"], consts["iotab"]
    with ExitStack() as ctx:
        def sb(n, s, d):
            return ctx.enter_context(nc.sbuf_tensor(f"{name}_{n}", s, d))

        def ps(n, s, d):
            return ctx.enter_context(nc.psum_tensor(f"{name}_{n}", s, d))

        def sem(n):
            return ctx.enter_context(signal(nc, f"{name}_{n}"))

        rec = sb("rec", [P, cols, 2], i32)
        raw = sb("raw", [P, 2, cols], i32)
        key_i = sb("key_i", [P, 2, cols], i32)
        key = sb("key", [P, 2, cols + WAY], bf16)
        fill = sb("fill", [P, chunks, 2], i32)
        OL = sb("OL", [P, 2, WAY, P], bf16)
        OH = sb("OH", [P, 2, WAY, KEYS], bf16)
        OLT = sb("OLT", [P, WAY, P], f32)
        OLTb = sb("OLTb", [P, WAY, P], bf16)
        same = sb("same", [P, WAY, P], bf16)
        table = sb("table", [P, WAY, KEYS], f32)
        base = sb("base", [P, WAY, KEYS], f32)
        tot = sb("tot", [P, KEYS], f32)
        size = sb("size", [P, KEYS], f32)
        size_i = sb("size_i", [P, KEYS], i32)
        nul = sb("nul", [P, KEYS], f32)
        start = sb("start", [P, KEYS], f32)
        picked = sb("picked", [P, WAY, KEYS], f32)
        pos = sb("pos", [P, WAY], f32)
        pos_i = sb("pos_i", [P, 3, WAY], i32)
        over = sb("over", [P, WAY], f32)
        slot = sb("slot", [P, WAY], f32)
        addr = sb("addr", [P, 2, WAY], i32)
        recs = sb("recs", [P, 2, WAY, 2], i32)
        zb = sb("zb", [P, WAY * KEYS], bf16)
        H = ps("H", [P, WAY * KEYS], f32)
        G = ps("G", [P, 2 * KEYS], f32)
        OT = ps("OT", [P, WAY, P], bf16)
        A = ps("A", [P, WAY, P], f32)
        T = ps("T", [P, WAY * KEYS], f32)
        W = ps("W", [P, WAY * KEYS], f32)

        loaded, keyed = sem("loaded"), sem("keyed")
        hot, counted, filled = sem("hot"), sem("counted"), sem("filled")
        chain = sem("chain")
        totals, summed, based = sem("totals"), sem("summed"), sem("based")
        r_hot, turned, turned_sb, alike, alike_sb = (sem(n) for n in ("r_hot", "turned", "turned_sb", "alike", "alike_sb"))
        table_sb, ranked, addressed = (sem(n) for n in ("table_sb", "ranked", "addressed"))
        scattered = pool_dma_signals(nc, name)
        issue, lchain, updated, idle, freed = (sem(n) for n in ("issue", "lchain", "updated", "idle", "freed"))

        block = ctx.enter_context(nc.Block())

        @block.sync
        def _(sp):
            sp.wait_ge(filled, 1)
            for which, part in ((0, src), (1, dst)):
                sp.dma_start(raw[:, which, 0:full], part[0:full * P].rearrange("(p c) -> p c", p=P)).then_inc(loaded, 16)
                if rest:
                    with nc.allow_non_contiguous_dma("the last few edges"):
                        sp.dma_start(raw[0:rest, which, full:full + 1],
                                     part[full * P:edges].rearrange("(p c) -> p c", c=1)).then_inc(loaded, 16)
            sp.wait_ge(loaded, 64 if rest else 32)

        @block.gpsimd
        def _(pool):
            nc.gpsimd.memset(raw[:, 0, full:cols], 0)
            nc.gpsimd.memset(raw[:, 1, full:cols], KEYS * P - 1)
            nc.gpsimd.memset(fill[:, :, 0], 0)
            last = nc.gpsimd.memset(fill[:, :, 1], NO_NODE)
            if loops:
                last.then_inc(issue, 1)
                pool.wait_ge(issue, 1)
                for which in range(2):
                    last = nc.gpsimd.iota(raw[:, which, used:used + TILES], [[P, TILES]], base=0, channel_multiplier=1)
            last.then_inc(filled, 1)
            bound = pool.to_reg(LIM - 1)
            pool.sem_inc(freed, 1)
            pool.wait_ge(filled, 1)
            pool.dma_start(sorted_rec.rearrange("(p c) w -> p (c w)", p=P),
                           fill[:].rearrange("p c w -> p (c w)")).then_inc(scattered[1], 16)
            pool.wait_ge(scattered[1], 16)
            with pool.Fori(0, steps // 2) as t:
                for half in range(2):
                    pool.wait_ge(addressed, t * 2 + (half + 1))
                    pool.sem_inc(idle, 1)
                    for k in range(WAY):
                        nc.gpsimd.indirect_dma_start(
                            sorted_rec, bass.IndirectOffsetOnAxis(ap=addr[:, half, k:k + 1].bitcast(u32), axis=0),
                            recs[:, half, k, :], None, bounds_check=bound, oob_is_err=False).then_inc(scattered[half], 16)
                    if half:
                        pool.wait_ge(scattered[0], t * (16 * WAY) + 16 * WAY)
                    else:
                        pool.wait_ge(scattered[1], t * (16 * WAY) + 16)
                    pool.sem_inc(freed, 1)
            pool.wait_ge(scattered[0], 16 * WAY * (steps // 2))
            pool.wait_ge(scattered[1], 16 * WAY * (steps // 2) + 16)

        @block.vector
        def _(dve):
            n = [0]

            def link(ins):
                n[0] += 1
                ins.then_inc(chain, 1)
                dve.wait_ge(chain, n[0])

            dve.wait_ge(loaded, 64 if rest else 32)
            link(nc.vector.memset(zb[:], 0.0))
            link(nc.vector.memset(nul[:], 0.0))
            nc.vector.tensor_scalar(rec[:, :, 0], raw[:, 0, :], N - 1, None, ALU.min)
            nc.vector.tensor_copy(rec[:, :, 1], raw[:, 1, :])
            nc.vector.tensor_scalar(key_i[:, 0, :], raw[:, 1, :], P - 1, None, ALU.bitwise_and)
            link(nc.vector.tensor_scalar(key_i[:, 1, :], raw[:, 1, :], 7, None, ALU.logical_shift_right))
            nc.vector.memset(key[:, :, cols:cols + WAY], 0.0)
            link(nc.vector.tensor_copy(key[:, :, 0:cols], key_i[:]))

            def one_hots(t, half, signal):
                c = bass.ds(t * 2 * WAY + half * WAY, WAY)
                nc.vector.tensor_tensor(OL[:, half], rows(iota[:, :], WAY), columns(key[:, 0, c], P), ALU.is_equal)
                nc.vector.tensor_tensor(OH[:, half], rows(iota[:, 0:KEYS], WAY), columns(key[:, 1, c], KEYS),
                                        ALU.is_equal).then_inc(signal, 1)

            dve.sem_inc(keyed, 1)
            with dve.Fori(0, steps // 2) as t:
                for half in range(2):
                    dve.wait_ge(counted, t * 2 + half + 1)
                    one_hots(t, half, hot)
            dve.wait_ge(counted, steps + 2)
            link(nc.vector.tensor_copy(base[:].rearrange("p k h -> p (k h)"), H[:]))
            link(nc.vector.tensor_reduce(tot[:], base[:].rearrange("p k h -> p h k"), AX.X, ALU.add))
            dve.sem_inc(totals, 1)
            dve.wait_ge(summed, 1)
            link(nc.vector.tensor_scalar(size_i[:], G[:, 0:KEYS], float(P - 1), None, ALU.add))
            link(nc.vector.tensor_scalar(size_i[:], size_i[:], 7, None, ALU.logical_shift_right))
            link(nc.vector.tensor_scalar(size[:], size_i[:], float(P), None, ALU.mult))
            link(nc.vector.tensor_tensor_scan(start[:], size[:], nul[:], 0.0, ALU.add, ALU.add))
            link(nc.vector.tensor_tensor(start[:], start[:], size[:], ALU.subtract))
            link(nc.vector.tensor_tensor(tot[:], start[:], G[:, KEYS:2 * KEYS], ALU.add))
            for k in range(WAY):
                link(nc.vector.tensor_copy(size[:], base[:, k, :]))
                link(nc.vector.tensor_copy(base[:, k, :], tot[:]))
                link(nc.vector.tensor_tensor(tot[:], tot[:], size[:], ALU.add))
            dve.sem_inc(based, 1)
            dve.sem_inc(lchain, 8)

            def hot_for_rank(half, at):
                nc.vector.tensor_tensor(OL[:, half], rows(iota[:, :], WAY), columns(key[:, 0, at], P), ALU.is_equal)
                nc.vector.tensor_tensor(OH[:, half], rows(iota[:, 0:KEYS], WAY), columns(key[:, 1, at], KEYS),
                                        ALU.is_equal).then_inc(r_hot, 1)

            def earlier_alike():
                nc.vector.tensor_tensor(same[:], A[:], rows(tri[:, :], WAY), ALU.mult).then_inc(alike_sb, 1)

            hot_for_rank(0, slice(0, WAY))
            dve.wait_ge(alike, 1)
            earlier_alike()
            with dve.Fori(0, steps // 2) as t:
                for half in range(2):
                    dve.wait_ge(updated, t * 2 + half + 1)
                    hot_for_rank(1 - half, bass.ds(t * 2 * WAY + (half + 1) * WAY, WAY))
                    dve.wait_ge(ranked, t * 2 + half + 1)
                    step = t * 16 + half * 8 + 8
                    nc.vector.tensor_tensor(picked[:].rearrange("p k h -> p (k h)"), W[:],
                                            OH[:, half].rearrange("p k h -> p (k h)"), ALU.mult).then_inc(lchain, 1)
                    dve.wait_ge(lchain, step + 1)
                    nc.vector.tensor_reduce(pos[:], picked[:], AX.X, ALU.add).then_inc(lchain, 1)
                    dve.wait_ge(alike, t * 2 + half + 2)
                    earlier_alike()
                    dve.wait_ge(lchain, step + 2)
                    nc.vector.tensor_copy(pos_i[:, 0, :], pos[:]).then_inc(lchain, 1)
                    nc.vector.tensor_scalar(over[:], pos[:], float(LIM), float(1 << 20), ALU.is_ge, ALU.mult).then_inc(lchain, 1)
                    dve.wait_ge(lchain, step + 4)
                    nc.vector.tensor_scalar(pos_i[:, 1, :], pos_i[:, 0, :], 7, None, ALU.logical_shift_right).then_inc(lchain, 1)
                    nc.vector.tensor_scalar(pos_i[:, 2, :], pos_i[:, 0, :], P - 1, None, ALU.bitwise_and).then_inc(lchain, 1)
                    dve.wait_ge(lchain, step + 6)
                    nc.vector.scalar_tensor_tensor(slot[:], pos_i[:, 2, :], float(chunks), pos_i[:, 1, :],
                                                   ALU.mult, ALU.add).then_inc(lchain, 1)
                    dve.wait_ge(freed, t * 2 + half + 1)
                    nc.vector.tensor_copy(recs[:, half], rec[:, bass.ds(t * 2 * WAY + half * WAY, WAY), :]).then_inc(lchain, 1)
                    dve.wait_ge(lchain, step + 8)
                    nc.vector.tensor_tensor(addr[:, half], slot[:], over[:], ALU.add).then_inc(addressed, 1)

        @block.scalar
        def _(act):
            def turn_copy():
                nc.scalar.activation(OLTb[:], OT[:], ACT.Copy).then_inc(turned_sb, 1)
                nc.scalar.activation(OLT[:], OT[:], ACT.Copy)

            def table_copy():
                nc.scalar.activation(table[:].rearrange("p k h -> p (k h)"), T[:], ACT.Copy).then_inc(table_sb, 1)

            act.wait_ge(turned, 1)
            turn_copy()
            act.wait_ge(updated, 1)
            table_copy()
            with act.Fori(0, steps) as t:
                act.wait_ge(turned, t + 2)
                turn_copy()
                act.wait_ge(updated, t + 2)
                table_copy()

        @block.tensor
        def _(pe):
            pe.wait_ge(keyed, 1)
            nc.tensor.matmul(H[:], zb[:, 0:P], zb[:], start=True, stop=True, skip_group_check=True).then_inc(counted, 2)
            with pe.Fori(0, steps // 2) as t:
                for half in range(2):
                    pe.wait_ge(hot, t * 2 + half + 1)
                    for k in range(WAY):
                        last = nc.tensor.matmul(H[:, k * KEYS:(k + 1) * KEYS], OL[:, half, k, :], OH[:, half, k, :],
                                                start=False, stop=True, skip_group_check=True)
                    last.then_inc(counted, 1)
            pe.wait_ge(totals, 1)
            nc.tensor.matmul(G[:, 0:KEYS], ones[:, :], tot[:], start=True, stop=True, skip_group_check=True)
            nc.tensor.matmul(G[:, KEYS:2 * KEYS], tri[:, :], tot[:], start=True, stop=True, skip_group_check=True).then_inc(summed, 1)
            pe.wait_ge(based, 1)
            nc.tensor.matmul(T[:], ident[:, :], base[:].rearrange("p k h -> p (k h)"), start=True, stop=True,
                             skip_group_check=True).then_inc(updated, 1)

            def turn(half):
                for k in range(WAY):
                    last = nc.tensor.transpose(OT[:, k, :], OL[:, half, k, :], identb[:, :])
                last.then_inc(turned, 1)

            def compare():
                for k in range(WAY):
                    last = nc.tensor.matmul(A[:, k, :], OLTb[:, k, :], OLTb[:, k, :], start=True, stop=True, skip_group_check=True)
                last.then_inc(alike, 1)

            pe.wait_ge(r_hot, 1)
            turn(0)
            pe.wait_ge(turned_sb, 1)
            compare()
            with pe.Fori(0, steps // 2) as t:
                for half in range(2):
                    pe.wait_ge(table_sb, t * 2 + half + 1)
                    pe.wait_ge(lchain, t * 16 + half * 8 + 1)
                    nc.tensor.matmul(W[:], zb[:, 0:P], zb[:], start=True, stop=True, skip_group_check=True)
                    for k in range(WAY):
                        nc.tensor.matmul(W[:, k * KEYS:(k + 1) * KEYS], OLT[:, k, :], table[:, k, :], start=False, stop=True,
                                         skip_group_check=True)
                    pe.wait_ge(alike_sb, t * 2 + half + 1)
                    for k in range(WAY):
                        last = nc.tensor.matmul(W[:, k * KEYS:(k + 1) * KEYS], same[:, k, :], OH[:, half, k, :], start=False, stop=True, skip_group_check=True)
                    last.then_inc(ranked, 1)
                    pe.wait_ge(r_hot, t * 2 + half + 2)
                    turn(1 - half)
                    for k in range(WAY):
                        last = nc.tensor.matmul(T[:, k * KEYS:(k + 1) * KEYS], OL[:, half, k, :], OH[:, half, k, :],
                                                start=False, stop=True, skip_group_check=True)
                    last.then_inc(updated, 1)
                    pe.wait_ge(turned_sb, t * 2 + half + 2)
                    compare()


def make_consts(nc, ctx):
    def sb(n, s, d):
        return ctx.enter_context(nc.sbuf_tensor(n, s, d))
    c = {"ident": sb("ident", [P, P], f32), "identb": sb("identb", [P, P], bf16), "tri": sb("tri", [P, P], f32),
         "ones": sb("ones", [P, P], f32), "iota": sb("iota", [P, P], f32), "iota_i": sb("iota_i", [P, P], i32),
         "iotab": sb("iotab", [P, P], bf16),
         "minus_half": sb("minus_half", [P, 1], f32)}
    with signal(nc, "const_step") as step, signal(nc, "const_done") as done, signal(nc, "const_float") as floated, nc.Block() as block:
        @block.gpsimd
        def _(pool):
            nc.gpsimd.memset(c["ident"][:], 0.0)
            nc.gpsimd.memset(c["identb"][:], 0.0)
            nc.gpsimd.memset(c["ones"][:], 1.0)
            nc.gpsimd.memset(c["minus_half"][:], -0.5)
            nc.gpsimd.iota(c["iota_i"][:], [[1, P]], base=0, channel_multiplier=0).then_inc(step, 1)
            pool.wait_ge(step, 1)
            for one in ("ident", "identb"):
                nc.gpsimd.affine_select(out=c[one][:], in_=c[one][:], pattern=[[-1, P]], compare_op=ALU.not_equal,
                                        fill=1.0, base=0, channel_multiplier=1)
            nc.gpsimd.affine_select(out=c["tri"][:], in_=c["ones"][:], pattern=[[1, P]], compare_op=ALU.is_gt,
                                    fill=0.0, base=0, channel_multiplier=-1).then_inc(done, 1)
            pool.wait_ge(done, 1)

        @block.vector
        def _(dve):
            dve.wait_ge(step, 1)
            nc.vector.tensor_copy(c["iotab"][:], c["iota_i"][:])
            nc.vector.tensor_copy(c["iota"][:], c["iota_i"][:]).then_inc(floated, 1)
            dve.wait_ge(floated, 1)
    return c




def chunk_arrays(nc, ctx, name, chunks, sorted_rec):
    wide = (chunks + P - 1) // P * P + 2 * UNIT
    arr = {
        "src": ctx.enter_context(nc.sbuf_tensor(f"{name}_src", [P, wide], i32)),
        "lo": ctx.enter_context(nc.sbuf_tensor(f"{name}_lo", [P, wide], f32)),
        "tile": ctx.enter_context(nc.sbuf_tensor(f"{name}_tile", [1, wide], i32)),
    }
    with (
        nc.sbuf_tensor(f"{name}_both", [P, chunks, 2], i32) as both,
        nc.sbuf_tensor(f"{name}_part", [P, 2, wide], i32) as part,
        nc.sbuf_tensor(f"{name}_none", [P, wide], f32) as none,
        signal(nc, f"{name}_in") as loaded,
        signal(nc, f"{name}_c") as chain,
        nc.Block() as block,
    ):
        @block.sync
        def _(sp):
            sp.dma_start(both[:].rearrange("p c w -> p (c w)"),
                         sorted_rec.rearrange("(p c) w -> p (c w)", p=P)).then_inc(loaded, 16)
            sp.wait_ge(loaded, 16)

        @block.vector
        def _(dve):
            n = [0]

            def link(ins):
                n[0] += 1
                ins.then_inc(chain, 1)
                dve.wait_ge(chain, n[0])

            nc.vector.memset(arr["src"][:], 0)
            nc.vector.memset(arr["tile"][:], DUMP)
            nc.vector.memset(none[:], 0.0)
            link(nc.vector.memset(part[:], NO_NODE))
            dve.wait_ge(loaded, 16)
            nc.vector.tensor_copy(arr["src"][:, 0:chunks], both[:, :, 0])
            link(nc.vector.tensor_copy(part[:, 1, 0:chunks], both[:, :, 1]))
            nc.vector.tensor_scalar(none[:], part[:, 1, :], float(NO_NODE), 1000.0, ALU.is_ge, ALU.mult)
            link(nc.vector.tensor_scalar(part[:, 0, :], part[:, 1, :], P - 1, None, ALU.bitwise_and))
            link(nc.vector.tensor_tensor(arr["lo"][:], part[:, 0, :], none[:], ALU.add))
            link(nc.vector.tensor_scalar(part[0:1, 0, :], part[0:1, 1, :], 7, None, ALU.logical_shift_right))
            link(nc.vector.tensor_scalar(arr["tile"][:], part[0:1, 0, :], DUMP, None, ALU.min))
    return arr


def segment_softmax_numerators(nc, name, heads, chunks, sorted_rec, S, consts):
    B = (chunks + P - 1) // P
    W = B * P
    ident = consts["ident"]
    with ExitStack() as ctx:
        def sb(n, s, d=f32):
            return ctx.enter_context(nc.sbuf_tensor(f"{name}_{n}", s, d))

        def sem(n):
            return ctx.enter_context(signal(nc, f"{name}_{n}"))

        Z = sb("Z", [P, heads, B, P])
        scan = sb("scan", [P, B, P])
        both = sb("both", [P, chunks, 2], i32)
        dst = sb("dst", [P, W])
        D = sb("D", [P, B, P])
        cut_f = sb("cut_f", [P, B, P])
        cut_b = sb("cut_b", [P, B, P])
        before = sb("before", [P, B, 2], i32)
        first = sb("first", [P, B])
        inner = sb("inner", [P, B])
        spread = sb("spread", [P, 3, B, heads])
        low = sb("low", [heads, 5, W])
        turn = [ctx.enter_context(nc.psum_tensor(f"{name}_turn{i}", [P, 4, P], f32)) for i in range(2)]
        lowp = [ctx.enter_context(nc.psum_tensor(f"{name}_low{i}", [P, 512], f32)) for i in range(3)]
        back = ctx.enter_context(nc.psum_tensor(f"{name}_back", [P, B, heads], f32))
        loaded, chain, ready, turned, used = (sem(n) for n in ("loaded", "chain", "ready", "turned", "used"))
        expd = sem("expd")

        jobs = [("dst", b) for b in range(B)] + [("S", h, b) for h in range(heads) for b in range(B)]
        outs = [(h, b) for h in range(heads) for b in range(B)]
        quads_in = [jobs[i:i + 4] for i in range(0, len(jobs), 4)]
        quads_out = [outs[i:i + 4] for i in range(0, len(outs), 4)]
        block = ctx.enter_context(nc.Block())

        @block.sync
        def _(sp):
            sp.dma_start(both[:].rearrange("p c w -> p (c w)"),
                         sorted_rec.rearrange("(p c) w -> p (c w)", p=P)).then_inc(loaded, 16)
            sp.wait_ge(ready, 1)
            whole = B - 1 if chunks % P else B
            last_slot = (P - 1) * chunks - 1
            with nc.allow_non_contiguous_dma("one word per chunk"):
                sp.dma_start(before[:, 0:whole, :],
                             sorted_rec[last_slot:last_slot + whole * P, :].rearrange("(b c) w -> c b w", c=P)
                             ).then_inc(loaded, 16)
                if chunks % P:
                    part = chunks - whole * P
                    sp.dma_start(before[0:part, whole:B, :],
                                 sorted_rec[last_slot + whole * P:last_slot + chunks, :].rearrange("(b c) w -> c b w", b=1)
                                 ).then_inc(loaded, 16)
            sp.wait_ge(loaded, 48 if chunks % P else 32)

        @block.vector
        def _(dve):
            n = [0]

            def link(ins):
                n[0] += 1
                ins.then_inc(chain, 1)
                dve.wait_ge(chain, n[0])

            link(nc.vector.memset(before[:], -1))
            dve.sem_inc(ready, 1)
            link(nc.vector.memset(dst[:], float(NO_NODE)))
            dve.wait_ge(loaded, 48 if chunks % P else 32)
            link(nc.vector.tensor_copy(dst[:, 0:chunks], both[:, :, 1]))
            dve.sem_inc(ready, 1)
            for i, quad in enumerate(quads_in):
                dve.wait_ge(turned, i + 1)
                for j, job in enumerate(quad):
                    to = D[:, job[1], :] if job[0] == "dst" else Z[:, job[1], job[2], :]
                    last = nc.vector.tensor_copy(to, turn[i % 2][:, j, :])
                last.then_inc(used, 1)
            dve.wait_ge(used, len(quads_in))
            link(nc.vector.tensor_copy(first[:], before[:, :, 1]))
            link(nc.vector.tensor_tensor(first[:], D[:, :, 0], first[:], ALU.not_equal))
            link(nc.vector.tensor_scalar(first[:], first[:], -BIG, None, ALU.mult))
            nc.vector.memset(cut_f[:, :, 0], -BIG)
            nc.vector.memset(cut_b[:, :, P - 1], -BIG)
            link(nc.vector.tensor_tensor(cut_f[:, :, 1:P], D[:, :, 1:P], D[:, :, 0:P - 1], ALU.not_equal))
            link(nc.vector.tensor_scalar(cut_f[:, :, 1:P], cut_f[:, :, 1:P], -BIG, None, ALU.mult))
            nc.vector.tensor_copy(cut_b[:, :, 0:P - 1], cut_f[:, :, 1:P])
            link(nc.vector.tensor_reduce(inner[:], cut_f[:, :, 1:P], AX.X, ALU.min))
            flat = lambda t: t.rearrange("p b e -> p (b e)")
            for h in range(heads):
                nc.vector.tensor_copy(spread[:, 1, :, h], first[:])
                nc.vector.tensor_copy(spread[:, 2, :, h], inner[:])
                link(nc.vector.tensor_tensor_scan(flat(scan[:]), flat(cut_f[:]), flat(Z[:, h]), -BIG, ALU.add, ALU.max))
                link(nc.vector.tensor_copy(spread[:, 0, :, h], scan[:, :, P - 1]))
            dve.sem_inc(ready, 1)

            def low_copy(which, count):
                at = 0
                for i in range(count):
                    width = min(512, W - at)
                    last = nc.vector.tensor_copy(low[:, which, at:at + width], lowp[i][0:heads, 0:width])
                    at += width
                link(last)

            NB = (W + 511) // 512
            for which in range(3):
                dve.wait_ge(turned, len(quads_in) + which + 1)
                low_copy(which, NB)
                dve.sem_inc(used, 1)
            link(nc.vector.tensor_tensor(low[:, 3, :], low[:, 1, :], low[:, 2, :], ALU.add))
            link(nc.vector.tensor_tensor_scan(low[:, 4, :], low[:, 3, :], low[:, 0, :], -BIG, ALU.add, ALU.max))
            link(nc.vector.memset(low[:, 3, 0:1], -BIG))
            link(nc.vector.tensor_tensor(low[:, 3, 1:W], low[:, 4, 0:W - 1], low[:, 1, 1:W], ALU.add))
            dve.sem_inc(ready, 1)
            dve.wait_ge(turned, len(quads_in) + 4)
            zfirst = Z[:, :, :, 0].rearrange("p h b -> p b h")
            link(nc.vector.tensor_tensor(zfirst, zfirst, back[:], ALU.max))
            for h in range(heads):
                link(nc.vector.tensor_tensor_scan(flat(Z[:, h]), flat(cut_f[:]), flat(Z[:, h]), -BIG, ALU.add, ALU.max))
            for h in range(heads):
                link(nc.vector.tensor_tensor_scan(flat(scan[:])[:, ::-1], flat(cut_b[:])[:, ::-1], flat(Z[:, h])[:, ::-1],
                                                  -BIG, ALU.add, ALU.max))
                link(nc.vector.tensor_copy(spread[:, 0, :, h], scan[:, :, 0]))
            dve.sem_inc(ready, 1)
            dve.wait_ge(turned, len(quads_in) + 5)
            low_copy(0, NB)
            link(nc.vector.memset(low[:, 3, W - 1:W], -BIG))
            link(nc.vector.tensor_tensor(low[:, 3, 0:W - 1], low[:, 1, 1:W], low[:, 2, 0:W - 1], ALU.add))
            link(nc.vector.tensor_tensor_scan(low[:, 4, ::-1], low[:, 3, ::-1], low[:, 0, ::-1], -BIG, ALU.add, ALU.max))
            link(nc.vector.tensor_tensor(low[:, 3, 0:W - 1], low[:, 4, 1:W], low[:, 1, 1:W], ALU.add))
            dve.sem_inc(ready, 1)
            dve.wait_ge(turned, len(quads_in) + 6)
            zlast = Z[:, :, :, P - 1].rearrange("p h b -> p b h")
            link(nc.vector.tensor_tensor(zlast, zlast, back[:], ALU.max))
            for h in range(heads):
                link(nc.vector.tensor_tensor_scan(flat(Z[:, h])[:, ::-1], flat(cut_b[:])[:, ::-1], flat(Z[:, h])[:, ::-1],
                                                  -BIG, ALU.add, ALU.max))
            dve.sem_inc(ready, 1)
            for i, quad in enumerate(quads_out):
                dve.wait_ge(turned, len(quads_in) + 6 + i + 1)
                for j, (h, b) in enumerate(quad):
                    s = S[:, h, b * P:(b + 1) * P]
                    last = nc.vector.tensor_tensor(s, s, turn[i % 2][:, j, :], ALU.subtract)
                last.then_inc(used, 1)

        @block.tensor
        def _(pe):
            pe.wait_ge(ready, 2)
            for i, quad in enumerate(quads_in):
                if i >= 2:
                    pe.wait_ge(used, i - 1)
                for j, job in enumerate(quad):
                    what = dst[:, job[1] * P:(job[1] + 1) * P] if job[0] == "dst" else S[:, job[1], job[2] * P:(job[2] + 1) * P]
                    last = nc.tensor.transpose(turn[i % 2][:, j, :], what, ident[:, :])
                last.then_inc(turned, 1)

            def per_chunk(which):
                for b in range(B):
                    last = nc.tensor.transpose(lowp[b // 4][0:heads, b % 4 * P:(b % 4 + 1) * P], spread[:, which, b, :], ident[:, :])
                last.then_inc(turned, 1)

            def per_chunk_back():
                for b in range(B):
                    last = nc.tensor.transpose(back[:, b, :], low[:, 3, b * P:(b + 1) * P], ident[0:heads, 0:heads])
                last.then_inc(turned, 1)

            pe.wait_ge(ready, 3)
            for which in range(3):
                if which:
                    pe.wait_ge(used, len(quads_in) + which)
                per_chunk(which)
            pe.wait_ge(ready, 4)
            per_chunk_back()
            pe.wait_ge(ready, 5)
            per_chunk(0)
            pe.wait_ge(ready, 6)
            per_chunk_back()
            pe.wait_ge(ready, 7)
            for i, quad in enumerate(quads_out):
                if i >= 2:
                    pe.wait_ge(used, len(quads_in) + 3 + i - 1)
                for j, (h, b) in enumerate(quad):
                    last = nc.tensor.transpose(turn[i % 2][:, j, :], Z[:, h, b, :], ident[:, :])
                last.then_inc(turned, 1)

        @block.scalar
        def _(act):
            act.wait_ge(used, len(quads_in) + 3 + len(quads_out))
            for h in range(heads):
                last = nc.scalar.activation(S[:, h, :], S[:, h, :], ACT.Exp)
            last.then_inc(expd, 1)
            act.wait_ge(expd, 1)


def load_tiles(engine, name, arr, at):
    regs = [engine.alloc_register(f"{name}_tile{k}") for k in range(UNIT)]
    engine.load(regs, arr["tile"][0:1, at])
    return [engine.snap(r, donate=True, min_val=0, max_val=DUMP) for r in regs]


def free_tiles(engine, tiles):
    for one in tiles:
        engine.free_register(one.val)


def gather_rows(nc, pool, table, got, idx, indexed, aside, gathered, steps, one_more=False):
    bound = pool.to_reg(table.shape[0] - 1)

    def step(slot):
        for k in range(UNIT):
            nc.gpsimd.indirect_dma_start(
                got[:, slot, k, :], None, table,
                bass.IndirectOffsetOnAxis(ap=idx[:, slot, k:k + 1].bitcast(u32), axis=0),
                bounds_check=bound, oob_is_err=False).then_inc(gathered[slot], 16)

    with pool.Fori(0, steps // SLOTS) as t:
        for slot in range(SLOTS):
            pool.wait_ge(indexed, t * SLOTS + (slot + 1))
            pool.sem_inc(aside, 1)
            step(slot)
    if one_more:
        pool.wait_ge(indexed, steps + 1)
        step(0)


def edge_scores(nc, name, width, heads, chunks, table, Q, arr, S, feats, consts):
    steps = chunks // UNIT
    ident, iota = consts["ident"], consts["iota"]
    qw = Q.shape[2]
    with ExitStack() as ctx:
        def sb(n, s, d=f32):
            return ctx.enter_context(nc.sbuf_tensor(f"{name}_{n}", s, d))

        def sem(n):
            return ctx.enter_context(signal(nc, f"{name}_{n}"))

        got = sb("got", [P, SLOTS, UNIT, width])
        idx = sb("idx", [P, SLOTS, UNIT], i32)
        OL = sb("OL", [P, 2, UNIT, P])
        OLT = sb("OLT", [P, 2, UNIT, P])
        prod = sb("prod", [P, UNIT * width])
        OT = [ctx.enter_context(nc.psum_tensor(f"{name}_OT{i}", [P, UNIT, P], f32)) for i in range(2)]
        QP = [ctx.enter_context(nc.psum_tensor(f"{name}_QP{i}", [P, UNIT, qw], f32)) for i in range(2)]
        indexed, hot, turned, turned_sb, queried, scored, multiplied, pool_aside, act_aside = (
            sem(n) for n in ("indexed", "hot", "turned", "turned_sb", "queried", "scored", "multiplied",
                             "pool_aside", "act_aside"))
        gathered = pool_dma_signals(nc, name, SLOTS)
        block = ctx.enter_context(nc.Block())

        @block.gpsimd
        def _(pool):
            gather_rows(nc, pool, table, got, idx, indexed, pool_aside, gathered, steps)

        @block.scalar
        def _(act):
            def indices(slot, at):
                nc.scalar.activation(idx[:, slot, :], arr["src"][:, at], ACT.Copy).then_inc(indexed, 1)

            def turn_copy(half):
                nc.scalar.activation(OLT[:, half], OT[half][:], ACT.Copy).then_inc(turned_sb, 1)

            indices(0, slice(0, UNIT))
            indices(1, slice(UNIT, 2 * UNIT))
            act.wait_ge(turned, 1)
            turn_copy(0)
            with act.Fori(0, steps // SLOTS) as t:
                for slot in range(SLOTS):
                    act.wait_ge(scored, t * SLOTS + (slot + 1))
                    act.sem_inc(act_aside, 1)
                    indices((slot + 2) % SLOTS, bass.ds(t * SLOTS * UNIT + (slot + 2) * UNIT, UNIT))
                    act.wait_ge(queried, t * SLOTS + (slot + 1))
                    act.wait_ge(turned, t * SLOTS + (slot + 2))
                    turn_copy((slot + 1) % 2)

        @block.vector
        def _(dve):
            def one_hots(half, at):
                nc.vector.tensor_tensor(OL[:, half], rows(iota[:, :], UNIT), columns(arr["lo"][:, at], P),
                                        ALU.is_equal).then_inc(hot, 1)

            dve.sem_inc(scored, 2)
            one_hots(0, slice(0, UNIT))
            with dve.Fori(0, steps // SLOTS) as t:
                for slot in range(SLOTS):
                    half = slot % 2
                    at = bass.ds(t * SLOTS * UNIT + slot * UNIT, UNIT)
                    one_hots(1 - half, bass.ds(t * SLOTS * UNIT + (slot + 1) * UNIT, UNIT))
                    dve.wait_ge(queried, t * SLOTS + (slot + 2))
                    dve.wait_ge(gathered[slot], t * (16 * UNIT) + 16 * UNIT)
                    if feats is None:
                        dve.wait_ge(scored, t * SLOTS + (slot + 2))
                        nc.vector.tensor_tensor(prod[:], got[:, slot].rearrange("p k d -> p (k d)"),
                                                QP[half][:].rearrange("p k d -> p (k d)"), ALU.mult).then_inc(multiplied, 1)
                        dve.wait_ge(multiplied, t * SLOTS + (slot + 1))
                        nc.vector.tensor_reduce(
                            S[:, :, at].rearrange("p h c -> p c h"),
                            prod[:].rearrange("p (k h d) -> p k h d", k=UNIT, h=heads), AX.X, ALU.add).then_inc(scored, 1)
                    else:
                        nc.vector.tensor_copy(feats[:, at, :], got[:, slot, :, 0:feats.shape[2]]).then_inc(multiplied, 1)
                        nc.vector.tensor_tensor(S[:, :, at].rearrange("p h c -> p c h"),
                                                got[:, slot, :, feats.shape[2]:feats.shape[2] + heads],
                                                QP[half][:], ALU.add).then_inc(scored, 1)
            dve.wait_ge(scored, steps + 2)

        @block.tensor
        def _(pe):
            def turn(half):
                for k in range(UNIT):
                    last = nc.tensor.transpose(OT[half][:, k, :], OL[:, half, k, :], ident[:, :])
                last.then_inc(turned, 1)

            pe.sem_inc(queried, 1)
            pe.wait_ge(hot, 1)
            turn(0)
            with pe.Fori(0, steps // SLOTS) as t:
                for slot in range(SLOTS):
                    half = slot % 2
                    tiles = load_tiles(pe, f"{name}_pe{slot}", arr, bass.ds(t * SLOTS * UNIT + slot * UNIT, UNIT))
                    pe.wait_ge(turned_sb, t * SLOTS + (slot + 1))
                    pe.wait_ge(scored, t * SLOTS + (slot + 1))
                    for k in range(UNIT):
                        last = nc.tensor.matmul(QP[half][:, k, :], OLT[:, half, k, :],
                                                Q[:, bass.ds(tiles[k], 1), :].rearrange("p a d -> p (a d)"),
                                                start=True, stop=True, skip_group_check=True)
                    last.then_inc(queried, 1)
                    free_tiles(pe, tiles)
                    pe.wait_ge(hot, t * SLOTS + (slot + 2))
                    turn(1 - half)


def edge_sums(nc, name, width, heads, chunks, table, AGG, arr, EX, consts):
    steps = chunks // UNIT
    iota = consts["iota"]
    total = AGG.shape[2]
    with ExitStack() as ctx:
        def sb(n, s, d=f32):
            return ctx.enter_context(nc.sbuf_tensor(f"{name}_{n}", s, d))

        def sem(n):
            return ctx.enter_context(signal(nc, f"{name}_{n}"))

        got = sb("got", [P, SLOTS, UNIT, width])
        W = sb("W", [P, 2, UNIT, total]) if EX is not None else None
        idx = sb("idx", [P, SLOTS, UNIT], i32)
        OL = sb("OL", [P, 2, UNIT, P])
        SP = [[ctx.enter_context(nc.psum_tensor(f"{name}_SP{i}{k}", [P, 512], f32)) for k in range(UNIT)] for i in range(2)]
        indexed, hot, weighted, summed, added, pool_aside, act_aside, cleared = (
            sem(n) for n in ("indexed", "hot", "weighted", "summed", "added", "pool_aside", "act_aside", "cleared"))
        gathered = pool_dma_signals(nc, name, SLOTS)
        CR = 2 * UNIT
        block = ctx.enter_context(nc.Block())

        @block.gpsimd
        def _(pool):
            nc.gpsimd.memset(AGG[:], 0.0).then_inc(cleared, 1)
            gather_rows(nc, pool, table, got, idx, indexed, pool_aside, gathered, steps, one_more=EX is not None)

        @block.scalar
        def _(act):
            def indices(slot, at):
                nc.scalar.activation(idx[:, slot, :], arr["src"][:, at], ACT.Copy).then_inc(indexed, 1)

            indices(0, slice(0, UNIT))
            indices(1, slice(UNIT, 2 * UNIT))
            with act.Fori(0, steps // SLOTS) as t:
                for slot in range(SLOTS):
                    act.wait_ge(weighted if EX is not None else summed,
                                t * (SLOTS * UNIT) + ((slot - 1) * UNIT + CR))
                    act.sem_inc(act_aside, 1)
                    indices((slot + 2) % SLOTS, bass.ds(t * SLOTS * UNIT + (slot + 2) * UNIT, UNIT))

        @block.vector
        def _(dve):
            def one_hots(half, at):
                nc.vector.tensor_tensor(OL[:, half], rows(iota[:, :], UNIT), columns(arr["lo"][:, at], P),
                                        ALU.is_equal).then_inc(hot, 1)

            def weigh(slot, k, c, at):
                per = (total - heads) // heads
                rows_in = got[:, slot, k, :]
                w = EX[:, :, at]
                nc.vector.tensor_tensor(
                    W[:, c, k, 0:total - heads].rearrange("p (h d) -> p h d", h=heads),
                    rows_in.rearrange("p (h d) -> p h d", h=heads), w.to_broadcast([P, heads, per]), ALU.mult)
                nc.vector.tensor_copy(W[:, c, k, total - heads:total], w.rearrange("p h c -> p (h c)")).then_inc(weighted, 1)

            dve.wait_ge(cleared, 1)
            dve.sem_inc(added, CR)
            one_hots(0, slice(0, UNIT))
            if EX is not None:
                dve.sem_inc(weighted, CR)
                dve.wait_ge(gathered[0], 16 * UNIT)
                for k in range(UNIT):
                    weigh(0, k, 0, slice(k, k + 1))
            with dve.Fori(0, steps // SLOTS) as t:
                for slot in range(SLOTS):
                    half = slot % 2
                    one_hots(1 - half, bass.ds(t * SLOTS * UNIT + (slot + 1) * UNIT, UNIT))
                    tiles = load_tiles(dve, f"{name}_dve{slot}", arr, bass.ds(t * SLOTS * UNIT + slot * UNIT, UNIT))
                    if EX is not None:
                        dve.wait_ge(gathered[(slot + 1) % SLOTS],
                                    t * (16 * UNIT) + (16 * UNIT if slot + 1 < SLOTS else 32 * UNIT))
                    for k in range(UNIT):
                        if EX is not None:
                            weigh((slot + 1) % SLOTS, k, 1 - half,
                                  bass.ds(t * SLOTS * UNIT + ((slot + 1) * UNIT + k), 1))
                        n = t * (SLOTS * UNIT) + (slot * UNIT + k)
                        dve.wait_ge(summed, n + (1 + CR))
                        dve.wait_ge(added, n + CR)
                        a = AGG[:, bass.ds(tiles[k], 1), :].rearrange("p a d -> p (a d)")
                        nc.vector.tensor_tensor(a, a, SP[half][k][:, 0:total], ALU.add).then_inc(added, 1)
                    free_tiles(dve, tiles)
            dve.wait_ge(added, steps * UNIT + CR)

        @block.tensor
        def _(pe):
            pe.sem_inc(summed, CR)
            with pe.Fori(0, steps // SLOTS) as t:
                for slot in range(SLOTS):
                    half = slot % 2
                    pe.wait_ge(hot, t * SLOTS + (slot + 1))
                    if EX is None:
                        pe.wait_ge(gathered[slot], t * (16 * UNIT) + 16 * UNIT)
                    for k in range(UNIT):
                        n = t * (SLOTS * UNIT) + (slot * UNIT + k)
                        if EX is not None:
                            pe.wait_ge(weighted, n + (1 + CR))
                        pe.wait_ge(added, n + 1)
                        nc.tensor.matmul(SP[half][k][:, 0:total], OL[:, half, k, :],
                                         W[:, half, k, :] if EX is not None else got[:, slot, k, :],
                                         start=True, stop=True, skip_group_check=True).then_inc(summed, 1)


def graph_sums(nc, chunks, AGG, arr, EX, feats, consts):
    steps = chunks // UNIT
    iota = consts["iota"]
    G = GH * GE
    with ExitStack() as ctx:
        def sb(n, s, d=f32):
            return ctx.enter_context(nc.sbuf_tensor(f"ev2_{n}", s, d))

        def sem(n):
            return ctx.enter_context(signal(nc, f"ev2_{n}"))

        W = sb("W", [P, 2, UNIT, G + GH])
        OL = sb("OL", [P, 2, UNIT, P])
        SP = [ctx.enter_context(nc.psum_tensor(f"ev2_SP{i}", [P, UNIT, G + GH], f32)) for i in range(2)]
        weighted, summed, added, chain = (sem(n) for n in ("weighted", "summed", "added", "chain"))
        block = ctx.enter_context(nc.Block())

        @block.vector
        def _(dve):
            def weigh(half, at):
                w = EX[:, :, at].rearrange("p h c -> p c h")
                nc.vector.tensor_tensor(OL[:, half], rows(iota[:, :], UNIT), columns(arr["lo"][:, at], P), ALU.is_equal)
                nc.vector.tensor_tensor(W[:, half, :, 0:G].rearrange("p k (h e) -> p k h e", h=GH),
                                        feats[:, at, :].rearrange("p k (h e) -> p k h e", h=GH),
                                        w.unsqueeze(3).to_broadcast([P, UNIT, GH, GE]), ALU.mult)
                nc.vector.tensor_copy(W[:, half, :, G:G + GH], w).then_inc(weighted, 1)

            nc.vector.memset(AGG[:], 0.0).then_inc(chain, 1)
            dve.wait_ge(chain, 1)
            dve.sem_inc(added, 1)
            weigh(0, slice(0, UNIT))
            with dve.Fori(0, steps // SLOTS) as t:
                for slot in range(SLOTS):
                    weigh(1 - slot % 2, bass.ds(t * SLOTS * UNIT + (slot + 1) * UNIT, UNIT))
                    tiles = load_tiles(dve, f"ev2_dve{slot}", arr, bass.ds(t * SLOTS * UNIT + slot * UNIT, UNIT))
                    dve.wait_ge(summed, t * SLOTS + (slot + 1))
                    dve.wait_ge(added, t * SLOTS + (slot + 1))
                    for k in range(UNIT):
                        a = AGG[:, k, bass.ds(tiles[k], 1), :].rearrange("p a d -> p (a d)")
                        last = nc.vector.tensor_tensor(a, a, SP[slot % 2][:, k, :], ALU.add)
                    last.then_inc(added, 1)
                    free_tiles(dve, tiles)
            dve.wait_ge(added, steps + 1)

        @block.tensor
        def _(pe):
            with pe.Fori(0, steps // SLOTS) as t:
                for slot in range(SLOTS):
                    pe.wait_ge(weighted, t * SLOTS + (slot + 1))
                    for k in range(UNIT):
                        last = nc.tensor.matmul(SP[slot % 2][:, k, :], OL[:, slot % 2, k, :], W[:, slot % 2, k, :],
                                                start=True, stop=True, skip_group_check=True)
                    last.then_inc(summed, 1)


def layer_norm(nc, root, link, x, stats, mean_var, rstd, out):
    link(nc.vector.bn_stats(stats, x))
    root.step_aside()
    link(nc.vector.bn_aggr(mean_var, stats))
    link(nc.vector.tensor_scalar(rstd[:], mean_var[:, 1:2], LN_EPS, None, ALU.add))
    root()
    link(nc.vector.tensor_scalar(out, x, mean_var[:, 0:1], rstd[:], ALU.subtract, ALU.mult))


def raise_to_minus_half(nc, pool, asked, raised, value, consts, times):
    with pool.Fori(0, times) as r:
        pool.wait_ge(asked, r + 1)
        nc.gpsimd.tensor_tensor(value, value, consts["minus_half"][:], ALU.pow).then_inc(raised, 1)


class Root:

    def __init__(self, engine, asked, raised, per, aside):
        self.aside = aside
        self.engine, self.asked, self.raised, self.per, self.n, self.base, self.t = engine, asked, raised, per, 0, 0, None

    def start(self, t):
        self.base, self.n, self.t = self.n, 0, t

    def step_aside(self):
        self.engine.sem_inc(self.aside, 1)

    def __call__(self):
        self.n += 1
        self.engine.sem_inc(self.asked, 1)
        self.engine.wait_ge(self.raised, self.n if self.t is None else self.t * self.per + (self.base + self.n))


class Chain:

    def __init__(self, engine, sem, per=0):
        self.engine, self.sem, self.per, self.n, self.base = engine, sem, per, 0, 0
        self.t = None

    def start(self, t):
        self.base, self.n, self.t = self.n, 0, t

    def link(self, ins):
        self.n += 1
        ins.then_inc(self.sem, 1)
        if self.t is None:
            self.engine.wait_ge(self.sem, self.n)
        else:
            self.engine.wait_ge(self.sem, self.t * self.per + (self.base + self.n))

    def end(self):
        assert self.n == self.per, (self.n, self.per)


def gnn_weights(nc, ctx, Wq, bq, Wk, bk, Wv, bv, Wa, ba, rel_att, rel_msg, rel_pri, skip, consts):
    wt = {}
    for n in ("q", "k", "v", "a"):
        wt[n] = ctx.enter_context(nc.sbuf_tensor(f"w_{n}", [P, 2, D], f32))
        wt["b" + n] = ctx.enter_context(nc.sbuf_tensor(f"b_{n}", [P, D], f32))
    wt["keep"] = ctx.enter_context(nc.sbuf_tensor("w_keep", [P, 2], f32))
    with ExitStack() as tmp:
        def sb(n, s, d=f32):
            return tmp.enter_context(nc.sbuf_tensor(f"gw_{n}", s, d))

        raw = {n: sb(f"raw_{n}", [P, 2, D]) for n in ("q", "k", "v", "a")}
        rel = {n: sb(f"rel_{n}", [P, 2, D]) for n in ("k", "v")}
        eye = sb("eye", [P, 2, D])
        pri = sb("pri", [P, HEADS])
        bias = {n: sb(f"bias_{n}", [P, 2]) for n in ("k", "v")}
        wide = {n: sb(f"wide_{n}", [P, 2, P]) for n in ("k", "v")}
        acc = {n: tmp.enter_context(nc.psum_tensor(f"gw_acc_{n}", [P, 2, D], f32)) for n in ("q", "k", "v", "a")}
        bacc = tmp.enter_context(nc.psum_tensor("gw_bacc", [P, 2, D], f32))
        zeroed, loaded, chain, made, folded, sig = (tmp.enter_context(signal(nc, f"gw_{n}")) for n in
                                                    ("zeroed", "loaded", "chain", "made", "folded", "sig"))
        block = tmp.enter_context(nc.Block())

        @block.gpsimd
        def _(pool):
            for n in ("k", "v"):
                last = nc.gpsimd.memset(rel[n][:], 0.0)
            last.then_inc(zeroed, 1)

        loads = 4 + 2 * HEADS + 1 + 2 + 2 + 1

        @block.sync
        def _(sp):
            for n, w in (("q", Wq), ("k", Wk), ("v", Wv), ("a", Wa)):
                sp.dma_start(raw[n][:], w.rearrange("(c p) d -> p c d", p=P)).then_inc(loaded, 16)
            sp.wait_ge(zeroed, 1)
            for n, r in (("k", rel_att), ("v", rel_msg)):
                for h in range(HEADS):
                    at = h * DK
                    sp.dma_start(rel[n][at % P:at % P + DK, at // P, at:at + DK], r[h]).then_inc(loaded, 16)
            sp.dma_start(pri[:], rel_pri.partition_broadcast(P)).then_inc(loaded, 16)
            for n, b in (("bq", bq), ("ba", ba)):
                sp.dma_start(wt[n][:], b.partition_broadcast(P)).then_inc(loaded, 16)
            with nc.allow_non_contiguous_dma("two short vectors"):
                for n, b in (("k", bk), ("v", bv)):
                    sp.dma_start(bias[n][:], b.rearrange("(c p) -> p c", p=P)).then_inc(loaded, 16)
                sp.dma_start(wt["keep"][:, 0:1], skip.partition_broadcast(P)).then_inc(loaded, 16)
            sp.wait_ge(loaded, 16 * loads)

        @block.scalar
        def _(act):
            act.wait_ge(loaded, 16 * loads)
            nc.scalar.activation(wt["keep"][:, 0:1], wt["keep"][:, 0:1], ACT.Sigmoid).then_inc(sig, 1)

        @block.vector
        def _(dve):
            c = Chain(dve, chain)
            c.link(nc.vector.memset(eye[:], 0.0))
            nc.vector.tensor_copy(eye[:, 0, 0:P], consts["ident"][:])
            c.link(nc.vector.tensor_copy(eye[:, 1, P:D], consts["ident"][:]))
            dve.wait_ge(loaded, 16 * loads)
            c.link(nc.vector.tensor_scalar(pri[:], pri[:], float(DK) ** -0.5, None, ALU.mult))
            for i in range(2):
                v = rel["k"][:, i, :].rearrange("p (h d) -> p h d", h=HEADS)
                c.link(nc.vector.tensor_tensor(v, v, columns(pri[:], DK), ALU.mult))
                for n in ("k", "v"):
                    c.link(nc.vector.tensor_copy(wide[n][:, i, :], bias[n][:, i:i + 1].to_broadcast([P, P])))
            dve.sem_inc(made, 1)
            dve.wait_ge(sig, 1)
            c.link(nc.vector.tensor_scalar(wt["keep"][:, 1:2], wt["keep"][:, 0:1], -1.0, 1.0, ALU.mult, ALU.add))
            dve.wait_ge(folded, 1)
            for n in ("q", "k", "v", "a"):
                nc.vector.tensor_copy(wt[n][:], acc[n][:])
            nc.vector.tensor_copy(wt["bk"][:], bacc[:, 0, :])
            c.link(nc.vector.tensor_copy(wt["bv"][:], bacc[:, 1, :]))

        @block.tensor
        def _(pe):
            pe.wait_ge(made, 1)
            for n, by in (("q", eye), ("k", rel["k"]), ("v", rel["v"]), ("a", eye)):
                for c in range(2):
                    for o in range(2):
                        nc.tensor.matmul(acc[n][:, c, :], raw[n][:, o, c * P:(c + 1) * P], by[:, o, :],
                                         start=(o == 0), stop=(o == 1), skip_group_check=True)
            for i, n in enumerate(("k", "v")):
                for o in range(2):
                    last = nc.tensor.matmul(bacc[:, i, :], wide[n][:, o, :], rel[n][:, o, :],
                                            start=(o == 0), stop=(o == 1), skip_group_check=True)
            last.then_inc(folded, 1)
    return wt


def copy_in(nc, x, X, later):
    spare = 2 * PAIRS * P
    with (
        nc.sbuf_tensor("ci_zero", [P, D], f32) as zero,
        signal(nc, "ci_zeroed") as zeroed,
        signal(nc, "ci_done") as done,
        nc.Block() as block,
    ):
        @block.vector
        def _(dve):
            nc.vector.memset(zero[:], 0.0).then_inc(zeroed, 1)

        @block.sync
        def _(sp):
            sp.dma_start(X[0:N, :], x).then_inc(done, 16)
            sp.wait_ge(zeroed, 1)
            first = TILES * P - N
            sp.dma_start(X[N:N + first, :], zero[0:first, :]).then_inc(done, 16)
            blank = [(X, i * P) for i in range(TILES, ROWS // P)] + [(one, r) for one in later for r in range(spare, ROWS, P)]
            for one, r in blank:
                sp.dma_start(one[r:r + P, :], zero[:]).then_inc(done, 16)
            sp.wait_ge(done, 16 * (2 + len(blank)))


def project(nc, X, Q, K, V, wt, consts):
    ident = consts["ident"]
    with ExitStack() as ctx:
        def sb(n, s, d=f32):
            return ctx.enter_context(nc.sbuf_tensor(f"pj_{n}", s, d))

        def ps(n, s):
            return ctx.enter_context(nc.psum_tensor(f"pj_{n}", s, f32))

        def sem(n):
            return ctx.enter_context(signal(nc, f"pj_{n}"))

        x = sb("x", [P, 2, D])
        stats, mv, rstd = sb("stats", [P, 6]), sb("mv", [P, 2]), sb("rstd", [P, 1])
        xn = sb("xn", [P, 2, D])
        xT = sb("xT", [P, 2, 2, P])
        kv = sb("kv", [P, 2, 2, D])
        XT = [ps(f"XT{i}", [P, 2, P]) for i in range(2)]
        QP = [ps(f"QP{i}", [P, 512]) for i in range(2)]
        KV = [ps(f"KV{i}", [P, 2, D]) for i in range(2)]
        loaded = [sem("loaded0"), sem("loaded1")]
        stored = [sem("stored0"), sem("stored1")]
        normed, turned, turned_sb, projected, ready, chain, free = (
            sem(n) for n in ("normed", "turned", "turned_sb", "projected", "ready", "chain", "free"))
        asked, raised, aside = sem("asked"), sem("raised"), sem("aside")
        block = ctx.enter_context(nc.Block())

        @block.gpsimd
        def _(pool):
            raise_to_minus_half(nc, pool, asked, raised, rstd[:], consts, 2 * PAIRS + 1)

        @block.sync
        def _(sp):
            def load(half, at):
                sp.dma_start(x[:, half, :], X[at, :]).then_inc(loaded[half], 16)

            sp.sem_inc(free, 2)
            load(0, slice(0, P))
            load(1, slice(P, 2 * P))
            with sp.Fori(0, PAIRS) as t:
                for half in range(2):
                    sp.wait_ge(normed, t * 2 + half + 1)
                    load(half, bass.ds((t * 2 + half + 2) * P, P))
                    sp.wait_ge(ready, t * 2 + half + 3)
                    at = bass.ds((t * 2 + half) * P, P)
                    sp.dma_start(K[at, :], kv[:, half, 0, :]).then_inc(stored[half], 16)
                    sp.dma_start(V[at, :], kv[:, half, 1, :]).then_inc(stored[half], 16)
                    sp.wait_ge(stored[half], t * 32 + 32)
                    sp.sem_inc(free, 1)
            for half in range(2):
                sp.wait_ge(loaded[half], 16 * (PAIRS + 1))

        @block.vector
        def _(dve):
            c = Chain(dve, chain, per=2 * 4)
            root = Root(dve, asked, raised, 2, aside)

            def norm(t, half, step):
                dve.wait_ge(loaded[half], t * 16 + (16 if step < 2 else 32))
                layer_norm(nc, root, c.link, x[:, half, :], stats[:], mv[:], rstd, xn[:, half, :])
                dve.sem_inc(normed, 1)

            dve.sem_inc(ready, 2)
            norm(0, 0, 0)
            with dve.Fori(0, PAIRS) as t:
                c.start(t)
                root.start(t)
                for half in range(2):
                    norm(t, 1 - half, 0 if half == 0 else 2)
                    dve.wait_ge(projected, t * 2 + half + 2)
                    dve.wait_ge(free, t * 2 + half + 1)
                    nc.vector.tensor_tensor(Q[:, bass.ds(t * 2 + half, 1), :].rearrange("p a d -> p (a d)"),
                                            QP[half][:, 0:D], wt["bq"][:], ALU.add)
                    nc.vector.tensor_tensor(kv[:, half, 0, :], KV[half][:, 0, :], wt["bk"][:], ALU.add)
                    nc.vector.tensor_tensor(kv[:, half, 1, :], KV[half][:, 1, :], wt["bv"][:], ALU.add).then_inc(ready, 1)
                c.end()

        @block.scalar
        def _(act):
            def turn_copy(half):
                nc.scalar.activation(xT[:, half], XT[half][:], ACT.Copy).then_inc(turned_sb, 1)

            act.wait_ge(turned, 1)
            turn_copy(0)
            with act.Fori(0, PAIRS) as t:
                for half in range(2):
                    act.wait_ge(projected, t * 2 + half + 1)
                    act.wait_ge(turned, t * 2 + half + 2)
                    turn_copy(1 - half)

        @block.tensor
        def _(pe):
            def turn(half):
                for c in range(2):
                    last = nc.tensor.transpose(XT[half][:, c, :], xn[:, half, c * P:(c + 1) * P], ident[:, :])
                last.then_inc(turned, 1)

            pe.wait_ge(normed, 1)
            turn(0)
            pe.sem_inc(projected, 1)
            with pe.Fori(0, PAIRS) as t:
                for half in range(2):
                    pe.wait_ge(turned_sb, t * 2 + half + 1)
                    pe.wait_ge(ready, t * 2 + half + 1)
                    for n, to in (("q", QP[half][:, 0:D]), ("k", KV[half][:, 0, :]), ("v", KV[half][:, 1, :])):
                        for c in range(2):
                            last = nc.tensor.matmul(to, xT[:, half, c, :], wt[n][:, c, :], start=(c == 0), stop=(c == 1),
                                                    skip_group_check=True)
                    last.then_inc(projected, 1)
                    pe.wait_ge(normed, t * 2 + half + 2)
                    turn(1 - half)


def attention_out(nc, X, AGG, X_out, wt, consts):
    ident = consts["ident"]
    with ExitStack() as ctx:
        def sb(n, s, d=f32):
            return ctx.enter_context(nc.sbuf_tensor(f"ao_{n}", s, d))

        def ps(n, s):
            return ctx.enter_context(nc.psum_tensor(f"ao_{n}", s, f32))

        def sem(n):
            return ctx.enter_context(signal(nc, f"ao_{n}"))

        x = sb("x", [P, 2, D])
        stats, mv, rstd = sb("stats", [P, 6]), sb("mv", [P, 2]), sb("rstd", [P, 1])
        z = sb("z", [P, AGG.shape[1], HEADS])
        xn, mean = sb("xn", [P, D]), sb("mean", [P, 2, D])
        mT = sb("mT", [P, 2, 2, P])
        u, rest, out = sb("u", [P, D]), sb("rest", [P, 2, D]), sb("out", [P, 2, D])
        MT = [ps(f"MT{i}", [P, 2, P]) for i in range(2)]
        YP = [ps(f"YP{i}", [P, 512]) for i in range(2)]
        loaded = [sem("loaded0"), sem("loaded1")]
        stored = [sem("stored0"), sem("stored1")]
        normed, turned, turned_sb, projected, ready, chain, free = (
            sem(n) for n in ("normed", "turned", "turned_sb", "projected", "ready", "chain", "free"))
        asked, raised, aside = sem("asked"), sem("raised"), sem("aside")
        block = ctx.enter_context(nc.Block())

        @block.gpsimd
        def _(pool):
            raise_to_minus_half(nc, pool, asked, raised, rstd[:], consts, 2 * PAIRS + 1)

        @block.sync
        def _(sp):
            def load(half, at):
                sp.dma_start(x[:, half, :], X[at, :]).then_inc(loaded[half], 16)

            sp.sem_inc(free, 2)
            load(0, slice(0, P))
            load(1, slice(P, 2 * P))
            with sp.Fori(0, PAIRS) as t:
                for half in range(2):
                    sp.wait_ge(normed, t * 2 + half + 1)
                    load(half, bass.ds((t * 2 + half + 2) * P, P))
                    sp.wait_ge(ready, t * 2 + half + 3)
                    sp.dma_start(X_out[bass.ds((t * 2 + half) * P, P), :], out[:, half, :]).then_inc(stored[half], 16)
                    sp.wait_ge(stored[half], t * 16 + 16)
                    sp.sem_inc(free, 1)
            for half in range(2):
                sp.wait_ge(loaded[half], 16 * (PAIRS + 1))

        @block.vector
        def _(dve):
            c = Chain(dve, chain, per=2 * (6 + 2))
            root = Root(dve, asked, raised, 2, aside)

            def front(half, at, arrived):
                dve.wait_ge(loaded[half], arrived)
                layer_norm(nc, root, c.link, x[:, half, :], stats[:], mv[:], rstd, xn[:])
                c.link(nc.vector.scalar_tensor_tensor(rest[:, half, :], xn[:], wt["keep"][:, 1:2], x[:, half, :],
                                                      ALU.mult, ALU.add))
                c.link(nc.vector.tensor_tensor(mean[:, half, :].rearrange("p (h d) -> p h d", h=HEADS),
                                               AGG[:, at, 0:D].rearrange("p a (h d) -> p (a h) d", h=HEADS),
                                               columns(z[:, at, :].rearrange("p a h -> p (a h)"), DK), ALU.mult))
                dve.sem_inc(normed, 1)

            c.link(nc.vector.tensor_scalar(z[:], AGG[:, :, D:D + HEADS], 1e-30, None, ALU.max))
            c.link(nc.vector.reciprocal(z[:], z[:]))
            dve.sem_inc(ready, 2)
            front(0, slice(0, 1), 16)
            with dve.Fori(0, PAIRS) as t:
                c.start(t)
                root.start(t)
                for half in range(2):
                    front(1 - half, bass.ds(t * 2 + half + 1, 1), t * 16 + (16 if half == 0 else 32))
                    dve.wait_ge(projected, t * 2 + half + 2)
                    dve.wait_ge(free, t * 2 + half + 1)
                    c.link(nc.vector.tensor_tensor(u[:], YP[half][:, 0:D], wt["ba"][:], ALU.add))
                    c.link(nc.vector.scalar_tensor_tensor(out[:, half, :], u[:], wt["keep"][:, 0:1], rest[:, half, :],
                                                          ALU.mult, ALU.add))
                    dve.sem_inc(ready, 1)
                c.end()

        @block.scalar
        def _(act):
            def turn_copy(half):
                nc.scalar.activation(mT[:, half], MT[half][:], ACT.Copy).then_inc(turned_sb, 1)

            act.wait_ge(turned, 1)
            turn_copy(0)
            with act.Fori(0, PAIRS) as t:
                for half in range(2):
                    act.wait_ge(projected, t * 2 + half + 1)
                    act.wait_ge(turned, t * 2 + half + 2)
                    turn_copy(1 - half)

        @block.tensor
        def _(pe):
            def turn(half):
                for c in range(2):
                    last = nc.tensor.transpose(MT[half][:, c, :], mean[:, half, c * P:(c + 1) * P], ident[:, :])
                last.then_inc(turned, 1)

            pe.sem_inc(projected, 1)
            pe.wait_ge(normed, 1)
            turn(0)
            with pe.Fori(0, PAIRS) as t:
                for half in range(2):
                    pe.wait_ge(turned_sb, t * 2 + half + 1)
                    pe.wait_ge(ready, t * 2 + half + 1)
                    for c in range(2):
                        last = nc.tensor.matmul(YP[half][:, 0:D], mT[:, half, c, :], wt["a"][:, c, :],
                                                start=(c == 0), stop=(c == 1), skip_group_check=True)
                    last.then_inc(projected, 1)
                    pe.wait_ge(normed, t * 2 + half + 2)
                    turn(1 - half)


def load_weights(nc, name, items):
    with signal(nc, f"{name}_loaded") as loaded, nc.Block() as block:
        @block.sync
        def _(sp):
            with nc.allow_non_contiguous_dma("short vectors"):
                for to, part in items:
                    sp.dma_start(to, part).then_inc(loaded, 16)
            sp.wait_ge(loaded, 16 * len(items))


def gat_project(nc, X, TAB, ADST, W_gat, att_src, att_dst, consts):
    ident = consts["ident"]
    G = GH * GE
    with ExitStack() as ctx:
        def sb(n, s, d=f32):
            return ctx.enter_context(nc.sbuf_tensor(f"gp_{n}", s, d))

        def ps(n, s):
            return ctx.enter_context(nc.psum_tensor(f"gp_{n}", s, f32))

        def sem(n):
            return ctx.enter_context(signal(nc, f"gp_{n}"))

        w = sb("w", [P, 2, G])
        att = sb("att", [P, 2, G])
        w24 = sb("w24", [P, 2, G + 2 * GH])
        tmp = sb("tmp", [P, G])
        x = sb("x", [P, 2, D])
        stats, mv, rstd = sb("stats", [P, 6]), sb("mv", [P, 2]), sb("rstd", [P, 1])
        xn = sb("xn", [P, 2, D])
        xT = sb("xT", [P, 2, 2, P])
        row = sb("row", [P, 2, G + GH])
        XT = [ps(f"XT{i}", [P, 2, P]) for i in range(2)]
        YP = [ps(f"YP{i}", [P, 512]) for i in range(2)]
        loaded = [sem("loaded0"), sem("loaded1")]
        stored = [sem("stored0"), sem("stored1")]
        normed, turned, turned_sb, projected, ready, chain, free, wl = (
            sem(n) for n in ("normed", "turned", "turned_sb", "projected", "ready", "chain", "free", "wl"))
        asked, raised, aside = sem("asked"), sem("raised"), sem("aside")
        block = ctx.enter_context(nc.Block())

        @block.gpsimd
        def _(pool):
            raise_to_minus_half(nc, pool, asked, raised, rstd[:], consts, 2 * PAIRS + 1)

        @block.sync
        def _(sp):
            def load(half, at):
                sp.dma_start(x[:, half, :], X[at, :]).then_inc(loaded[half], 16)

            sp.dma_start(w[:], W_gat.rearrange("(c p) g -> p c g", p=P)).then_inc(wl, 16)
            sp.dma_start(att[:, 0, :], att_src.rearrange("h e -> (h e)").partition_broadcast(P)).then_inc(wl, 16)
            sp.dma_start(att[:, 1, :], att_dst.rearrange("h e -> (h e)").partition_broadcast(P)).then_inc(wl, 16)
            sp.sem_inc(free, 2)
            load(0, slice(0, P))
            load(1, slice(P, 2 * P))
            with sp.Fori(0, PAIRS) as t:
                for half in range(2):
                    sp.wait_ge(normed, t * 2 + half + 1)
                    load(half, bass.ds((t * 2 + half + 2) * P, P))
                    sp.wait_ge(ready, t * 2 + half + 3)
                    sp.dma_start(TAB[bass.ds((t * 2 + half) * P, P), :], row[:, half, :]).then_inc(stored[half], 16)
                    sp.wait_ge(stored[half], t * 16 + 16)
                    sp.sem_inc(free, 1)
            for half in range(2):
                sp.wait_ge(loaded[half], 16 * (PAIRS + 1))

        @block.vector
        def _(dve):
            c = Chain(dve, chain, per=8)
            root = Root(dve, asked, raised, 2, aside)
            dve.wait_ge(wl, 48)
            for i in range(2):
                nc.vector.tensor_copy(w24[:, i, 0:G], w[:, i, :])
                for j in range(2):
                    c.link(nc.vector.tensor_tensor(tmp[:], w[:, i, :], att[:, j, :], ALU.mult))
                    c.link(nc.vector.tensor_reduce(w24[:, i, G + j * GH:G + (j + 1) * GH],
                                                   tmp[:].rearrange("p (h e) -> p h e", h=GH), AX.X, ALU.add))

            def norm(half, arrived):
                dve.wait_ge(loaded[half], arrived)
                layer_norm(nc, root, c.link, x[:, half, :], stats[:], mv[:], rstd, xn[:, half, :])
                dve.sem_inc(normed, 1)

            dve.sem_inc(ready, 2)
            norm(0, 16)
            with dve.Fori(0, PAIRS) as t:
                c.start(t)
                root.start(t)
                for half in range(2):
                    norm(1 - half, t * 16 + (16 if half == 0 else 32))
                    dve.wait_ge(projected, t * 2 + half + 2)
                    dve.wait_ge(free, t * 2 + half + 1)
                    nc.vector.tensor_copy(row[:, half, :], YP[half][:, 0:G + GH])
                    nc.vector.tensor_scalar(ADST[:, bass.ds(t * 2 + half, 1), :].rearrange("p a d -> p (a d)"),
                                            YP[half][:, G + GH:G + 2 * GH], 1.0, None, ALU.mult).then_inc(ready, 1)
                c.end()

        @block.scalar
        def _(act):
            def turn_copy(half):
                nc.scalar.activation(xT[:, half], XT[half][:], ACT.Copy).then_inc(turned_sb, 1)

            act.wait_ge(turned, 1)
            turn_copy(0)
            with act.Fori(0, PAIRS) as t:
                for half in range(2):
                    act.wait_ge(projected, t * 2 + half + 1)
                    act.wait_ge(turned, t * 2 + half + 2)
                    turn_copy(1 - half)

        @block.tensor
        def _(pe):
            def turn(half):
                for c in range(2):
                    last = nc.tensor.transpose(XT[half][:, c, :], xn[:, half, c * P:(c + 1) * P], ident[:, :])
                last.then_inc(turned, 1)

            pe.sem_inc(projected, 1)
            pe.wait_ge(normed, 1)
            turn(0)
            with pe.Fori(0, PAIRS) as t:
                for half in range(2):
                    pe.wait_ge(turned_sb, t * 2 + half + 1)
                    pe.wait_ge(ready, t * 2 + half + 1)
                    for c in range(2):
                        last = nc.tensor.matmul(YP[half][:, 0:G + 2 * GH], xT[:, half, c, :], w24[:, c, :],
                                                start=(c == 0), stop=(c == 1), skip_group_check=True)
                    last.then_inc(projected, 1)
                    pe.wait_ge(normed, t * 2 + half + 2)
                    turn(1 - half)


def leaky(nc, S, chunks):
    with nc.sbuf_tensor("lk_low", [P, S.shape[2]], f32) as low, signal(nc, "lk_chain") as chain, nc.Block() as block:
        @block.vector
        def _(dve):
            c = Chain(dve, chain)
            for h in range(S.shape[1]):
                c.link(nc.vector.tensor_scalar(low[:], S[:, h, :], 0.2, None, ALU.mult))
                c.link(nc.vector.tensor_tensor(S[:, h, :], S[:, h, :], low[:], ALU.max))


def gates(nc, AGG, GATE, b_gat, gamma, beta, consts):
    G = GH * GE
    T = AGG.shape[2]
    with ExitStack() as ctx:
        def sb(n, s, d=f32):
            return ctx.enter_context(nc.sbuf_tensor(f"gt_{n}", s, d))

        par = sb("par", [P, 3, G])
        a = sb("a", [P, T, G])
        sq = sb("sq", [P, T, G])
        z = sb("z", [P, T, GH])
        mean, var = sb("mean", [P, T]), sb("var", [P, T])
        sc, ex, rank, cmp, best = sb("sc", [P, T, GE]), sb("ex", [P, T, GE]), sb("rank", [P, T, GE]), sb("cmp", [P, T]), sb("best", [P, T])
        wl, chain, ready, done, asked, raised = (
            ctx.enter_context(signal(nc, f"gt_{n}")) for n in ("wl", "chain", "ready", "done", "asked", "raised"))
        block = ctx.enter_context(nc.Block())

        @block.gpsimd
        def _(pool):
            pool.wait_ge(asked, 1)
            nc.gpsimd.tensor_tensor(var[:], var[:], consts["minus_half"][:].to_broadcast([P, T]), ALU.pow).then_inc(raised, 1)

        @block.sync
        def _(sp):
            for i, v in enumerate((b_gat, gamma, beta)):
                sp.dma_start(par[:, i, :], v.partition_broadcast(P)).then_inc(wl, 16)
            sp.wait_ge(wl, 48)

        @block.scalar
        def _(act):
            act.wait_ge(ready, 1)
            nc.scalar.activation(ex[:], sc[:], ACT.Exp).then_inc(done, 1)

        @block.vector
        def _(dve):
            c = Chain(dve, chain)
            V = nc.vector
            bc = lambda i: par[:, i, :].unsqueeze(1).to_broadcast([P, T, G])
            wide = lambda v, n: v.unsqueeze(2).to_broadcast([P, T, n])
            dve.wait_ge(wl, 48)
            for k in range(1, UNIT):
                c.link(V.tensor_tensor(AGG[:, 0], AGG[:, 0], AGG[:, k], ALU.add))
            c.link(V.tensor_scalar(z[:], AGG[:, 0, :, G:G + GH], 1e-16, None, ALU.add))
            c.link(V.reciprocal(z[:], z[:]))
            c.link(V.tensor_tensor(a[:].rearrange("p t (h e) -> p t h e", h=GH),
                                   AGG[:, 0, :, 0:G].rearrange("p t (h e) -> p t h e", h=GH),
                                   z[:].unsqueeze(3).to_broadcast([P, T, GH, GE]), ALU.mult))
            c.link(V.tensor_tensor(a[:], a[:], bc(0), ALU.add))
            c.link(V.tensor_reduce(mean[:], a[:], AX.X, ALU.add))
            c.link(V.tensor_scalar(mean[:], mean[:], 1.0 / G, None, ALU.mult))
            c.link(V.tensor_tensor(a[:], a[:], wide(mean[:], G), ALU.subtract))
            c.link(V.tensor_tensor(sq[:], a[:], a[:], ALU.mult))
            c.link(V.tensor_reduce(var[:], sq[:], AX.X, ALU.add))
            c.link(V.tensor_scalar(var[:], var[:], 1.0 / G, LN_EPS, ALU.mult, ALU.add))
            dve.sem_inc(asked, 1)
            dve.wait_ge(raised, 1)
            c.link(V.tensor_tensor(a[:], a[:], wide(var[:], G), ALU.mult))
            c.link(V.tensor_tensor(a[:], a[:], bc(1), ALU.mult))
            c.link(V.tensor_tensor(a[:], a[:], bc(2), ALU.add))
            c.link(V.tensor_reduce(sc[:], a[:].rearrange("p t (h e) -> p t e h", h=GH), AX.X, ALU.add))
            c.link(V.tensor_scalar(sc[:], sc[:], 1.0 / GH, None, ALU.mult))
            c.link(V.memset(rank[:], 0.0))
            for i in range(GE):
                for j in range(GE):
                    if i != j:
                        c.link(V.tensor_tensor(cmp[:], sc[:, :, j], sc[:, :, i], ALU.is_ge if j < i else ALU.is_gt))
                        c.link(V.tensor_tensor(rank[:, :, i], rank[:, :, i], cmp[:], ALU.add))
            c.link(V.tensor_scalar(rank[:], rank[:], 2.0, None, ALU.is_lt))
            c.link(V.tensor_reduce(best[:], sc[:], AX.X, ALU.max))
            c.link(V.tensor_tensor(sc[:], sc[:], wide(best[:], GE), ALU.subtract))
            dve.sem_inc(ready, 1)
            dve.wait_ge(done, 1)
            c.link(V.tensor_tensor(ex[:], ex[:], rank[:], ALU.mult))
            c.link(V.tensor_reduce(best[:], ex[:], AX.X, ALU.add))
            c.link(V.reciprocal(best[:], best[:]))
            c.link(V.tensor_tensor(GATE[:, 0:T, :], ex[:], wide(best[:], GE), ALU.mult))


def experts(nc, name, X, X_out, XN, count, hidden, layers, w_first, w_mid, w_last, bias, scale, func, GATE, router,
            before, consts):
    ident = consts["ident"]
    HC = hidden // P
    with ExitStack() as ctx:
        def sb(n, s, d=f32):
            return ctx.enter_context(nc.sbuf_tensor(f"{name}_{n}", s, d))

        def ps(n, s):
            return ctx.enter_context(nc.psum_tensor(f"{name}_{n}", s, f32))

        def sem(n):
            return ctx.enter_context(signal(nc, f"{name}_{n}"))

        x = sb("x", [P, 2, D])
        stats, mv, rstd = sb("stats", [P, 6]), sb("mv", [P, 2]), sb("rstd", [P, 1])
        xn = sb("xn", [P, 2, D])
        xT = sb("xT", [P, 2, 2, P])
        hT = [sb(f"hT{l}", [P, 2, HC, P]) for l in range(layers)]
        out = sb("out", [P, 2, D])
        on = sb("on", [P, 2, D]) if XN is not None else None
        gate = sb("gate", [P, 2, count])
        gmax, gsum = sb("gmax", [P, 1]), sb("gsum", [P, 1])
        XTR = ps("XT", [P, 3, P])
        XT, RP = XTR[:, 0:2, :], XTR[:, 2, :]
        HP = [[ps(f"HP{l}{i}", [P, HC * P]) for i in range(2)] for l in range(layers)]
        YP = [ps(f"YP{i}", [P, D]) for i in range(2)]
        loaded = [sem("loaded0"), sem("loaded1")]
        stored = [sem("stored0"), sem("stored1")]
        normed, turned, turned_sb, ready, chain, free, taken = (
            sem(n) for n in ("normed", "turned", "turned_sb", "ready", "chain", "free", "taken"))
        hid = [sem(f"hid{l}") for l in range(layers)]
        hid_sb = [sem(f"hid_sb{l}") for l in range(layers)]
        summed, routed, logits, exped = sem("summed"), sem("routed"), sem("logits"), sem("exped")
        asked, raised, aside = sem("asked"), sem("raised"), sem("aside")
        if before is not None:
            before.open(ctx)
        roots = 1 + (1 if XN is not None else 0) + (before.ROOTS if before is not None else 0)
        roots_ahead = 1 + (2 * before.AHEAD + 1 if before is not None else 0)
        block = ctx.enter_context(nc.Block())

        @block.gpsimd
        def _(pool):
            raise_to_minus_half(nc, pool, asked, raised, rstd[:], consts, 2 * PAIRS * roots + roots_ahead)

        @block.sync
        def _(sp):
            def load(half, at):
                sp.dma_start(x[:, half, :], X[at, :]).then_inc(loaded[half], 16)

            stores = 16 if XN is None else 32
            sp.sem_inc(free, 2)
            if before is None:
                load(0, slice(0, P))
                load(1, slice(P, 2 * P))
            else:
                before.loads_ahead(sp)
            with sp.Fori(0, PAIRS) as t:
                for half in range(2):
                    sp.wait_ge(ready, t * 2 + half + 1)
                    sp.dma_start(X_out[bass.ds((t * 2 + half) * P, P), :], out[:, half, :]).then_inc(stored[half], 16)
                    if XN is not None:
                        sp.dma_start(XN[bass.ds((t * 2 + half) * P, P), :], on[:, half, :]).then_inc(stored[half], 16)
                    if before is None:
                        load(half, bass.ds((t * 2 + half + 2) * P, P))
                    else:
                        before.load(sp, half, bass.ds((t * 2 + half + 4) * P, P))
                    sp.wait_ge(stored[half], t * stores + stores)
                    sp.sem_inc(free, 1)
            for half in range(2):
                if before is None:
                    sp.wait_ge(loaded[half], 16 * (PAIRS + 1))
                else:
                    sp.wait_ge(before.loaded[half], 16 * (PAIRS + 2))

        gate_steps = 0 if GATE is not None else 4

        @block.vector
        def _(dve):
            links = 4 + gate_steps + count + (4 if XN is not None else 0) + (before.LINKS if before is not None else 0)
            c = Chain(dve, chain, per=2 * links)
            root = Root(dve, asked, raised, 2 * roots, aside)
            buffers = (stats[:], mv[:], rstd)

            def norm(half, arrived):
                if before is None:
                    dve.wait_ge(loaded[half], arrived)
                layer_norm(nc, root, c.link, x[:, half, :], stats[:], mv[:], rstd, xn[:, half, :])
                dve.sem_inc(normed, 1)

            dve.sem_inc(taken, 2)
            if before is not None:
                before.one_plus_eps(c.link)
                for g in range(before.AHEAD):
                    before.front(dve, root, c.link, g, slice(g, g + 1), 16, *buffers)
                    before.back(dve, root, c.link, g, g + 1, x[:, g, :], *buffers)
                before.front(dve, root, c.link, 0, slice(2, 3), 32, *buffers)
            norm(0, 16)
            with dve.Fori(0, PAIRS) as t:
                c.start(t)
                root.start(t)
                for half in range(2):
                    if GATE is None:
                        dve.wait_ge(routed, t * 2 + half + 1)
                        c.link(nc.vector.tensor_tensor(gate[:, half, :], RP[:, 0:count], router[1], ALU.add))
                        c.link(nc.vector.tensor_reduce(gmax[:], gate[:, half, :], AX.X, ALU.max, negate=True))
                        dve.sem_inc(logits, 1)
                        dve.wait_ge(exped, t * 2 + half + 1)
                        c.link(nc.vector.reciprocal(gsum[:], gsum[:]))
                        c.link(nc.vector.tensor_scalar(gate[:, half, :], gate[:, half, :], gsum[:], None, ALU.mult))
                    dve.wait_ge(free, t * 2 + half + 1)
                    for e in range(count):
                        dve.wait_ge(summed, t * (2 * count) + (half * count + e + 3))
                        g = gate[:, half, e:e + 1] if GATE is None else \
                            GATE[:, bass.ds(t * 2 + half, 1), e:e + 1].rearrange("p a b -> p (a b)")
                        c.link(nc.vector.scalar_tensor_tensor(
                            out[:, half, :], YP[e % 2][:, 0:D], g, x[:, half, :] if e == 0 else out[:, half, :],
                            ALU.mult, ALU.add))
                        dve.sem_inc(taken, 1)
                        if e == count // 4 - 1:
                            norm(1 - half, t * 16 + (16 if half == 0 else 32))
                        if before is not None and e == 6:
                            before.back(dve, root, c.link, half, t * 2 + half + 3, x[:, half, :], *buffers)
                        if before is not None and e == 7:
                            before.front(dve, root, c.link, 1 - half, bass.ds(t * 2 + half + 3, 1),
                                         t * 16 + (32 if half == 0 else 48), *buffers)
                    if XN is not None:
                        layer_norm(nc, root, c.link, out[:, half, :], stats[:], mv[:], rstd, on[:, half, :])
                    dve.sem_inc(ready, 1)
                c.end()

        units = 2 * count

        @block.scalar
        def _(act):
            def turn_copy(half):
                nc.scalar.activation(xT[:, half], XT, ACT.Copy).then_inc(turned_sb, 1)

            def hide(l, e, slot):
                for j in range(HC):
                    last = nc.scalar.activation(hT[l][:, slot, j, :], HP[l][slot][:, j * P:(j + 1) * P], func,
                                                bias=bias[l][:, e, j:j + 1],
                                                scale=1.0 if scale is None else scale[l][:, e, j:j + 1])
                last.then_inc(hid_sb[l], 1)

            for l in range(layers):
                act.sem_inc(hid_sb[l], 1)
            if before is not None:
                for g in range(before.AHEAD):
                    before.turn_copy(act, g + 1)
                    before.hide(act, g + 1)
            act.wait_ge(turned, 1)
            turn_copy(0)
            for last in range(layers):
                for l in range(last + 1):
                    act.wait_ge(hid[l], last - l + 1)
                    hide(l, last - l, (last - l) % 2)
            with act.Fori(0, PAIRS) as t:
                for v in range(units):
                    if before is not None and v % count == 3:
                        before.turn_copy(act, t * 2 + (v // count + 3))
                    if before is not None and v % count == 5:
                        before.hide(act, t * 2 + (v // count + 3))
                    if v % count == 1 and GATE is None:
                        half = v // count
                        act.wait_ge(logits, t * 2 + half + 1)
                        nc.scalar.activation(gate[:, half, :], gate[:, half, :], ACT.Exp, bias=gmax[:],
                                             accum_out=gsum[:]).then_inc(exped, 1)
                    if v % count == count - layers - 1:
                        act.wait_ge(turned, t * 2 + (v // count + 2))
                        turn_copy(1 - v // count)
                    for l in range(layers):
                        u = v + layers - l
                        act.wait_ge(hid[l], t * units + (u + 1))
                        if l == layers - 1:
                            act.wait_ge(summed, t * units + (u - 2 + 1 + 2))
                        else:
                            act.wait_ge(hid[l + 1], t * units + (u - 2 + 1))
                        hide(l, u % count, u % 2)

        @block.tensor
        def _(pe):
            def turn(half):
                for c in range(2):
                    last = nc.tensor.transpose(XT[:, c, :], xn[:, half, c * P:(c + 1) * P], ident[:, :])
                last.then_inc(turned, 1)

            def layer(l, e, slot, half):
                for j in range(HC):
                    to = HP[l][slot][:, j * P:(j + 1) * P]
                    for c in range(2 if l == 0 else HC):
                        w = (w_first if l == 0 else w_mid)[:, e, c, j * P:(j + 1) * P]
                        r = xT[:, half, c, :] if l == 0 else hT[l - 1][:, slot, c, :]
                        last = nc.tensor.matmul(to, w, r, start=(c == 0), stop=(c == (2 if l == 0 else HC) - 1),
                                                skip_group_check=True)
                last.then_inc(hid[l], 1)

            def route(half):
                for c in range(2):
                    last = nc.tensor.matmul(RP[:, 0:count], xT[:, half, c, :], router[0][:, c, :], start=(c == 0),
                                            stop=(c == 1), skip_group_check=True)
                last.then_inc(routed, 1)

            pe.sem_inc(summed, 2)
            if before is not None:
                for g in range(before.AHEAD):
                    before.turn(pe, g + 1)
                    before.first_product(pe, g + 1)
                    before.second_product(pe, g + 1)
            pe.wait_ge(normed, 1)
            turn(0)
            pe.wait_ge(turned_sb, 1)
            for last in range(layers):
                for l in range(last + 1):
                    u = last - l
                    if l > 0:
                        pe.wait_ge(hid_sb[l - 1], u + 2)
                    layer(l, u, u % 2, 0)
            with pe.Fori(0, PAIRS) as t:
                for v in range(units):
                    half = v // count
                    if before is not None and v % count == 2:
                        before.turn(pe, t * 2 + half + 3)
                    if before is not None and v % count == 4:
                        before.first_product(pe, t * 2 + half + 3)
                    if before is not None and v % count == 6:
                        before.second_product(pe, t * 2 + half + 3)
                    if v % count == 0 and GATE is None:
                        route(half)
                    if v % count == count - layers - 1:
                        pe.wait_ge(normed, t * 2 + half + 2)
                        turn(1 - half)
                    if v % count == count - layers:
                        pe.wait_ge(turned_sb, t * 2 + half + 2)
                    for l in range(layers):
                        u = v + layers - l
                        pe.wait_ge(hid_sb[l], t * units + u)
                        if l > 0:
                            pe.wait_ge(hid_sb[l - 1], t * units + (u + 2))
                        layer(l, u % count, u % 2, (u // count) % 2)
                    pe.wait_ge(hid_sb[layers - 1], t * units + (v + 2))
                    pe.wait_ge(taken, t * units + (v + 1))
                    y = YP[v % 2][:, 0:D]
                    for c in range(HC):
                        nc.tensor.matmul(y, hT[layers - 1][:, v % 2, c, :], w_last[:, v % count, c, :],
                                         start=(c == 0), stop=False, skip_group_check=True)
                    nc.tensor.matmul(y, consts["ones"][0:1, :], bias[layers][0:1, v % count, :], start=False, stop=True,
                                     skip_group_check=True).then_inc(summed, 1)


class IsomorphismLayer:
    AHEAD = 2
    LINKS, ROOTS = 14, 2

    def __init__(self, nc, ctx, X, AGG, W1, b1, W2, b2, eps, gamma, beta, consts):
        def sb(n, s, d=f32):
            return ctx.enter_context(nc.sbuf_tensor(f"gi_{n}", s, d))

        self.nc, self.X, self.AGG, self.ident = nc, X, AGG, consts["ident"]
        self.w1, self.w2 = sb("w1", [P, 2, D]), sb("w2", [P, 2, D])
        self.bias1 = sb("bias1", [P, 2])
        self.row = sb("row", [P, 3, D])
        self.keep = sb("keep", [P, 1])
        load_weights(nc, "gi", [
            (self.w1[:], W1.rearrange("(c p) d -> p c d", p=P)), (self.w2[:], W2.rearrange("(c p) d -> p c d", p=P)),
            (self.bias1[:], b1.rearrange("(c p) -> p c", p=P)), (self.row[:, 0, :], b2.partition_broadcast(P)),
            (self.row[:, 1, :], gamma.partition_broadcast(P)), (self.row[:, 2, :], beta.partition_broadcast(P)),
            (self.keep[:], eps.partition_broadcast(P))])
        self.x = sb("x", [P, 2, D])
        self.xn, self.z, self.r = sb("xn", [P, D]), sb("z", [P, D]), sb("r", [P, D])
        self.zT, self.hT = sb("zT", [P, 2, P]), sb("hT", [P, 2, P])

    def open(self, ctx):
        nc = self.nc
        bank = ctx.enter_context(nc.psum_tensor("gi_bank", [P, 4, P], f32))
        self.ZT, self.HP, self.YP = bank[:, 0:2, :], bank[:, 2:4, :], bank[:, 0:2, :].rearrange("p a d -> p (a d)")
        (self.loaded0, self.loaded1, self.normed, self.turned, self.turned_sb, self.hid, self.hid_sb, self.projected,
         self.backed) = (ctx.enter_context(signal(nc, f"gi_{n}")) for n in (
             "loaded0", "loaded1", "normed", "turned", "turned_sb", "hid", "hid_sb", "projected", "backed"))
        self.loaded = (self.loaded0, self.loaded1)


    def load(self, sp, half, at):
        sp.dma_start(self.x[:, half, :], self.X[at, :]).then_inc(self.loaded[half], 16)

    def loads_ahead(self, sp):
        for g in range(2):
            self.load(sp, g, slice(g * P, (g + 1) * P))
        for g in range(2):
            sp.wait_ge(self.backed, g + 1)
            self.load(sp, g, slice((g + 2) * P, (g + 3) * P))

    def one_plus_eps(self, link):
        link(self.nc.vector.tensor_scalar(self.keep[:], self.keep[:], 1.0, None, ALU.add))

    def front(self, dve, root, link, half, at, arrived, stats, mv, rstd):
        dve.wait_ge(self.loaded[half], arrived)
        layer_norm(self.nc, root, link, self.x[:, half, :], stats, mv, rstd, self.xn[:])
        link(self.nc.vector.scalar_tensor_tensor(self.z[:], self.xn[:], self.keep[:],
                                                 self.AGG[:, at, :].rearrange("p a d -> p (a d)"), ALU.mult, ALU.add))
        dve.sem_inc(self.normed, 1)

    def back(self, dve, root, link, half, made, to, stats, mv, rstd):
        V, r = self.nc.vector, self.r
        dve.wait_ge(self.projected, made)
        link(V.tensor_tensor(r[:], self.YP, self.row[:, 0, :], ALU.add))
        link(V.tensor_tensor(r[:], r[:], self.xn[:], ALU.add))
        layer_norm(self.nc, root, link, r[:], stats, mv, rstd, r[:])
        link(V.tensor_tensor(r[:], r[:], self.row[:, 1, :], ALU.mult))
        link(V.tensor_tensor(r[:], r[:], self.row[:, 2, :], ALU.add))
        link(V.scalar_tensor_tensor(to, r[:], 0.0, self.x[:, half, :], ALU.max, ALU.add))
        dve.sem_inc(self.backed, 1)

    def turn(self, pe, made):
        pe.wait_ge(self.normed, made)
        for c in range(2):
            last = self.nc.tensor.transpose(self.ZT[:, c, :], self.z[:, c * P:(c + 1) * P], self.ident[:, :])
        last.then_inc(self.turned, 1)

    def turn_copy(self, act, made):
        act.wait_ge(self.turned, made)
        self.nc.scalar.activation(self.zT[:], self.ZT, ACT.Copy).then_inc(self.turned_sb, 1)

    def first_product(self, pe, made):
        pe.wait_ge(self.turned_sb, made)
        for j in range(2):
            for c in range(2):
                last = self.nc.tensor.matmul(self.HP[:, j, :], self.w1[:, c, j * P:(j + 1) * P], self.zT[:, c, :],
                                             start=(c == 0), stop=(c == 1), skip_group_check=True)
        last.then_inc(self.hid, 1)

    def hide(self, act, made):
        act.wait_ge(self.hid, made)
        for j in range(2):
            last = self.nc.scalar.activation(self.hT[:, j, :], self.HP[:, j, :], ACT.Relu, bias=self.bias1[:, j:j + 1])
        last.then_inc(self.hid_sb, 1)

    def second_product(self, pe, made):
        pe.wait_ge(self.hid_sb, made)
        for c in range(2):
            last = self.nc.tensor.matmul(self.YP, self.hT[:, c, :], self.w2[:, c, :],
                                         start=(c == 0), stop=(c == 1), skip_group_check=True)
        last.then_inc(self.projected, 1)


def first_experts(nc, X, X_out, XN, GATE, W1, b1, W2, b2, consts):
    hidden = W1.shape[2]
    HC = hidden // P
    with ExitStack() as ctx:
        def sb(n, s, d=f32):
            return ctx.enter_context(nc.sbuf_tensor(f"fe_{n}", s, d))

        w1, w2 = sb("w1", [P, GE, 2, hidden]), sb("w2", [P, GE, HC, D])
        bias1, bias2 = sb("bias1", [P, GE, HC]), sb("bias2", [1, GE, D])
        items = [(bias2[:].rearrange("p e d -> p (e d)"), b2.rearrange("e d -> (e d)").unsqueeze(0))]
        for e in range(GE):
            items += [(w1[:, e], W1[e].rearrange("(c p) h -> p c h", p=P)), (w2[:, e], W2[e].rearrange("(c p) d -> p c d", p=P)),
                      (bias1[:, e, :], b1[e].rearrange("(c p) -> p c", p=P))]
        load_weights(nc, "fe", items)
        experts(nc, "fx", X, X_out, XN, GE, hidden, 1, w1, None, w2, [bias1, bias2], None, ACT.Gelu, GATE, None, None, consts)


def second_experts(nc, before, X_out, Wr, br, W1, b1, g1, be1, m1, v1, W2, b2, g2, be2, m2, v2, Wo, bo, consts):
    count = W1.shape[0]
    with ExitStack() as ctx:
        def sb(n, s, d=f32):
            return ctx.enter_context(nc.sbuf_tensor(f"se_{n}", s, d))

        w = [sb(f"w{i}", [P, count, 2, D]) for i in range(3)]
        wr, rb = sb("wr", [P, 2, count]), sb("rb", [P, count])
        raw = sb("raw", [P, 2, 5, count, 2])
        scale, bias = [sb(f"scale{i}", [P, count, 2]) for i in range(2)], [sb(f"bias{i}", [P, count, 2]) for i in range(2)]
        bias3 = sb("bias3", [1, count, D])
        items = [(wr[:], Wr.rearrange("(c p) e -> p c e", p=P)), (rb[:], br.partition_broadcast(P)),
                 (bias3[:].rearrange("p e d -> p (e d)"), bo.rearrange("e d -> (e d)").unsqueeze(0))]
        for i, one in enumerate((W1, W2, Wo)):
            for e in range(count):
                items.append((w[i][:, e], one[e].rearrange("(c p) d -> p c d", p=P)))
        for l, group in enumerate(((b1, g1, be1, m1, v1), (b2, g2, be2, m2, v2))):
            for j, one in enumerate(group):
                items.append((raw[:, l, j].rearrange("p e c -> p (e c)"), one.rearrange("e (c p) -> p (e c)", p=P)))
        load_weights(nc, "se", items)
        with (signal(nc, "se_chain") as chain, signal(nc, "se_asked") as asked, signal(nc, "se_raised") as raised,
              nc.Block() as block):
            @block.gpsimd
            def _(pool):
                pool.wait_ge(asked, 1)
                for l in range(2):
                    v = raw[:, l, 4].rearrange("p e c -> p (e c)")
                    nc.gpsimd.tensor_tensor(v, v, consts["minus_half"][:].to_broadcast([P, 2 * count]),
                                            ALU.pow).then_inc(raised, 1)

            @block.vector
            def _(dve):
                c = Chain(dve, chain)
                for l in range(2):
                    v = raw[:, l, 4]
                    c.link(nc.vector.tensor_scalar(v, v, BN_EPS, None, ALU.add))
                dve.sem_inc(asked, 1)
                dve.wait_ge(raised, 2)
                for l in range(2):
                    b, g, be, m, v = (raw[:, l, j] for j in range(5))
                    c.link(nc.vector.tensor_tensor(scale[l][:], v, g, ALU.mult))
                    c.link(nc.vector.tensor_tensor(b, b, m, ALU.subtract))
                    c.link(nc.vector.tensor_tensor(b, b, scale[l][:], ALU.mult))
                    c.link(nc.vector.tensor_tensor(bias[l][:], b, be, ALU.add))
        experts(nc, "sx", None, X_out, None, count, D, 2, w[0], w[1], w[2], [bias[0], bias[1], bias3], scale, ACT.Relu,
                None, (wr, rb[:]), before, consts)


def copy_out(nc, X, out):
    with signal(nc, "co_done") as done, nc.Block() as block:
        @block.sync
        def _(sp):
            sp.dma_start(out, X[0:N, :]).then_inc(done, 16)
            sp.wait_ge(done, 16)


def build(nc, ins, out):
    i = ins
    wide = lambda name, r, c, d=f32: nc.dram_tensor(name, [r, c], d, kind="Internal").ap()
    rec1, rec2 = wide("rec1", CHUNKS1 * P, 2, i32), wide("rec2", CHUNKS2 * P, 2, i32)
    X0, X1, X2, X4 = (wide(f"X{n}", ROWS, D) for n in (0, 1, 2, 4))
    K, V, XN = wide("K", ROWS, D), wide("V", ROWS, D), wide("XN", ROWS, D)
    TAB = wide("TAB", ROWS, GH * GE + GH)
    G = GH * GE
    w1 = (CHUNKS1 + P - 1) // P * P
    w2 = (CHUNKS2 + P - 1) // P * P
    with ExitStack() as ctx:
        c = make_consts(nc, ctx)
        sort_edges(nc, "s1", COLS1, CHUNKS1, False, i["src"], i["dst"], rec1, c)
        copy_in(nc, i["x"], X0, (X1, X2))
        with ExitStack() as layer:
            arr = chunk_arrays(nc, layer, "c1", CHUNKS1, rec1)
            wt = gnn_weights(nc, layer, *(i["L0_gnn_" + n] for n in
                                          ("Wq", "bq", "Wk", "bk", "Wv", "bv", "Wa", "ba", "rel_att", "rel_msg", "rel_pri", "skip")), c)
            S = layer.enter_context(nc.sbuf_tensor("S1", [P, HEADS, w1], f32))
            with nc.sbuf_tensor("Q", [P, TILES + 1, D], f32) as Q:
                project(nc, X0, Q, K, V, wt, c)
                clear(nc, "cs1", [S[:], Q[:, DUMP, :]])
                edge_scores(nc, "es1", D, HEADS, CHUNKS1, K[0:N, :], Q, arr, S, None, c)
            segment_softmax_numerators(nc, "sm1", HEADS, CHUNKS1, rec1, S, c)
            with nc.sbuf_tensor("AGG1", [P, TILES + 2, D + HEADS], f32) as AGG:
                edge_sums(nc, "ev1", D, HEADS, CHUNKS1, V[0:N, :], AGG, arr, S, c)
                attention_out(nc, X0, AGG, X1, wt, c)
        sort_edges(nc, "s2", COLS2, CHUNKS2, True, i["L0_ffn_edge_index"][0], i["L0_ffn_edge_index"][1], rec2, c)
        with ExitStack() as layer:
            GATE = layer.enter_context(nc.sbuf_tensor("GATE", [P, TILES + 1, GE], f32))
            with ExitStack() as inner:
                arr = chunk_arrays(nc, inner, "c2", CHUNKS2, rec2)
                S = inner.enter_context(nc.sbuf_tensor("S2", [P, GH, w2], f32))
                ADST = inner.enter_context(nc.sbuf_tensor("ADST", [P, TILES + 1, GH], f32))
                feats = inner.enter_context(nc.sbuf_tensor("feats", [P, CHUNKS2 + UNIT, G], f32))
                gat_project(nc, X1, TAB, ADST, i["L0_ffn_W_gat"], i["L0_ffn_att_src"], i["L0_ffn_att_dst"], c)
                clear(nc, "cs2", [S[:], feats[:, CHUNKS2:CHUNKS2 + UNIT, :]])
                edge_scores(nc, "es2", G + GH, GH, CHUNKS2, TAB[0:N, :], ADST, arr, S, feats, c)
                leaky(nc, S, CHUNKS2)
                segment_softmax_numerators(nc, "sm2", GH, CHUNKS2, rec2, S, c)
                AGG = inner.enter_context(nc.sbuf_tensor("AGG2", [P, UNIT, TILES + 1, G + GH], f32))
                graph_sums(nc, CHUNKS2, AGG, arr, S, feats, c)
                gates(nc, AGG, GATE, i["L0_ffn_b_gat"], i["L0_ffn_ln_gamma"], i["L0_ffn_ln_beta"], c)
            first_experts(nc, X1, X2, XN, GATE, *(i["L0_ffn_" + n] for n in ("W1", "b1", "W2", "b2")), c)
        with ExitStack() as layer:
            arr = chunk_arrays(nc, layer, "c3", CHUNKS1, rec1)
            AGG = layer.enter_context(nc.sbuf_tensor("AGG3", [P, 2 * PAIRS + 3, D], f32))
            edge_sums(nc, "ev3", D, 0, CHUNKS1, XN[0:N, :], AGG, arr, None, c)
            iso = IsomorphismLayer(nc, layer, X2, AGG, *(i["L1_gnn_" + n] for n in ("W1", "b1", "W2", "b2", "eps", "gamma", "beta")), c)
            second_experts(nc, iso, X4, *(i["L1_ffn_" + n] for n in
                                          ("Wr", "br", "W1", "b1", "g1", "be1", "m1", "v1", "W2", "b2", "g2", "be2", "m2", "v2", "Wo", "bo")), c)
        copy_out(nc, X4, out)


def clear(nc, name, tiles):
    with signal(nc, name) as done, nc.Block() as block:
        @block.vector
        def _(dve):
            for one in tiles:
                last = nc.vector.memset(one, 0.0)
            last.then_inc(done, 1)
            dve.wait_ge(done, 1)




_INS = ['x', 'src', 'dst', 'L0_gnn_Wk', 'L0_gnn_bk', 'L0_gnn_Wq', 'L0_gnn_bq', 'L0_gnn_Wv', 'L0_gnn_bv', 'L0_gnn_Wa', 'L0_gnn_ba', 'L0_gnn_rel_att', 'L0_gnn_rel_msg', 'L0_gnn_rel_pri', 'L0_gnn_skip', 'L0_ffn_W_gat', 'L0_ffn_att_src', 'L0_ffn_att_dst', 'L0_ffn_b_gat', 'L0_ffn_ln_gamma', 'L0_ffn_ln_beta', 'L0_ffn_W1', 'L0_ffn_b1', 'L0_ffn_W2', 'L0_ffn_b2', 'L0_ffn_edge_index', 'L1_gnn_W1', 'L1_gnn_b1', 'L1_gnn_W2', 'L1_gnn_b2', 'L1_gnn_eps', 'L1_gnn_gamma', 'L1_gnn_beta', 'L1_ffn_Wr', 'L1_ffn_br', 'L1_ffn_W1', 'L1_ffn_b1', 'L1_ffn_g1', 'L1_ffn_be1', 'L1_ffn_m1', 'L1_ffn_v1', 'L1_ffn_W2', 'L1_ffn_b2', 'L1_ffn_g2', 'L1_ffn_be2', 'L1_ffn_m2', 'L1_ffn_v2', 'L1_ffn_Wo', 'L1_ffn_bo']
_OUTS = [((6250, 256), 'float32')]


def kernel(**inputs):
    import numpy as _np
    import concourse.bacc as _bacc
    from concourse import mybir as _mybir
    from concourse.bass_utils import run_bass_kernel_spmd as _run

    nc = _bacc.Bacc("TRN2", target_bir_lowering=False, num_devices=1)
    arrays, args = {}, {}
    for name in _INS:
        a = _np.ascontiguousarray(inputs[name])
        if not a.ndim or a.shape == ():
            a = a.reshape(1)
        arrays[f"in_{name}_dram"] = a
        args[name] = nc.dram_tensor(f"in_{name}_dram", a.shape, _mybir.dt.from_np(a.dtype), kind="ExternalInput").ap()
    (shape, dtype), = _OUTS
    out = nc.dram_tensor("out_0_dram", shape, _mybir.dt.from_np(_np.dtype(dtype)), kind="ExternalOutput").ap()
    build(nc, args, out)
    r = _run(nc, [arrays], core_ids=[0])
    return r.results[0]["out_0_dram"]
```
